# Optimizing a Trainium2 kernel written in Bass

```python
import numpy as np
import jax
import jax.numpy as jnp

def _softmax(x, axis=-1):
    return jax.nn.softmax(x, axis=axis)

def _gelu(x):
    return jax.nn.gelu(x, approximate=True)

def _silu(x):
    return jax.nn.silu(x)

def _sigmoid(x):
    return jax.nn.sigmoid(x)

def _layernorm(x, axis=-1, eps=1e-05):
    m = jnp.mean(x, axis=axis, keepdims=True)
    v = jnp.var(x, axis=axis, keepdims=True)
    return (x - m) / jnp.sqrt(v + eps)

def _scatter_add(tgt, idx, src, axis=0):
    return tgt.at[idx].add(src)

def _segment_sum(src, seg, n):
    return jax.ops.segment_sum(src, seg, n)
kernel_name = 'mk_flamingo_gated_d4_seqx_r8_0932b4'

def setup_inputs(seed: int=0):
    np.random.seed(seed)
    _w = jnp.asarray

    def _rec_inputs():
        import jax
        import jax.numpy as jnp
        _rk = jax.random.key(seed)
        x = 7.22e-05 + 1 * jax.random.normal(jax.random.fold_in(_rk, 1), (32, 56, 128), jnp.float32)
        _lenS = 56 - jax.random.randint(jax.random.fold_in(_rk, 7), (32,), 0, max(1, 56 // 4) + 1, jnp.int32)
        _lenS2 = 1500 - jax.random.randint(jax.random.fold_in(_rk, 8), (32,), 0, max(1, 1500 // 4) + 1, jnp.int32)
        _ctx_1024P = jax.random.normal(jax.random.fold_in(_rk, 11), (32, 16, 128), jnp.float32)
        _ctx_1024c = jax.random.dirichlet(jax.random.fold_in(_rk, 511), 0.3 * jnp.ones((16,), jnp.float32), (32, 1500))
        _ctx_1024t = jnp.einsum('bsk,bkd->bsd', _ctx_1024c, _ctx_1024P)
        _ctx_1024t = _ctx_1024t * jax.lax.rsqrt(jnp.mean(jnp.square(_ctx_1024t)) + 1e-12) * 0.953939
        ctx_1024 = 4.13588e-05 + 0.999923 * (_ctx_1024t + 0.3 * jax.random.normal(jax.random.fold_in(_rk, 611), (32, 1500, 128), jnp.float32))
        fside_1x16xSxS2_0 = 7.48737e-06 + 1.00011 * jax.random.normal(jax.random.fold_in(_rk, 13), (1, 16, 56, 1500), jnp.float32)
        _validS = jnp.arange(56)[None, :] < _lenS[:, None]
        _validS2 = jnp.arange(1500)[None, :] < _lenS2[:, None]
        _causal = jnp.tril(jnp.ones((56, 56), dtype=bool))
        mask_Bx1xSxS2_ik1 = jnp.where(jnp.broadcast_to(_validS2[:, None, None, :], (32, 1, 56, 1500)), 1, 0).astype(jnp.int32)
        mask_Bx1xSxS2_fk0 = jnp.where(jnp.broadcast_to(_validS2[:, None, None, :], (32, 1, 56, 1500)), 0.0, 1.0).astype(jnp.float32)
        _g = jax.random.normal(jax.random.fold_in(_rk, 9001), (2, 4), jnp.float32)
        _g = jnp.sign(_g) * jnp.maximum(jnp.abs(_g), 1.0) + (_g == 0) * 1.0
        g_xattn = _g[0]
        g_ffn = _g[1]
        return (x, ctx_1024, fside_1x16xSxS2_0, mask_Bx1xSxS2_ik1, mask_Bx1xSxS2_fk0, g_xattn, g_ffn)
    x, ctx_1024, fside_1x16xSxS2_0, mask_Bx1xSxS2_ik1, mask_Bx1xSxS2_fk0, g_xattn, g_ffn = _rec_inputs()

    def _L0_xattn_setup():
        import jax, jax.numpy as jnp
        import numpy as np
        import math
        D_MODEL = 128
        NUM_HEADS = 16
        D_K = D_MODEL // NUM_HEADS
        B, L = (4, 256)

        def _nan_clamp(x):
            x = jnp.where(jnp.isnan(x), 0.0, x)
            x = jnp.where(jnp.isposinf(x), 10000.0, x)
            x = jnp.where(jnp.isneginf(x), -10000.0, x)
            return x

        def _split_heads(x):
            b, l, _ = x.shape
            return x.reshape(b, l, NUM_HEADS, D_K).transpose(0, 2, 1, 3)
        key = jax.random.key(seed)
        ks = jax.random.split(key, 14)
        s = 1.0 / math.sqrt(D_MODEL)
        return {'Q': jax.random.normal(ks[0], (B, L, D_MODEL), jnp.float32), 'K': jax.random.normal(ks[1], (B, L, D_MODEL), jnp.float32), 'V': jax.random.normal(ks[2], (B, L, D_MODEL), jnp.float32), 'mask': jax.random.randint(ks[3], (B, 1, L, L), 0, 2, jnp.int32), 'attn_bias': jax.random.normal(ks[4], (1, NUM_HEADS, L, L), jnp.float32), 'W_q': jax.random.normal(ks[5], (D_MODEL, D_MODEL), jnp.float32) * s, 'b_q': jax.random.normal(ks[6], (D_MODEL,), jnp.float32) * s, 'W_k': jax.random.normal(ks[7], (D_MODEL, D_MODEL), jnp.float32) * s, 'b_k': jax.random.normal(ks[8], (D_MODEL,), jnp.float32) * s, 'W_v': jax.random.normal(ks[9], (D_MODEL, D_MODEL), jnp.float32) * s, 'b_v': jax.random.normal(ks[10], (D_MODEL,), jnp.float32) * s, 'W_o': jax.random.normal(ks[11], (D_MODEL, D_MODEL), jnp.float32) * s, 'b_o': jax.random.normal(ks[12], (D_MODEL,), jnp.float32) * s}
    _L0_xattn_all = _L0_xattn_setup()
    _L0_xattn_in = {k: v for k, v in _L0_xattn_all.items() if k in ('W_q', 'b_q', 'W_k', 'b_k', 'W_v', 'b_v', 'W_o', 'b_o')}
    del _L0_xattn_all

    def _L0_ffn_setup():
        import jax, jax.numpy as jnp
        import numpy as np

        def _bitlinear(x, w_latent):
            scale = jax.lax.stop_gradient(jnp.clip(jnp.mean(jnp.abs(w_latent), axis=1, keepdims=True), 1e-05, None))
            tern = jnp.clip(jnp.round(w_latent / scale), -1.0, 1.0)
            w = w_latent + jax.lax.stop_gradient(tern - w_latent)
            return x @ (w * scale).T
        key = jax.random.key(seed)
        ks = jax.random.split(key, 6)
        dim, hidden, rank = (128, 512, 16)
        B, S = (4, 512)
        x = jax.random.normal(ks[0], (B, S, dim), dtype=jnp.float32)
        w_fc = 0.02 * jax.random.normal(ks[1], (hidden, dim), dtype=jnp.float32)
        w_proj = 0.02 * jax.random.normal(ks[2], (dim, hidden), dtype=jnp.float32)
        u = 0.02 * jax.random.normal(ks[3], (hidden, rank), dtype=jnp.float32)
        v = 0.02 * jax.random.normal(ks[4], (rank, dim), dtype=jnp.float32)
        fast_b = jax.random.normal(ks[5], (rank, rank), dtype=jnp.float32)
        gate = jnp.float32(0.05)
        return {'x': x, 'fast_b': fast_b, 'w_fc': w_fc, 'w_proj': w_proj, 'u': u, 'v': v, 'gate': gate}
    _L0_ffn_all = _L0_ffn_setup()
    _L0_ffn_in = {k: v for k, v in _L0_ffn_all.items() if k in ('fast_b', 'w_fc', 'w_proj', 'u', 'v', 'gate')}
    del _L0_ffn_all

    def _L1_xattn_setup():
        import jax, jax.numpy as jnp
        import numpy as np
        D_MODEL = 128
        N_HEADS = 16
        HEAD_DIM = D_MODEL // N_HEADS
        key = jax.random.key(seed)
        k1, k2, k3, k4, k5, k6 = jax.random.split(key, 6)
        B, T_q, T_kv = (4, 128, 512)
        s = 1.0 / np.sqrt(D_MODEL)
        return {'query': jax.random.normal(k1, (B, T_q, D_MODEL), dtype=jnp.float32), 'kv_source': jax.random.normal(k2, (B, T_kv, D_MODEL), dtype=jnp.float32), 'w_q': jax.random.normal(k3, (D_MODEL, D_MODEL), dtype=jnp.float32) * s, 'w_k': jax.random.normal(k4, (D_MODEL, D_MODEL), dtype=jnp.float32) * s, 'w_v': jax.random.normal(k5, (D_MODEL, D_MODEL), dtype=jnp.float32) * s, 'w_o': jax.random.normal(k6, (D_MODEL, D_MODEL), dtype=jnp.float32) * s}
    _L1_xattn_all = _L1_xattn_setup()
    _L1_xattn_in = {k: v for k, v in _L1_xattn_all.items() if k in ('w_q', 'w_k', 'w_v', 'w_o')}
    del _L1_xattn_all

    def _L1_ffn_setup():
        import jax, jax.numpy as jnp
        import numpy as np
        B, S, D = (4, 256, 128)
        E = 8
        TOPK = 2
        I = 938

        def _swiglu(x, gate_up, down):
            h = jnp.einsum('bsd,fd->bsf', x, gate_up)
            g, u = jnp.split(h, 2, axis=-1)
            return jnp.einsum('bsi,di->bsd', jax.nn.silu(g) * u, down)
        key = jax.random.key(seed)
        ks = jax.random.split(key, 6)
        scale = 1.0 / np.sqrt(D)
        return {'hidden_states': jax.random.normal(ks[0], (B, S, D), dtype=jnp.float32), 'gate_weight': jax.random.normal(ks[1], (E, D), dtype=jnp.float32) * scale, 'shared_gate_up': jax.random.normal(ks[2], (2 * I, D), dtype=jnp.float32) * scale, 'shared_down': jax.random.normal(ks[3], (D, I), dtype=jnp.float32) * (1.0 / np.sqrt(I)), 'experts_gate_up': jax.random.normal(ks[4], (E, 2 * I, D), dtype=jnp.float32) * scale, 'experts_down': jax.random.normal(ks[5], (E, D, I), dtype=jnp.float32) * (1.0 / np.sqrt(I))}
    _L1_ffn_all = _L1_ffn_setup()
    _L1_ffn_in = {k: v for k, v in _L1_ffn_all.items() if k in ('gate_weight', 'shared_gate_up', 'shared_down', 'experts_gate_up', 'experts_down')}
    del _L1_ffn_all

    def _L2_xattn_setup():
        import jax, jax.numpy as jnp
        import numpy as np
        DIM = 128
        HEADS = 16
        DIM_HEAD = 64
        INNER = HEADS * DIM_HEAD
        MLP = 512
        EPS = 1e-05

        def _layernorm(x, g, b):
            mu = jnp.mean(x, axis=-1, keepdims=True)
            var = jnp.mean(jnp.square(x - mu), axis=-1, keepdims=True)
            return (x - mu) * jax.lax.rsqrt(var + EPS) * g + b

        def _l2norm(x):
            n = jnp.sqrt(jnp.sum(jnp.square(x), axis=-1, keepdims=True))
            return x / jnp.maximum(n, 1e-12)

        def _split_heads(x, B, N):
            return x.reshape(B, N, HEADS, DIM_HEAD).transpose(0, 2, 1, 3)
        key = jax.random.key(seed)
        ks = jax.random.split(key, 16)
        B, N = (4, 256)
        s = 0.02
        return {'Q': jax.random.normal(ks[0], (B, N, DIM), jnp.float32), 'K': jax.random.normal(ks[1], (B, N, DIM), jnp.float32), 'V': jax.random.normal(ks[2], (B, N, DIM), jnp.float32), 'wq': jax.random.normal(ks[3], (DIM, INNER), jnp.float32) * s, 'wk': jax.random.normal(ks[4], (DIM, INNER), jnp.float32) * s, 'wv': jax.random.normal(ks[5], (DIM, INNER), jnp.float32) * s, 'wo': jax.random.normal(ks[6], (INNER, DIM), jnp.float32) * s, 'bo': jnp.zeros((DIM,), jnp.float32), 'w1': jax.random.normal(ks[7], (DIM, MLP), jnp.float32) * s, 'b1': jnp.zeros((MLP,), jnp.float32), 'w2': jax.random.normal(ks[8], (MLP, DIM), jnp.float32) * s, 'b2': jnp.zeros((DIM,), jnp.float32), 'ln1_g': jnp.ones((DIM,), jnp.float32), 'ln1_b': jnp.zeros((DIM,), jnp.float32), 'ln2_g': jnp.ones((DIM,), jnp.float32), 'ln2_b': jnp.zeros((DIM,), jnp.float32)}
    _L2_xattn_all = _L2_xattn_setup()
    _L2_xattn_in = {k: v for k, v in _L2_xattn_all.items() if k in ('wq', 'wk', 'wv', 'wo', 'bo', 'w1', 'b1', 'w2', 'b2', 'ln1_g', 'ln1_b', 'ln2_g', 'ln2_b')}
    del _L2_xattn_all

    def _L2_ffn_setup():
        import jax, jax.numpy as jnp
        import numpy as np
        TOP_K = 2
        EPS = 1e-10
        key = jax.random.key(seed)
        k1, k2, k3, k4 = jax.random.split(key, 4)
        B, S, H, E = (4, 256, 128, 8)
        tokens = jax.random.normal(k1, (B, S, H), dtype=jnp.float32)
        router_w = jax.random.normal(k2, (E, H), dtype=jnp.float32) * (1.0 / np.sqrt(H))
        router_b = jax.random.normal(k3, (E,), dtype=jnp.float32) * 0.01
        expert_weights = jax.random.normal(k4, (E, H, H), dtype=jnp.float32) * (1.0 / np.sqrt(H))
        return {'tokens': tokens, 'router_w': router_w, 'router_b': router_b, 'expert_weights': expert_weights}
    _L2_ffn_all = _L2_ffn_setup()
    _L2_ffn_in = {k: v for k, v in _L2_ffn_all.items() if k in ('router_w', 'router_b', 'expert_weights')}
    del _L2_ffn_all

    def _L3_xattn_setup():
        import jax, jax.numpy as jnp
        import numpy as np
        D_MODEL = 128
        NUM_HEADS = 16
        DEPTH = D_MODEL // NUM_HEADS
        B, S = (4, 256)

        def _split(t):
            b, s, _ = t.shape
            return t.reshape(b, s, NUM_HEADS, DEPTH).transpose(0, 2, 1, 3)
        key = jax.random.key(seed)
        ks = jax.random.split(key, 13)
        sd = 1.0 / np.sqrt(D_MODEL)
        inp = {'q_in': jax.random.normal(ks[0], (B, S, D_MODEL), jnp.float32), 'k_in': jax.random.normal(ks[1], (B, S, D_MODEL), jnp.float32), 'v_in': jax.random.normal(ks[2], (B, S, D_MODEL), jnp.float32), 'm_in': (jax.random.uniform(ks[3], (B, 1, S, S)) < 0.1).astype(jnp.float32), 'Wq': jax.random.normal(ks[4], (D_MODEL, D_MODEL), jnp.float32) * sd, 'bq': jax.random.normal(ks[5], (D_MODEL,), jnp.float32) * 0.01, 'Wk': jax.random.normal(ks[6], (D_MODEL, D_MODEL), jnp.float32) * sd, 'bk': jax.random.normal(ks[7], (D_MODEL,), jnp.float32) * 0.01, 'Wv': jax.random.normal(ks[8], (D_MODEL, D_MODEL), jnp.float32) * sd, 'bv': jax.random.normal(ks[9], (D_MODEL,), jnp.float32) * 0.01, 'Wo': jax.random.normal(ks[10], (D_MODEL, D_MODEL), jnp.float32) * sd, 'bo': jax.random.normal(ks[11], (D_MODEL,), jnp.float32) * 0.01}
        return inp
    _L3_xattn_all = _L3_xattn_setup()
    _L3_xattn_in = {k: v for k, v in _L3_xattn_all.items() if k in ('Wq', 'bq', 'Wk', 'bk', 'Wv', 'bv', 'Wo', 'bo')}
    del _L3_xattn_all

    def _L3_ffn_setup():
        import jax, jax.numpy as jnp
        import numpy as np
        B, S, H, E = (4, 256, 128, 8)
        key = jax.random.key(seed)
        k1, k2, k3 = jax.random.split(key, 3)
        scale_w = 1.0 / np.sqrt(H)
        return {'x': jax.random.normal(k1, (B, S, H), dtype=jnp.float32), 'router_w': jax.random.normal(k2, (H, E), dtype=jnp.float32) * scale_w, 'router_b': jnp.zeros((E,), dtype=jnp.float32), 'expert_w': jax.random.normal(k3, (E, H, H), dtype=jnp.float32) * scale_w, 'expert_b': jnp.zeros((E, H), dtype=jnp.float32)}
    _L3_ffn_all = _L3_ffn_setup()
    _L3_ffn_in = {k: v for k, v in _L3_ffn_all.items() if k in ('router_w', 'router_b', 'expert_w', 'expert_b')}
    del _L3_ffn_all
    return {'x': x, 'ctx_1024': ctx_1024, 'fside_1x16xSxS2_0': fside_1x16xSxS2_0, 'mask_Bx1xSxS2_ik1': mask_Bx1xSxS2_ik1, 'mask_Bx1xSxS2_fk0': mask_Bx1xSxS2_fk0, 'g_xattn': g_xattn, 'g_ffn': g_ffn, 'L0_xattn_W_q': _L0_xattn_in['W_q'], 'L0_xattn_b_q': _L0_xattn_in['b_q'], 'L0_xattn_W_k': _L0_xattn_in['W_k'], 'L0_xattn_b_k': _L0_xattn_in['b_k'], 'L0_xattn_W_v': _L0_xattn_in['W_v'], 'L0_xattn_b_v': _L0_xattn_in['b_v'], 'L0_xattn_W_o': _L0_xattn_in['W_o'], 'L0_xattn_b_o': _L0_xattn_in['b_o'], 'L0_ffn_fast_b': _L0_ffn_in['fast_b'], 'L0_ffn_w_fc': _L0_ffn_in['w_fc'], 'L0_ffn_w_proj': _L0_ffn_in['w_proj'], 'L0_ffn_u': _L0_ffn_in['u'], 'L0_ffn_v': _L0_ffn_in['v'], 'L0_ffn_gate': _L0_ffn_in['gate'], 'L1_xattn_w_q': _L1_xattn_in['w_q'], 'L1_xattn_w_k': _L1_xattn_in['w_k'], 'L1_xattn_w_v': _L1_xattn_in['w_v'], 'L1_xattn_w_o': _L1_xattn_in['w_o'], 'L1_ffn_gate_weight': _L1_ffn_in['gate_weight'], 'L1_ffn_shared_gate_up': _L1_ffn_in['shared_gate_up'], 'L1_ffn_shared_down': _L1_ffn_in['shared_down'], 'L1_ffn_experts_gate_up': _L1_ffn_in['experts_gate_up'], 'L1_ffn_experts_down': _L1_ffn_in['experts_down'], 'L2_xattn_wq': _L2_xattn_in['wq'], 'L2_xattn_wk': _L2_xattn_in['wk'], 'L2_xattn_wv': _L2_xattn_in['wv'], 'L2_xattn_wo': _L2_xattn_in['wo'], 'L2_xattn_bo': _L2_xattn_in['bo'], 'L2_xattn_w1': _L2_xattn_in['w1'], 'L2_xattn_b1': _L2_xattn_in['b1'], 'L2_xattn_w2': _L2_xattn_in['w2'], 'L2_xattn_b2': _L2_xattn_in['b2'], 'L2_xattn_ln1_g': _L2_xattn_in['ln1_g'], 'L2_xattn_ln1_b': _L2_xattn_in['ln1_b'], 'L2_xattn_ln2_g': _L2_xattn_in['ln2_g'], 'L2_xattn_ln2_b': _L2_xattn_in['ln2_b'], 'L2_ffn_router_w': _L2_ffn_in['router_w'], 'L2_ffn_router_b': _L2_ffn_in['router_b'], 'L2_ffn_expert_weights': _L2_ffn_in['expert_weights'], 'L3_xattn_Wq': _L3_xattn_in['Wq'], 'L3_xattn_bq': _L3_xattn_in['bq'], 'L3_xattn_Wk': _L3_xattn_in['Wk'], 'L3_xattn_bk': _L3_xattn_in['bk'], 'L3_xattn_Wv': _L3_xattn_in['Wv'], 'L3_xattn_bv': _L3_xattn_in['bv'], 'L3_xattn_Wo': _L3_xattn_in['Wo'], 'L3_xattn_bo': _L3_xattn_in['bo'], 'L3_ffn_router_w': _L3_ffn_in['router_w'], 'L3_ffn_router_b': _L3_ffn_in['router_b'], 'L3_ffn_expert_w': _L3_ffn_in['expert_w'], 'L3_ffn_expert_b': _L3_ffn_in['expert_b']}

def reference(x, ctx_1024, fside_1x16xSxS2_0, mask_Bx1xSxS2_ik1, mask_Bx1xSxS2_fk0, g_xattn, g_ffn, L0_xattn_W_q, L0_xattn_b_q, L0_xattn_W_k, L0_xattn_b_k, L0_xattn_W_v, L0_xattn_b_v, L0_xattn_W_o, L0_xattn_b_o, L0_ffn_fast_b, L0_ffn_w_fc, L0_ffn_w_proj, L0_ffn_u, L0_ffn_v, L0_ffn_gate, L1_xattn_w_q, L1_xattn_w_k, L1_xattn_w_v, L1_xattn_w_o, L1_ffn_gate_weight, L1_ffn_shared_gate_up, L1_ffn_shared_down, L1_ffn_experts_gate_up, L1_ffn_experts_down, L2_xattn_wq, L2_xattn_wk, L2_xattn_wv, L2_xattn_wo, L2_xattn_bo, L2_xattn_w1, L2_xattn_b1, L2_xattn_w2, L2_xattn_b2, L2_xattn_ln1_g, L2_xattn_ln1_b, L2_xattn_ln2_g, L2_xattn_ln2_b, L2_ffn_router_w, L2_ffn_router_b, L2_ffn_expert_weights, L3_xattn_Wq, L3_xattn_bq, L3_xattn_Wk, L3_xattn_bk, L3_xattn_Wv, L3_xattn_bv, L3_xattn_Wo, L3_xattn_bo, L3_ffn_router_w, L3_ffn_router_b, L3_ffn_expert_w, L3_ffn_expert_b):
    import jax
    import jax.numpy as jnp

    def _L0_xattn_ref(Q, K, V, mask, attn_bias, W_q, b_q, W_k, b_k, W_v, b_v, W_o, b_o):
        import jax, jax.numpy as jnp
        import numpy as np
        import math
        D_MODEL = 128
        NUM_HEADS = 16
        D_K = D_MODEL // NUM_HEADS
        B, L = (4, 256)

        def _nan_clamp(x):
            x = jnp.where(jnp.isnan(x), 0.0, x)
            x = jnp.where(jnp.isposinf(x), 10000.0, x)
            x = jnp.where(jnp.isneginf(x), -10000.0, x)
            return x

        def _split_heads(x):
            b, l, _ = x.shape
            return x.reshape(b, l, NUM_HEADS, D_K).transpose(0, 2, 1, 3)
        q = _split_heads(Q @ W_q.T + b_q)
        k = _split_heads(K @ W_k.T + b_k)
        v = _split_heads(V @ W_v.T + b_v)
        q = _nan_clamp(q)
        k = _nan_clamp(k)
        v = _nan_clamp(v)
        bias = jnp.clip(_nan_clamp(attn_bias), -10000.0, 10000.0)
        scale = 1.0 / math.sqrt(D_K)
        logits = jnp.einsum('bhqd,bhkd->bhqk', q.astype(jnp.float32), k.astype(jnp.float32)) * scale
        logits = logits + bias.astype(jnp.float32)
        logits = jnp.where(mask == 0, -10000.0, logits)
        probs = jax.nn.softmax(logits, axis=-1)
        probs = jnp.where(jnp.isnan(probs), 0.0, probs)
        out = jnp.einsum('bhqk,bhkd->bhqd', probs, v.astype(jnp.float32)).astype(q.dtype)
        out = out.transpose(0, 2, 1, 3).reshape(Q.shape[0], Q.shape[1], D_MODEL)
        return out @ W_o.T + b_o

    def _L0_ffn_ref(x, fast_b, w_fc, w_proj, u, v, gate):
        import jax, jax.numpy as jnp
        import numpy as np

        def _bitlinear(x, w_latent):
            scale = jax.lax.stop_gradient(jnp.clip(jnp.mean(jnp.abs(w_latent), axis=1, keepdims=True), 1e-05, None))
            tern = jnp.clip(jnp.round(w_latent / scale), -1.0, 1.0)
            w = w_latent + jax.lax.stop_gradient(tern - w_latent)
            return x @ (w * scale).T
        h = _bitlinear(x, w_fc) + gate * (x @ v.T @ fast_b.T @ u.T)
        r = jnp.maximum(h, 0.0)
        return _bitlinear(r * r, w_proj)

    def _L1_xattn_ref(query, kv_source, w_q, w_k, w_v, w_o):
        import jax, jax.numpy as jnp
        import numpy as np
        D_MODEL = 128
        N_HEADS = 16
        HEAD_DIM = D_MODEL // N_HEADS
        B, T_q, _ = query.shape
        T_kv = kv_source.shape[1]
        q = (query @ w_q.T).reshape(B, T_q, N_HEADS, HEAD_DIM)
        k = (kv_source @ w_k.T).reshape(B, T_kv, N_HEADS, HEAD_DIM)
        v = (kv_source @ w_v.T).reshape(B, T_kv, N_HEADS, HEAD_DIM)
        scale = HEAD_DIM ** (-0.5)
        attn = jax.nn.softmax(jnp.einsum('bqhd,bkhd->bhqk', q, k) * scale, axis=-1)
        out = jnp.einsum('bhqk,bkhd->bqhd', attn, v).reshape(B, T_q, D_MODEL)
        return out @ w_o.T

    def _L1_ffn_ref(hidden_states, gate_weight, shared_gate_up, shared_down, experts_gate_up, experts_down):
        import jax, jax.numpy as jnp
        import numpy as np
        B, S, D = (4, 256, 128)
        E = 8
        TOPK = 2
        I = 938

        def _swiglu(x, gate_up, down):
            h = jnp.einsum('bsd,fd->bsf', x, gate_up)
            g, u = jnp.split(h, 2, axis=-1)
            return jnp.einsum('bsi,di->bsd', jax.nn.silu(g) * u, down)
        x = hidden_states
        out = _swiglu(x, shared_gate_up, shared_down)
        logits = jnp.einsum('bsd,ed->bse', x, gate_weight)
        probs = jax.nn.softmax(logits.astype(jnp.float32), axis=-1)
        top_p, sel = jax.lax.top_k(probs, TOPK)
        top_p = top_p / (jnp.sum(top_p, axis=-1, keepdims=True) + 1e-08)
        cw = jnp.sum(top_p[..., None] * jax.nn.one_hot(sel, E, dtype=top_p.dtype), axis=2)
        for e in range(E):
            y = _swiglu(x, experts_gate_up[e], experts_down[e])
            out = out + cw[..., e:e + 1] * y
        return out

    def _L2_xattn_ref(Q, K, V, wq, wk, wv, wo, bo, w1, b1, w2, b2, ln1_g, ln1_b, ln2_g, ln2_b):
        import jax, jax.numpy as jnp
        import numpy as np
        DIM = 128
        HEADS = 16
        DIM_HEAD = 64
        INNER = HEADS * DIM_HEAD
        MLP = 512
        EPS = 1e-05

        def _layernorm(x, g, b):
            mu = jnp.mean(x, axis=-1, keepdims=True)
            var = jnp.mean(jnp.square(x - mu), axis=-1, keepdims=True)
            return (x - mu) * jax.lax.rsqrt(var + EPS) * g + b

        def _l2norm(x):
            n = jnp.sqrt(jnp.sum(jnp.square(x), axis=-1, keepdims=True))
            return x / jnp.maximum(n, 1e-12)

        def _split_heads(x, B, N):
            return x.reshape(B, N, HEADS, DIM_HEAD).transpose(0, 2, 1, 3)
        B, Nq, _ = Q.shape
        Nk = K.shape[1]
        Qn = _layernorm(Q, ln1_g, ln1_b)
        Kn = _layernorm(K, ln1_g, ln1_b)
        Vn = _layernorm(V, ln1_g, ln1_b)
        q = _split_heads(Qn @ wq, B, Nq)
        k = _split_heads(Kn @ wk, B, Nk)
        v = _split_heads(Vn @ wv, B, Nk)
        qn = _l2norm(q)
        kn = _l2norm(k)
        attn = jnp.einsum('bhqd,bhkd->bhqk', qn, kn)
        out = jnp.einsum('bhqk,bhkd->bhqd', attn, v)
        out = out.transpose(0, 2, 1, 3).reshape(B, Nq, INNER)
        x = Q + out @ wo + bo
        xn = _layernorm(x, ln2_g, ln2_b)
        h = jax.nn.gelu(xn @ w1 + b1, approximate=False)
        return x + h @ w2 + b2

    def _L2_ffn_ref(tokens, router_w, router_b, expert_weights):
        import jax, jax.numpy as jnp
        import numpy as np
        TOP_K = 2
        EPS = 1e-10
        B, S, H = tokens.shape
        E = expert_weights.shape[0]
        logits = jnp.einsum('bsh,eh->bse', tokens, router_w) + router_b
        probs = jax.nn.softmax(logits, axis=-1)
        top_p, top_i = jax.lax.top_k(probs, TOP_K)
        w = top_p / (jnp.sum(top_p, axis=-1, keepdims=True) + EPS)
        x = tokens.reshape(-1, H)
        idx = top_i.reshape(-1, TOP_K)
        wf = w.reshape(-1, TOP_K)
        y_all = jnp.einsum('nh,ehd->ned', x, expert_weights)
        y_k = jnp.take_along_axis(y_all, idx[:, :, None], axis=1)
        out = jnp.einsum('nk,nkh->nh', wf, y_k)
        acc = jnp.clip(jnp.sum(wf, axis=-1), EPS, None)
        out = (out / acc[:, None]).reshape(B, S, H)
        scale = 1.0 + jnp.sum(w, axis=-1, keepdims=True) * EPS
        return out * scale

    def _L3_xattn_ref(q_in, k_in, v_in, m_in, Wq, bq, Wk, bk, Wv, bv, Wo, bo):
        import jax, jax.numpy as jnp
        import numpy as np
        D_MODEL = 128
        NUM_HEADS = 16
        DEPTH = D_MODEL // NUM_HEADS
        B, S = (4, 256)

        def _split(t):
            b, s, _ = t.shape
            return t.reshape(b, s, NUM_HEADS, DEPTH).transpose(0, 2, 1, 3)
        q = _split(q_in @ Wq.T + bq)
        k = _split(k_in @ Wk.T + bk)
        v = _split(v_in @ Wv.T + bv)
        scale = jnp.sqrt(jnp.asarray(DEPTH, jnp.float32))
        scores = jnp.einsum('bhqd,bhkd->bhqk', q, k) / scale
        scores = scores - m_in * 1000000.0
        attn = jax.nn.softmax(scores, axis=-1)
        out = jnp.einsum('bhqk,bhkd->bhqd', attn, v)
        out = out.transpose(0, 2, 1, 3).reshape(q_in.shape[0], -1, D_MODEL)
        return out @ Wo.T + bo

    def _L3_ffn_ref(x, router_w, router_b, expert_w, expert_b):
        import jax, jax.numpy as jnp
        import numpy as np
        B, S, H, E = (4, 256, 128, 8)
        b, s, h = x.shape
        xt = x.reshape(b * s, h)
        logits = xt @ router_w + router_b
        probs = jax.nn.softmax(logits, axis=-1)
        gate = jnp.max(probs, axis=-1)
        idx = jnp.argmax(probs, axis=-1)
        out_all = jnp.einsum('th,ehd->ted', xt, expert_w) + expert_b[None, :, :]
        e_out = jnp.take_along_axis(out_all, idx[:, None, None], axis=1)[:, 0, :]
        y = gate[:, None] * e_out
        return y.reshape(b, s, h)
    x = x + jnp.tanh(g_xattn[0]) * _L0_xattn_ref(_layernorm(x, axis=-1), ctx_1024, ctx_1024, mask_Bx1xSxS2_ik1, fside_1x16xSxS2_0, L0_xattn_W_q, L0_xattn_b_q, L0_xattn_W_k, L0_xattn_b_k, L0_xattn_W_v, L0_xattn_b_v, L0_xattn_W_o, L0_xattn_b_o)
    x = x + jnp.tanh(g_ffn[0]) * _L0_ffn_ref(_layernorm(x, axis=-1), L0_ffn_fast_b, L0_ffn_w_fc, L0_ffn_w_proj, L0_ffn_u, L0_ffn_v, L0_ffn_gate)
    x = x + jnp.tanh(g_xattn[1]) * _L1_xattn_ref(_layernorm(x, axis=-1), ctx_1024, L1_xattn_w_q, L1_xattn_w_k, L1_xattn_w_v, L1_xattn_w_o)
    x = x + jnp.tanh(g_ffn[1]) * _L1_ffn_ref(_layernorm(x, axis=-1), L1_ffn_gate_weight, L1_ffn_shared_gate_up, L1_ffn_shared_down, L1_ffn_experts_gate_up, L1_ffn_experts_down)
    x = x + jnp.tanh(g_xattn[2]) * _L2_xattn_ref(_layernorm(x, axis=-1), ctx_1024, ctx_1024, L2_xattn_wq, L2_xattn_wk, L2_xattn_wv, L2_xattn_wo, L2_xattn_bo, L2_xattn_w1, L2_xattn_b1, L2_xattn_w2, L2_xattn_b2, L2_xattn_ln1_g, L2_xattn_ln1_b, L2_xattn_ln2_g, L2_xattn_ln2_b)
    x = x + jnp.tanh(g_ffn[2]) * _L2_ffn_ref(_layernorm(x, axis=-1), L2_ffn_router_w, L2_ffn_router_b, L2_ffn_expert_weights)
    x = x + jnp.tanh(g_xattn[3]) * _L3_xattn_ref(_layernorm(x, axis=-1), ctx_1024, ctx_1024, mask_Bx1xSxS2_fk0, L3_xattn_Wq, L3_xattn_bq, L3_xattn_Wk, L3_xattn_bk, L3_xattn_Wv, L3_xattn_bv, L3_xattn_Wo, L3_xattn_bo)
    x = x + jnp.tanh(g_ffn[3]) * _L3_ffn_ref(_layernorm(x, axis=-1), L3_ffn_router_w, L3_ffn_router_b, L3_ffn_expert_w, L3_ffn_expert_b)
    return x

_drawn_inputs = setup_inputs


def setup_inputs(seed=0):
    import zlib

    import numpy as np

    out = dict(_drawn_inputs(seed))
    spreads = {'L2_xattn_bo': (0.0, 0.513),
     'L2_xattn_b1': (0.0, 0.8),
     'L2_xattn_b2': (0.0, 0.544),
     'L2_xattn_ln1_g': (1.0, 0.2),
     'L2_xattn_ln1_b': (0.0, 0.1),
     'L2_xattn_ln2_g': (1.0, 0.6),
     'L2_xattn_ln2_b': (0.0, 0.8),
     'L3_ffn_router_b': (0.0, 0.591),
     'L3_ffn_expert_b': (0.0, 0.8)}
    factors = {'g_ffn': 22.92,
     'L0_xattn_b_k': 64.0,
     'L0_ffn_fast_b': 8.0,
     'L0_ffn_w_fc': 3.107,
     'L0_ffn_u': 8.0,
     'L0_ffn_v': 8.0,
     'L2_xattn_w1': 6.793,
     'L2_xattn_w2': 6.447,
     'L2_ffn_router_b': 25.978,
     'L3_xattn_bq': 64.0,
     'L3_xattn_bk': 64.0,
     'L3_xattn_bv': 49.674,
     'L3_xattn_bo': 51.708,
     'L3_xattn_Wq': 2.855,
     'L3_xattn_Wk': 2.826}
    for name, (base, spread) in spreads.items():
        noise = np.random.default_rng([zlib.crc32(name.encode()), seed]).standard_normal(out[name].shape)
        drawn = base * np.exp(spread * noise) if base else spread * noise
        out[name] = jnp.asarray(drawn.astype(out[name].dtype))
    for name, factor in factors.items():
        out[name] = (out[name] * factor).astype(out[name].dtype)
    return out
```

```python
import math
from contextlib import ExitStack

import numpy as np
import concourse.bass as bass
from concourse import mybir

F32 = mybir.dt.float32
I32 = mybir.dt.int32
ALU = mybir.AluOpType
ACT = mybir.ActivationFunctionType
AX = mybir.AxisListType

B, S, KEYS, D = 32, 56, 1500, 128
T = B * S
PAIR = 2 * S
TILES = T // PAIR
QUAD = 4 * PAIR
NQ = T // QUAD
H, DH = 16, 8
HP = H // 2
CH, KC = 12, 125
THIRD = KEYS // 3
BIG = 2.0 ** 100
LOW = -3.0e38
FLT_MAX = float(np.finfo(np.float32).max)
MASKED = -10000.0
EPS = 1e-5
E = 8
F1, F1C, F1K = 938, 118, 8
H2, DH2 = 16, 64


STEPS = (0, 1, "k", 2, 3, 4, 5, "v", 6, 7)
TURNED = (-2, -1, None, 0, 1, 2, 3, 4, 5, None)
SLOT = (0, 1, 1, 0, 1, 0, 0, 1)


class Names:
    pass


def wait(eng, sem, count):
    if isinstance(count, int) and count <= 0:
        return
    eng.wait_ge(sem, count)


def sequences(eng, body):
    for n in (0, 1):
        body(n, n, 0)
    with eng.Fori(1, B // 2 - 1) as half:
        for j in (0, 1):
            body(half * 2 + j, j, half)
    for n in (B - 2, B - 1):
        body(n, n % 2, n // 2)


def is_at(n, where):
    return isinstance(n, int) and n == where


class Chain:

    def __init__(self, eng, sem):
        self.eng, self.sem, self.n = eng, sem, 0

    def __call__(self, ins):
        self.n += 1
        ins.then_inc(self.sem, 1)
        self.eng.wait_ge(self.sem, self.n)


def scope(nc, name):
    ctx = ExitStack()
    r = Names()
    r.ctx = ctx
    r.sb = lambda n, shape, dt=F32: ctx.enter_context(nc.sbuf_tensor(f"{name}_{n}", shape, dt))
    r.ps = lambda n, shape: ctx.enter_context(nc.psum_tensor(f"{name}_{n}", shape, F32))
    sems = []

    def sem(n):
        sems.append(nc.alloc_semaphore(f"{name}_{n}"))
        return sems[-1]

    def clear():
        nc.clear_and_free_semaphores(sems)
        nc.all_engine_barrier()

    r.sem = sem
    ctx.callback(clear)
    return r


def setup(nc, g, a):
    r = scope(nc, "setup")
    with r.ctx:
        loaded, tanhs = r.sem("loaded"), r.sem("tanhs")
        with nc.Block() as block:
            @block.sync
            def _(sp):
                sp.dma_start(g.x[:], a["x"].rearrange("(t p) d -> p t d", p=PAIR)).then_inc(loaded, 16)
                sp.dma_start(g.ident[:], a["c_ident"]).then_inc(loaded, 16)
                sp.dma_start(g.gates[:, 0:4], a["g_xattn"].partition_broadcast(PAIR)).then_inc(loaded, 16)
                sp.dma_start(g.gates[:, 4:8], a["g_ffn"].partition_broadcast(PAIR)).then_inc(loaded, 16)
                sp.wait_ge(loaded, 64)

            @block.scalar
            def _(act):
                act.wait_ge(loaded, 64)
                act.activation(g.gates[:], g.gates[:], ACT.Tanh).then_inc(tanhs, 1)
                act.wait_ge(tanhs, 1)


def norm(nc, g, name, gate=None, out=None, twice=None, only_y=None):
    r = scope(nc, name)
    with r.ctx:
        x = r.sb("y_rows", [PAIR, TILES, D]) if only_y else g.x
        stats = r.sb("stats", [PAIR, TILES, 6])
        mv = r.sb("mv", [PAIR, TILES, 2])
        sd = r.sb("sd", [PAIR, TILES])
        rs = r.sb("rs", [PAIR, TILES])
        xn = r.sb("xn", [PAIR, TILES, D])
        py = r.ps("py", [128, NQ, 512])
        px = r.ps("px", [128, NQ, 512])
        y_turned, x_ready, steps, var_ready, sd_ready, xn_ready, xn_turned, copied, stored = (
            r.sem(n) for n in ("y_turned", "x_ready", "steps", "var_ready", "sd_ready", "xn_ready",
                               "xn_turned", "copied", "stored"))
        rounds = 2 if twice else 1
        with nc.Block() as block:
            @block.tensor
            def _(pe):
                if gate is not None or only_y:
                    for t in range(TILES):
                        last = pe.transpose(py[0:PAIR, t // 4, (t % 4) * D:(t % 4 + 1) * D],
                                            g.y_t[:, t * PAIR:(t + 1) * PAIR], g.ident[:])
                        if t % 4 == 3:
                            last.then_inc(y_turned, 1)
                if out is not None:
                    return
                for rd in range(rounds):
                    for t in range(TILES):
                        pe.wait_ge(xn_ready, rd * TILES + t + 1)
                        if rd and t % 4 == 0:
                            pe.wait_ge(copied, t // 4 + 1)
                        last = pe.transpose(px[:, t // 4, (t % 4) * PAIR:(t % 4 + 1) * PAIR],
                                            xn[:, t, :], g.ident[0:PAIR, 0:PAIR])
                        if t % 4 == 3:
                            last.then_inc(xn_turned, 1)

            @block.vector
            def _(dve):
                if gate is not None or only_y:
                    for q in range(NQ):
                        dve.wait_ge(y_turned, q + 1)
                        xq = x[:, 4 * q:4 * q + 4, :].rearrange("p t d -> p (t d)")
                        if only_y:
                            dve.tensor_copy(xq, py[0:PAIR, q, :]).then_inc(x_ready, 1)
                            continue
                        dve.scalar_tensor_tensor(xq, py[0:PAIR, q, :], g.gates[:, gate:gate + 1], xq,
                                                 ALU.mult, ALU.add).then_inc(x_ready, 1)
                if out is not None:
                    return
                chain = Chain(dve, steps)
                for rd in range(rounds):
                    src = x if rd == 0 else xn
                    if rd:
                        dve.wait_ge(xn_turned, NQ)
                        dve.wait_ge(xn_ready, TILES)
                    for t in range(TILES):
                        if (gate is not None or only_y) and t % 4 == 0 and rd == 0:
                            dve.wait_ge(x_ready, t // 4 + 1)
                        last = dve.bn_stats(stats[:, t, :], src[:, t, :])
                    chain(last)
                    for t in range(TILES):
                        last = dve.bn_aggr(mv[:, t, :], stats[:, t, :])
                    chain(last)
                    dve.tensor_scalar(sd[:], mv[:, :, 1], EPS, None, ALU.add).then_inc(var_ready, 1)
                    dve.wait_ge(sd_ready, rd + 1)
                    chain(dve.reciprocal(rs[:], sd[:]))
                    for t in range(TILES):
                        dve.tensor_scalar(xn[:, t, :], src[:, t, :], mv[:, t, 0:1], rs[:, t:t + 1],
                                          ALU.subtract, ALU.mult).then_inc(xn_ready, 1)

            @block.scalar
            def _(act):
                if out is not None:
                    return
                for rd in range(rounds):
                    act.wait_ge(var_ready, rd + 1)
                    act.activation(sd[:], sd[:], ACT.Sqrt).then_inc(sd_ready, 1)
                    for q in range(NQ):
                        act.wait_ge(xn_turned, rd * NQ + q + 1)
                        cols = slice(q * QUAD, (q + 1) * QUAD)
                        affine = only_y or (rd and twice)
                        if not affine:
                            act.activation(g.xn_t[:, cols], px[:, q, 0:QUAD], ACT.Copy).then_inc(copied, 1)
                        else:
                            act.activation(g.z_t[:, cols], px[:, q, 0:QUAD], ACT.Identity,
                                           bias=affine[1], scale=affine[0]).then_inc(copied, 1)

            @block.sync
            def _(sp):
                if out is not None:
                    sp.wait_ge(x_ready, NQ)
                    sp.dma_start(out.rearrange("(t p) d -> p t d", p=PAIR), g.x[:]).then_inc(stored, 16)
                    sp.wait_ge(stored, 16)


def attention(nc, g, name, a, w, mode):
    r = scope(nc, name)
    select, plain, add = mode == "select", mode == "plain", mode == "add"
    with r.ctx:
        wq, wk, wv, wo = (r.sb(n, [D, D]) for n in ("wq", "wk", "wv", "wo"))
        bq, bk, bo = (r.sb(n, [D, 1]) for n in ("bq", "bk", "bo"))
        bv = r.sb("bv", [128, D])
        q_t = g.y_t
        q_blocks = r.sb("q_blocks", [D, 2, H, S])
        head_of = r.sb("head_of", [D, H])
        in_group = r.sb("in_group", [D, 4])
        head_rows = r.sb("head_rows", [PAIR, HP, D])
        eye2 = r.sb("eye2", [PAIR, S])
        ctx_t = r.sb("ctx_t", [D, KEYS])
        k_t = r.sb("k_t", [D, 2, KEYS])
        v = r.sb("v", [KC, 2, CH, D])
        probs = r.sb("probs", [PAIR, 2, KEYS])
        probs_t = r.sb("probs_t", [KC, CH, H * S])
        top = r.sb("top", [PAIR, HP])
        neg_top = r.sb("neg_top", [PAIR, 2, HP])
        sums = r.sb("sums", [PAIR, 2, HP])
        inv = r.sb("inv", [PAIR, HP])
        NR = 2 if select else 1
        spread = r.sb("spread", [PAIR, HP, NR, S])
        diag = r.sb("diag", [D, 4, S])
        mixed = r.sb("mixed", [D, S])
        scores = [r.ps(f"scores{i}", [128, 3, 512]) for i in range(2)]
        pt = r.ps("pt", [128, 512])
        po = r.ps("po", [128, 512])
        if not plain:
            shift = r.sb("shift", [PAIR, 2, KEYS])
        if add:
            mask = r.sb("mask", [PAIR, 1, KEYS])
        if select:
            mask = r.sb("mask", [PAIR, 1, KEYS], I32)
            out_t = r.sb("out_t", [KC, 2, CH, S])
            push = r.sb("push", [PAIR, KEYS])
            bias = r.sb("bias", [PAIR, HP, KEYS])
            counted = r.sb("counted", [PAIR, 2])
            floor = r.sb("floor", [PAIR, 1])
            tenk = r.sb("tenk", [PAIR, 1])
            odd = r.sb("odd", [128, CH * D], I32)
            stand_ins = r.sb("stand_ins", [128, 2, 3])
            share = r.sb("share", [PAIR, HP])
            share_den = r.sb("share_den", [PAIR, HP])
            out_sum = r.sb("out_sum", [D, S])
            out_part = r.sb("out_part", [D, S])

        (const_in, steps, psteps, q_turned, q_ready, blocks_ready, ctx_in, scores_ready, k_turned, k_ready,
         v_turned, v_ready, top_ready, probs_ready, logits_ready, pt_ready, act_copied, dve_copied,
         spread_ready, pv_ready, attn_ready, y_turned, mask_in, mask_t_in, shift_ready, push_ready,
         out_t_ready, counted_ready, guarded, raw_top, inv_steps, share_ready, clean_steps, mask_t_in1, held) = (
            r.sem(n) for n in (
                "const_in", "steps", "psteps", "q_turned", "q_ready", "blocks_ready", "ctx_in", "scores_ready",
                "k_turned", "k_ready", "v_turned", "v_ready", "top_ready", "probs_ready", "logits_ready",
                "pt_ready", "act_copied", "dve_copied", "spread_ready", "pv_ready", "attn_ready",
                "y_turned", "mask_in", "mask_t_in", "shift_ready", "push_ready", "out_t_ready",
                "counted_ready", "guarded", "raw_top", "inv_steps", "share_ready", "clean_steps", "mask_t_in1", "held"))
        mask_t_in = (mask_t_in, mask_t_in1)
        banks_free = probs_ready if plain else logits_ready
        by_act = (0, 1, 2) if select else (0, 2)
        scale = 1.0 / math.sqrt(DH)

        def hold(eng):
            eng.sem_inc(held, 1)

        GUARD = 6
        GUARD_Q = 2 * GUARD
        GUARD_END = GUARD_Q + B * 2 * GUARD

        consts = [(wq, w["wq"]), (wk, w["wk"]), (wv, w["wv"]), (wo, w["wo"]), (head_of, a["c_head_of"]),
                  (in_group, a["c_in_group"]), (head_rows, a["c_head_rows"]), (eye2, a["c_eye2"])]
        if w["bq"] is not None:
            consts += [(bq, w["bq"]), (bk, w["bk"]), (bo, w["bo"]), (bv, w["bv"].partition_broadcast(128))]
        if select:
            consts += [(bias, a["bias"])]
        nconst = 16 * len(consts)

        with nc.Block() as block:
            @block.sync
            def _(sp):
                for dst, src in consts:
                    sp.dma_start(dst[:], src).then_inc(const_in, 16)

                def loads(n, j, half):
                    wait(sp, v_turned, n)
                    sp.dma_start(ctx_t[:], a["ctx_t"][n]).then_inc(ctx_in, 16)
                    if add or select:
                        wait(sp, push_ready, n)
                        if select:
                            wait(sp, counted_ready, n)
                        for i in range(2):
                            sp.dma_start(mask[i * S:(i + 1) * S, 0, :], w["mask"][n]).then_inc(mask_in, 16)
                    if select:
                        wait(sp, pv_ready, n - 1)
                        sp.dma_start(out_t[:, j, :, :].bitcast(I32), w["mask_t"][n]).then_inc(mask_t_in[j], 16)

                sequences(sp, loads)

            @block.gpsimd
            def _(pool):
                chain = Chain(pool, psteps)
                if w["bq"] is None:
                    for t in (bq, bk, bo, bv):
                        last = pool.memset(t[:], 0.0)
                    chain(last)
                if select:
                    for i, value in enumerate((0.0, -MASKED, MASKED)):
                        pool.memset(stand_ins[:, 0, i:i + 1], value)
                        pool.memset(stand_ins[:, 1, i:i + 1], value * scale)
                    chain(pool.memset(tenk[:], MASKED))
                pool.wait_ge(const_in, nconst)

                def prepare(n, j, half):
                    if select:
                        wait(pool, guarded, GUARD_Q)
                    else:
                        wait(pool, q_ready, NQ)
                    wait(pool, scores_ready, (n - 1) * HP)
                    qs = q_t[:, n * S:(n + 1) * S] if isinstance(n, int) else q_t[:, bass.ds(n * S, S)]
                    pool.tensor_tensor(q_blocks[:, j, :, :],
                                       qs.unsqueeze(1).broadcast_to((D, H, S)),
                                       head_of[:].unsqueeze(2).broadcast_to((D, H, S)),
                                       ALU.mult).then_inc(blocks_ready, 1)
                    if add:
                        pool.wait_ge(mask_in, n * 32 + 32)
                        wait(pool, logits_ready, (n - 1) * HP)
                        hold(pool)
                        pool.tensor_scalar(shift[:, j, :], mask[:, 0, :], -1000000.0, None,
                                           ALU.mult).then_inc(push_ready, 1)
                    if select:
                        pool.wait_ge(mask_t_in[j], half * 16 + 16)
                        hold(pool)
                        pool.tensor_scalar(out_t[:, j, :, :], out_t[:, j, :, :].bitcast(I32), 0.0, None,
                                           ALU.is_equal).then_inc(out_t_ready, 1)
                        for p in range(HP):
                            if p == 0:
                                pool.wait_ge(push_ready, n + 1)
                            if p == 0:
                                wait(pool, clean_steps, 1 + 3 * HP)
                            wait(pool, logits_ready, n * HP + p - 1)
                            pool.tensor_tensor(shift[:, p % 2, :], bias[:, p, :], push[:],
                                               ALU.add).then_inc(shift_ready, 1)

                sequences(pool, prepare)

            @block.tensor
            def _(pe):
                pe.wait_ge(const_in, nconst)
                for q in range(NQ):
                    pe.matmul(scores[q // 3][:, q % 3, 0:QUAD], wq[:], g.xn_t[:, q * QUAD:(q + 1) * QUAD],
                              start=True, stop=True).then_inc(q_turned, 1)
                pe.wait_ge(q_ready, NQ)

                def k_proj(slot, c):
                    last = pe.matmul(scores[slot][:, c, 0:THIRD], wk[:],
                                     ctx_t[:, c * THIRD:(c + 1) * THIRD], start=True, stop=True)
                    if c == 2:
                        last.then_inc(k_turned, 1)

                def v_proj(slot, b):
                    for c in range(4 * b, 4 * b + 4):
                        last = pe.matmul(scores[slot][0:KC, b, (c % 4) * D:(c % 4 + 1) * D],
                                         ctx_t[:, c * KC:(c + 1) * KC], wv[:], start=True, stop=True)
                    if b == 2:
                        last.then_inc(v_turned, 1)

                def turn(n, p, t):
                    if t == 0:
                        pe.wait_ge(probs_ready, n * HP + p + 1)
                    if t == 2 and t - 1 not in by_act:
                        pe.wait_ge(dve_copied, n * HP + p + 1)
                    else:
                        wait(pe, act_copied, (n * HP + p) * len(by_act) + t)
                    for c in range(4 * t, 4 * t + 4):
                        last = pe.transpose(pt[0:KC, (c % 4) * PAIR:(c % 4 + 1) * PAIR],
                                            probs[:, p % 2, c * KC:(c + 1) * KC], g.ident[0:PAIR, 0:PAIR])
                    last.then_inc(pt_ready, 1)

                def values(m, j):
                    pe.wait_ge(act_copied, (m + 1) * HP * len(by_act))
                    if not select:
                        pe.wait_ge(dve_copied, (m + 1) * HP)
                    wait(pe, attn_ready, m)
                    if select:
                        pe.wait_ge(guarded, GUARD_END if is_at(m, B - 1) else GUARD_Q + (m * 2 + 3) * GUARD)
                    for c in range(CH):
                        for grp in range(4):
                            pe.matmul(po[32 * grp:32 * grp + 32, 0:4 * S], v[:, j, c, 32 * grp:32 * grp + 32],
                                      probs_t[:, c, grp * 4 * S:(grp + 1) * 4 * S],
                                      start=(c == 0), stop=(c == CH - 1))
                    pe.wait_ge(spread_ready, m + 1)
                    for p in range(HP):
                        last = pe.matmul(po[:, 4 * S:(4 + NR) * S], head_rows[:, p, :],
                                         spread[:, p, :, :].rearrange("p a s -> p (a s)"),
                                         start=(p == 0), stop=(p == HP - 1))
                    if select:
                        pe.wait_ge(out_t_ready, m + 1)
                        for c in range(CH):
                            last = pe.matmul(po[:, 6 * S:7 * S], v[:, j, c, :], out_t[:, j, c, :],
                                             start=(c == 0), stop=(c == CH - 1))
                    last.then_inc(pv_ready, 1)

                pe.wait_ge(ctx_in, 16)
                for c in range(3):
                    k_proj(0, c)
                for c in range(3):
                    v_proj(1, c)

                def sequence(n, j, half):
                    first, final = is_at(n, 0), is_at(n, B - 1)
                    slot_free = [(banks_free, n * HP - 1), (banks_free, n * HP), (banks_free, n * HP + 2),
                                 (k_ready, n + 2), (banks_free, n * HP + 3), (banks_free, n * HP + 4),
                                 (banks_free, n * HP + 6), (v_ready, n + 2)]
                    if final:
                        slot_free[3], slot_free[7] = (banks_free, n * HP + 1), (banks_free, n * HP + 5)
                    for step, turned in zip(STEPS, TURNED):
                        if step == "k" and not final:
                            wait(pe, banks_free, n * HP + 1)
                            pe.wait_ge(ctx_in, n * 16 + 32)
                        if step == "v" and not final:
                            wait(pe, banks_free, n * HP + 5)
                        if step == 0:
                            pe.wait_ge(blocks_ready, n + 1)
                            if select:
                                pe.wait_ge(guarded, GUARD_Q + (GUARD if first else n * 2 * GUARD))
                            pe.wait_ge(k_ready, n + 1)
                        if step == 1:
                            pe.wait_ge(v_ready, n + 1)
                        if step not in ("k", "v"):
                            wait(pe, *slot_free[step])
                        for c in range(3):
                            if step == "k":
                                if not final:
                                    k_proj(0, c)
                            elif step == "v":
                                if not final:
                                    v_proj(1, c)
                            else:
                                mm = pe.matmul(scores[SLOT[step]][0:PAIR, c, 0:THIRD],
                                               q_blocks[:, j, 2 * step:2 * step + 2, :].rearrange("p a s -> p (a s)"),
                                               k_t[:, j, c * THIRD:(c + 1) * THIRD], start=True, stop=True)
                                if c == 2:
                                    mm.then_inc(scores_ready, 1)
                            if turned is not None and turned >= 0:
                                turn(n, turned, c)
                            elif turned is not None and not first:
                                turn(n - 1, HP + turned, c)
                        if step == "k" and not first:
                            values(n - 1, 1 - j)

                sequences(pe, sequence)
                for p in (HP - 2, HP - 1):
                    for c in range(3):
                        turn(B - 1, p, c)
                values(B - 1, 1)
                pe.wait_ge(attn_ready, B)
                if select:
                    pe.wait_ge(guarded, GUARD_END + 4)
                for q in range(NQ):
                    pe.matmul(scores[q // 3][:, q % 3, 0:QUAD], wo[:], q_t[:, q * QUAD:(q + 1) * QUAD],
                              start=True, stop=True).then_inc(y_turned, 1)

            @block.scalar
            def _(act):
                act.wait_ge(const_in, nconst)
                if w["bq"] is None:
                    act.wait_ge(psteps, 1)
                for q in range(NQ):
                    act.wait_ge(q_turned, q + 1)
                    qs = q_t[:, q * QUAD:(q + 1) * QUAD]
                    act.activation(qs, scores[q // 3][:, q % 3, 0:QUAD], ACT.Identity,
                                   bias=bq[:]).then_inc(steps, 1)
                    act.wait_ge(steps, q + 1)
                    act.activation(qs, qs, ACT.Copy, scale=scale).then_inc(q_ready, 1)

                def k_copy(n, j):
                    act.wait_ge(k_turned, n + 1)
                    wait(act, scores_ready, (n - 1) * HP)
                    act.activation(k_t[:, j, :].rearrange("p (c k) -> p c k", c=3), scores[0][:, :, 0:THIRD],
                                   ACT.Identity, bias=bk[:]).then_inc(k_ready, 1)

                def copy(n, p, t):
                    act.wait_ge(pt_ready, (n * HP + p) * 3 + t + 1)
                    if p == 0:
                        wait(act, pv_ready, n)
                    act.activation(probs_t[:, 4 * t:4 * t + 4, p * PAIR:(p + 1) * PAIR],
                                   pt[0:KC, 0:QUAD].rearrange("p (c q) -> p c q", c=4),
                                   ACT.Copy).then_inc(act_copied, 1)

                k_copy(0, 0)

                def exp(n, j, p):
                    act.wait_ge(top_ready, n * HP + p + 1)
                    if plain:
                        wait(act, pt_ready, (n * HP + p) * 3 - 3)
                        src = scores[SLOT[p]][0:PAIR, :, 0:THIRD]
                        dst = probs[:, p % 2, :].rearrange("p (c k) -> p c k", c=3)
                    else:
                        src = dst = probs[:, p % 2, :]
                    act.activation(dst, src, ACT.Exp, bias=neg_top[:, j, p:p + 1],
                                   accum_out=sums[:, j, p:p + 1]).then_inc(probs_ready, 1)

                def close(n, j):
                    exp(n, j, HP - 1)
                    if select:
                        wait(act, spread_ready, n)
                        act.activation(share[:], neg_top[:, j, :], ACT.Exp, bias=tenk[:]).then_inc(share_ready, 1)

                made = (-1, 0, 1, None, 2, 3, 4, 5, None, 6)

                def sequence(n, j, half):
                    first, final = is_at(n, 0), is_at(n, B - 1)
                    for step, turned, p in zip(STEPS, TURNED, made):
                        for t in by_act:
                            if turned is not None and turned >= 0:
                                copy(n, turned, t)
                            elif turned is not None and not first:
                                copy(n - 1, HP + turned, t)
                            if t > 0:
                                continue
                            if p == -1 and not first:
                                close(n - 1, 1 - j)
                            if p not in (-1, None):
                                exp(n, j, p)
                            if step == "k" and not final:
                                k_copy(n + 1, 1 - j)
                        if select and p == -1:
                            act.wait_ge(push_ready, n + 1)
                            wait(act, spread_ready, n - 1)
                            act.activation(mask[:, 0, :].bitcast(F32), push[:], ACT.Copy, scale=-1.0 / BIG,
                                           accum_out=counted[:, j:j + 1]).then_inc(counted_ready, 1)

                if select:
                    act.wait_ge(psteps, 1)
                sequences(act, sequence)
                for p in (HP - 2, HP - 1):
                    for t in by_act:
                        copy(B - 1, p, t)
                        if p == HP - 2 and t == 0:
                            close(B - 1, 1)
                for q in range(NQ):
                    act.wait_ge(y_turned, q + 1)
                    act.activation(g.y_t[:, q * QUAD:(q + 1) * QUAD], scores[q // 3][:, q % 3, 0:QUAD],
                                   ACT.Identity, bias=bo[:]).then_inc(steps, 1)

            @block.vector
            def _(dve):
                dve.wait_ge(const_in, nconst)
                if w["bq"] is None:
                    dve.wait_ge(psteps, 1)
                if select:
                    clean = Chain(dve, clean_steps)
                    clean(dve.memset(shift[:, 0, :], 0.0))
                    for p in range(HP):
                        is_nan = probs[:, 0, :].bitcast(I32)
                        clean(dve.tensor_tensor(is_nan, bias[:, p, :], bias[:, p, :], ALU.not_equal))
                        clean(dve.copy_predicated(bias[:, p, :], is_nan, shift[:, 0, :]))
                        clean(dve.tensor_scalar(bias[:, p, :], bias[:, p, :], -MASKED, MASKED, ALU.min, ALU.max))

                def guard(i, x, done, scaled=0):
                    rows, cols = x.shape
                    where = odd[0:rows, 0:cols]
                    wait(dve, guarded, done)
                    if i % 2:
                        hold(dve)
                        dve.copy_predicated(x, where, stand_ins[0:rows, scaled, i // 2:i // 2 + 1].broadcast_to(
                            (rows, cols))).then_inc(guarded, 1)
                    elif i == 0:
                        dve.tensor_tensor(where, x, x, ALU.not_equal).then_inc(guarded, 1)
                    else:
                        dve.tensor_scalar(where, x, FLT_MAX if i == 2 else -FLT_MAX, None,
                                          ALU.is_gt if i == 2 else ALU.is_lt).then_inc(guarded, 1)

                def guard_keys(n, j, steps):
                    done = GUARD_Q + (0 if is_at(n, 0) else (n * 2 - 1) * GUARD)
                    for i in steps:
                        dve.wait_ge(k_ready, n + 1)
                        guard(i, k_t[:, j, :], done + i)

                def guard_values(n, j, steps):
                    done = GUARD_END - GUARD if is_at(n, B - 1) else GUARD_Q + (n * 2 + 2) * GUARD
                    for i in steps:
                        dve.wait_ge(v_ready, n + 1)
                        guard(i, v[:, j, :, :].rearrange("p c d -> p (c d)"), done + i)

                if select:
                    dve.wait_ge(psteps, 1)
                    dve.wait_ge(q_ready, NQ)
                    for h in range(2):
                        for i in range(GUARD):
                            guard(i, q_t[:, h * T // 2:(h + 1) * T // 2], h * GUARD + i, 1)
                    guard_keys(0, 0, range(GUARD))

                def push_masked(n):
                    dve.wait_ge(mask_in, n * 32 + 32)
                    wait(dve, counted_ready, n)
                    wait(dve, shift_ready, n * HP)
                    dve.tensor_scalar(push[:], mask[:, 0, :], 0.0, -BIG, ALU.is_equal,
                                      ALU.mult).then_inc(push_ready, 1)

                def v_copy(n, j):
                    dve.wait_ge(v_turned, n + 1)
                    wait(dve, pv_ready, n - 1)
                    dve.tensor_tensor(v[:, j, :, :].rearrange("p (b c) d -> p b c d", b=3),
                                      scores[1][0:KC, :, :].rearrange("p b (c d) -> p b c d", c=4),
                                      bv[0:KC, :].unsqueeze(1).unsqueeze(1).broadcast_to((KC, 3, 4, D)),
                                      ALU.add).then_inc(v_ready, 1)

                def copy(n, p):
                    dve.wait_ge(pt_ready, (n * HP + p) * 3 + 2)
                    if p == 0:
                        wait(dve, pv_ready, n)
                    dve.tensor_copy(probs_t[:, 4:8, p * PAIR:(p + 1) * PAIR],
                                    pt[0:KC, 0:QUAD].rearrange("p (c q) -> p c q", c=4)).then_inc(dve_copied, 1)

                K_INV = 5 if select else 1
                K_FIN = 5 if select else 2

                def divide(m, j):
                    dve.wait_ge(probs_ready, (m + 1) * HP)
                    at = m * (K_INV + K_FIN)
                    if select:
                        dve.wait_ge(share_ready, m + 1)
                        dve.wait_ge(counted_ready, m + 1)
                        dve.tensor_scalar(share_den[:], share[:], counted[:, j:j + 1], None,
                                          ALU.mult).then_inc(inv_steps, 1)
                        dve.wait_ge(inv_steps, at + 1)
                        dve.tensor_tensor(share_den[:], share_den[:], sums[:, j, :],
                                          ALU.add).then_inc(inv_steps, 1)
                        dve.wait_ge(inv_steps, at + 2)
                        dve.reciprocal(inv[:], share_den[:]).then_inc(inv_steps, 1)
                        dve.wait_ge(inv_steps, at + 3)
                        dve.tensor_tensor(share_den[:], share[:], inv[:], ALU.mult).then_inc(inv_steps, 1)
                        dve.wait_ge(inv_steps, at + 4)
                        wait(dve, pv_ready, m)
                        dve.tensor_tensor(spread[:, :, 1, :], eye2[:].unsqueeze(1).broadcast_to((PAIR, HP, S)),
                                          share_den[:].unsqueeze(2).broadcast_to((PAIR, HP, S)),
                                          ALU.mult).then_inc(inv_steps, 1)
                    else:
                        dve.reciprocal(inv[:], sums[:, j, :]).then_inc(inv_steps, 1)
                        dve.wait_ge(inv_steps, at + 1)
                        wait(dve, pv_ready, m)
                    dve.tensor_tensor(spread[:, :, 0, :], eye2[:].unsqueeze(1).broadcast_to((PAIR, HP, S)),
                                      inv[:].unsqueeze(2).broadcast_to((PAIR, HP, S)),
                                      ALU.mult).then_inc(spread_ready, 1)

                def finish(m):
                    dve.wait_ge(pv_ready, m + 1)
                    at = m * (K_INV + K_FIN) + K_INV
                    wait(dve, attn_ready, m)
                    dve.tensor_tensor(diag[:], po[:, 0:4 * S].rearrange("p (h q) -> p h q", h=4),
                                      in_group[:].unsqueeze(2).broadcast_to((D, 4, S)),
                                      ALU.mult).then_inc(inv_steps, 1)
                    dve.wait_ge(inv_steps, at + 1)
                    dve.tensor_reduce(mixed[:], diag[:].rearrange("p h q -> p q h"), AX.X,
                                      ALU.add).then_inc(inv_steps, 1)
                    dve.wait_ge(inv_steps, at + 2)
                    dst = q_t[:, m * S:(m + 1) * S] if isinstance(m, int) else q_t[:, bass.ds(m * S, S)]
                    if select:
                        dve.tensor_copy(out_sum[:], po[:, 6 * S:7 * S]).then_inc(inv_steps, 1)
                        dve.wait_ge(inv_steps, at + 3)
                        dve.tensor_tensor(out_part[:], out_sum[:], po[:, 5 * S:6 * S],
                                          ALU.mult).then_inc(inv_steps, 1)
                        dve.tensor_tensor(mixed[:], mixed[:], po[:, 4 * S:5 * S], ALU.mult).then_inc(inv_steps, 1)
                        dve.wait_ge(inv_steps, at + 5)
                        dve.tensor_tensor(dst, mixed[:], out_part[:], ALU.add).then_inc(attn_ready, 1)
                    else:
                        dve.tensor_tensor(dst, mixed[:], po[:, 4 * S:5 * S], ALU.mult).then_inc(attn_ready, 1)

                v_copy(0, 0)
                if select:
                    push_masked(0)
                VALUE_GUARDS = {3: (0,), 4: (1,), 5: (2,), "v": (3, 4), 7: (5,)}
                KEY_GUARDS = {"k": range(GUARD)}

                def sequence(n, j, half):
                    first, final = is_at(n, 0), is_at(n, B - 1)
                    for p, turned in zip(STEPS, TURNED):
                        if p == 1 and not first:
                            divide(n - 1, 1 - j)
                        if p == 6 and not final:
                            v_copy(n + 1, 1 - j)
                        if turned is not None and turned >= 0 and not select:
                            copy(n, turned)
                        elif turned is not None and not first and not select:
                            copy(n - 1, HP + turned)
                        if select and p in VALUE_GUARDS:
                            guard_values(n, j, VALUE_GUARDS[p])
                        if select and p in KEY_GUARDS and not final:
                            guard_keys(n + 1, 1 - j, KEY_GUARDS[p])
                        if select and p == 7 and not final:
                            push_masked(n + 1)
                        if p in ("k", "v"):
                            continue
                        if select and p == 0:
                            dve.wait_ge(counted_ready, n + 1)
                            wait(dve, top_ready, n * HP)
                            dve.tensor_scalar(floor[:], counted[:, j:j + 1], 0.5, LOW, ALU.is_lt,
                                              ALU.mult).then_inc(raw_top, 1)
                            dve.wait_ge(raw_top, n * 2 + 1)
                            dve.tensor_scalar(floor[:], floor[:], MASKED, None, ALU.add).then_inc(raw_top, 1)
                        dve.wait_ge(scores_ready, n * HP + p + 1)
                        sc = scores[SLOT[p]][0:PAIR, :, 0:THIRD]
                        wait(dve, top_ready, n * HP + p)
                        if plain:
                            dve.tensor_reduce(top[:, p:p + 1], sc, AX.XY, ALU.max).then_inc(raw_top, 1)
                            dve.wait_ge(raw_top, n * HP + p + 1)
                        else:
                            wait(dve, pt_ready, (n * HP + p) * 3 - 3)
                            if select:
                                dve.wait_ge(shift_ready, n * HP + p + 1)
                                sh = shift[:, p % 2, :]
                            else:
                                dve.wait_ge(push_ready, n + 1)
                                sh = shift[:, j, :]
                            hold(dve)
                            dve.tensor_tensor_reduce(
                                out=probs[:, p % 2, :].rearrange("p (c k) -> p c k", c=3), in0=sc,
                                in1=sh.rearrange("p (c k) -> p c k", c=3), scale=1.0, scalar=LOW,
                                op0=ALU.add, op1=ALU.max, accum_out=top[:, p:p + 1]).then_inc(logits_ready, 1)
                            dve.wait_ge(logits_ready, n * HP + p + 1)
                        wait(dve, probs_ready, (n - 1) * HP)
                        if select:
                            dve.wait_ge(raw_top, n * 2 + 2)
                            wait(dve, share_ready, n - 1)
                            dve.tensor_scalar(neg_top[:, j, p:p + 1], top[:, p:p + 1], floor[:], -1.0,
                                              ALU.max, ALU.mult).then_inc(top_ready, 1)
                        else:
                            dve.tensor_scalar(neg_top[:, j, p:p + 1], top[:, p:p + 1], -1.0, None,
                                              ALU.mult).then_inc(top_ready, 1)
                        if p == 3 and not first:
                            finish(n - 1)

                sequences(dve, sequence)
                divide(B - 1, 1)
                if not select:
                    copy(B - 1, HP - 2)
                    copy(B - 1, HP - 1)
                finish(B - 1)
                if select:
                    dve.wait_ge(attn_ready, B)
                    for h in range(2):
                        for i in (0, 1):
                            guard(i, q_t[:, h * T // 2:(h + 1) * T // 2], GUARD_END + 2 * h + i)




def hidden_layer(nc, r, block, src, up, down, chunks, rows, act_fn, put, psum, extra=None):
    up_ready, raw_free, h_ready, down_ready, y_used = (
        r.sem(n) for n in ("up_ready", "raw_free", "h_ready", "down_ready", "y_used"))
    h = r.sb("h", [rows, 2, QUAD])
    pu = [psum("pu0", [128, 512]), psum("pu1", [128, 512])]
    py = [psum("py0", [128, 512]), psum("py1", [128, 512])]
    items = [(q, k) for q in range(NQ) for k in range(chunks)]

    @block.tensor
    def _(pe):
        def add_down(i):
            q, k = items[i]
            pe.wait_ge(h_ready, i + 1)
            if k == 0:
                wait(pe, y_used, q - 1)
            pe.matmul(py[q % 2][:, 0:QUAD], down(k), h[:, i % 2, :], start=(k == 0),
                      stop=(k == chunks - 1)).then_inc(down_ready, 1)

        if extra is not None:
            extra["tensor"](pe)
        for i, (q, k) in enumerate(items):
            wait(pe, h_ready, i - 1)
            last = pe.matmul(pu[i % 2][0:rows, 0:QUAD], up(k), src[:, q * QUAD:(q + 1) * QUAD],
                             start=True, stop=extra is None)
            if extra is not None:
                last = extra["add"](pe, pu[i % 2][0:rows, 0:QUAD], q, k)
            last.then_inc(up_ready, 1)
            if i:
                add_down(i - 1)
        add_down(len(items) - 1)

    @block.scalar
    def _(act):
        if extra is not None:
            extra["scalar"](act)
        for i, (q, k) in enumerate(items):
            act.wait_ge(up_ready, i + 1)
            wait(act, down_ready, i - 1)
            act_fn(act, h[:, i % 2, :], pu[i % 2][0:rows, 0:QUAD], k, i, raw_free, h_ready).then_inc(h_ready, 1)

    @block.vector
    def _(dve):
        if extra is not None:
            extra["vector"](dve)
        for q in range(NQ):
            dve.wait_ge(down_ready, (q + 1) * chunks)
            put(dve, q, py[q % 2][:, 0:QUAD]).then_inc(y_used, 1)


def ternary(dve, chain, w, r, name, rows, cols):
    scale, half, neg = (r.sb(f"{name}_{n}", [128, rows]) for n in ("scale", "half", "neg"))
    below, tern = r.sb(f"{name}_below", [128, cols]), r.sb(f"{name}_tern", [128, cols])
    chain(dve.tensor_reduce(scale[:], w[:], AX.X, ALU.add, apply_absolute_value=True))
    chain(dve.tensor_scalar(scale[:], scale[:], 1.0 / cols, 1e-5, ALU.mult, ALU.max))
    chain(dve.tensor_scalar(half[:], scale[:], 0.5, None, ALU.mult))
    chain(dve.tensor_scalar(neg[:], scale[:], -0.5, None, ALU.mult))
    for i in range(rows):
        wi = w[:, i, :]
        chain(dve.tensor_scalar(below[:], wi, neg[:, i:i + 1], None, ALU.is_lt))
        chain(dve.scalar_tensor_tensor(tern[:], wi, half[:, i:i + 1], below[:], ALU.is_gt, ALU.subtract))
        chain(dve.tensor_tensor(tern[:], tern[:], wi, ALU.subtract))
        chain(dve.tensor_tensor(wi, wi, tern[:], ALU.add))
        chain(dve.tensor_scalar(wi, wi, scale[:, i:i + 1], None, ALU.mult))


def ffn0(nc, g, a):
    r = scope(nc, "ffn0")
    FC, RANK = 4, 16
    with r.ctx:
        w_fc, w_proj = r.sb("w_fc", [128, FC, D]), r.sb("w_proj", [128, 1, FC * D])
        fc_t, proj_t = r.sb("fc_t", [D, FC, 128]), r.sb("proj_t", [128, FC, D])
        v_t, b_t, u_t = r.sb("v_t", [D, RANK]), r.sb("b_t", [RANK, RANK]), r.sb("u_t", [RANK, FC * 128])
        gate = r.sb("gate", [RANK, 1])
        low, mid = r.sb("low", [RANK, T]), r.sb("mid", [RANK, T])
        relu = r.sb("relu", [128, QUAD])
        loaded, steps, w_ready, w_turned, w_copied, low_ready, low_copied, mid_ready, mid_copied = (
            r.sem(n) for n in ("loaded", "steps", "w_ready", "w_turned", "w_copied", "low_ready",
                               "low_copied", "mid_ready", "mid_copied"))
        pw = [r.ps("pw0", [128, 512]), r.ps("pw1", [128, 512])]
        pl = [r.ps("pl0", [128, 512]), r.ps("pl1", [128, 512])]
        loads = [(w_fc[:], a["w_fc"].rearrange("(k p) i -> p k i", p=128)), (w_proj[:, 0, :], a["w_proj"]),
                 (v_t[:], a["v_t"]), (b_t[:], a["fast_b_t"]), (u_t[:], a["u_t"]),
                 (gate[:], a["gate0"].partition_broadcast(RANK))]

        def tensor(pe):
            pe.wait_ge(w_ready, 1)
            for k in range(FC):
                last = pe.transpose(pw[0][:, k * 128:(k + 1) * 128], w_fc[:, k, :], g.ident[:])
            last.then_inc(w_turned, 1)
            for k in range(FC):
                last = pe.transpose(pw[1][:, k * D:(k + 1) * D], w_proj[:, 0, k * 128:(k + 1) * 128], g.ident[:])
            last.then_inc(w_turned, 1)
            for q in range(NQ):
                cols = slice(q * QUAD, (q + 1) * QUAD)
                wait(pe, low_copied, q - 1)
                pe.matmul(pl[q % 2][0:RANK, 0:QUAD], v_t[:], g.xn_t[:, cols], start=True,
                          stop=True).then_inc(low_ready, 1)
            for q in range(NQ):
                cols = slice(q * QUAD, (q + 1) * QUAD)
                pe.wait_ge(low_copied, NQ)
                wait(pe, mid_copied, q - 1)
                pe.matmul(pl[q % 2][0:RANK, 0:QUAD], b_t[:], low[:, cols], start=True,
                          stop=True).then_inc(mid_ready, 1)
            pe.wait_ge(mid_copied, NQ)
            pe.wait_ge(w_copied, 2)

        def scalar(act):
            act.wait_ge(loaded, 16 * len(loads))
            for i, dst in ((0, fc_t), (1, proj_t)):
                act.wait_ge(w_turned, i + 1)
                act.activation(dst[:].rearrange("p k f -> p (k f)"), pw[i][:], ACT.Copy).then_inc(w_copied, 1)
            for q in range(NQ):
                act.wait_ge(low_ready, q + 1)
                act.activation(low[:, q * QUAD:(q + 1) * QUAD], pl[q % 2][0:RANK, 0:QUAD],
                               ACT.Copy).then_inc(low_copied, 1)
            for q in range(NQ):
                act.wait_ge(mid_ready, q + 1)
                act.activation(mid[:, q * QUAD:(q + 1) * QUAD], pl[q % 2][0:RANK, 0:QUAD], ACT.Copy,
                               scale=gate[:]).then_inc(mid_copied, 1)

        def vector(dve):
            chain = Chain(dve, steps)
            dve.wait_ge(loaded, 16 * len(loads))
            ternary(dve, chain, w_fc, r, "fc", FC, D)
            ternary(dve, chain, w_proj, r, "proj", 1, FC * D)
            dve.drain().then_inc(w_ready, 1)

        def add(pe, out, q, k):
            return pe.matmul(out, u_t[:, k * 128:(k + 1) * 128], mid[:, q * QUAD:(q + 1) * QUAD],
                             start=False, stop=True)

        def square_of_relu(act, out, in_, k, i, raw_free, h_ready):
            wait(act, h_ready, i)
            act.activation(relu[:], in_, ACT.Relu).then_inc(raw_free, 1)
            act.wait_ge(raw_free, i + 1)
            return act.activation(out, relu[:], ACT.Square)

        def put(dve, q, y):
            return dve.tensor_copy(g.y_t[:, q * QUAD:(q + 1) * QUAD], y)

        with nc.Block() as block:
            @block.sync
            def _(sp):
                for dst, src in loads:
                    sp.dma_start(dst, src).then_inc(loaded, 16)

            hidden_layer(nc, r, block, g.xn_t, lambda k: fc_t[:, k, :], lambda k: proj_t[:, k, :], FC, 128,
                         square_of_relu, put, r.ps,
                         extra=dict(tensor=tensor, scalar=scalar, vector=vector, add=add))


def route(nc, g, name, a, w_router, b_router, weigh, cw, cwb, cw_t=None):
    r = scope(nc, name)
    with r.ctx:
        wr, br, order = r.sb("wr", [D, E]), r.sb("br", [PAIR, E]), r.sb("order", [PAIR, E])
        shape = [PAIR, TILES, E]
        p, t1, hot1, hot2 = (r.sb(n, shape) for n in ("p", "t1", "hot1", "hot2"))
        m1, m2, s1, s2 = (r.sb(n, [PAIR, TILES]) for n in ("m1", "m2", "s1", "s2"))
        pl = r.ps("pl", [128, TILES, E])
        pb = [r.ps(f"pb{i}", [128, 512]) for i in range(4)]
        loaded, logits_ready, steps, arg_ready, exp_ready, cw_ready, spread, act_used, dve_used, turned = (
            r.sem(n) for n in ("loaded", "logits_ready", "steps", "arg_ready", "exp_ready", "cw_ready",
                               "spread", "act_used", "dve_used", "turned"))
        wide = lambda t: t[:].unsqueeze(2).broadcast_to(tuple(shape))
        with nc.Block() as block:
            @block.sync
            def _(sp):
                sp.dma_start(wr[:], w_router).then_inc(loaded, 16)
                sp.dma_start(order[:], a["c_order"].partition_broadcast(PAIR)).then_inc(loaded, 16)
                if b_router is not None:
                    sp.dma_start(br[:], b_router.partition_broadcast(PAIR)).then_inc(loaded, 16)

            @block.tensor
            def _(pe):
                pe.wait_ge(loaded, 48 if b_router is not None else 32)
                for t in range(TILES):
                    last = pe.matmul(pl[0:PAIR, t, :], g.xn_t[:, t * PAIR:(t + 1) * PAIR], wr[:],
                                     start=True, stop=True)
                last.then_inc(logits_ready, 1)
                pe.wait_ge(cw_ready, 1)
                for i in range(E * NQ):
                    e, q = divmod(i, NQ)
                    if i >= 4:
                        pe.wait_ge(act_used if i % 2 == 0 else dve_used, i // 2 - 1)
                    for t in range(4 * q, 4 * q + 4):
                        last = pe.matmul(pb[i % 4][:, (t % 4) * PAIR:(t % 4 + 1) * PAIR],
                                         cw[:, t, e:e + 1].broadcast_to((PAIR, 128)),
                                         g.ident[0:PAIR, 0:PAIR], start=True, stop=True)
                    last.then_inc(spread, 1)
                if cw_t is not None:
                    for q in range(NQ):
                        pe.wait_ge(act_used if q % 2 == 0 else dve_used, E * NQ // 2)
                        for t in range(4 * q, 4 * q + 4):
                            last = pe.transpose(pb[q][0:E, (t % 4) * PAIR:(t % 4 + 1) * PAIR],
                                                cw[:, t, :], g.ident[0:PAIR, 0:PAIR])
                        last.then_inc(turned, 1)

            @block.scalar
            def _(act):
                act.wait_ge(arg_ready, 1)
                act.activation(p[:], p[:], ACT.Exp).then_inc(exp_ready, 1)
                for i in range(0, E * NQ, 2):
                    e, q = divmod(i, NQ)
                    act.wait_ge(spread, i + 1)
                    act.activation(cwb[:, e, q * QUAD:(q + 1) * QUAD], pb[i % 4][:, 0:QUAD],
                                   ACT.Copy).then_inc(act_used, 1)
                if cw_t is not None:
                    for q in range(NQ):
                        act.wait_ge(turned, q + 1)
                        act.activation(cw_t[:, q * QUAD:(q + 1) * QUAD], pb[q][0:E, 0:QUAD],
                                       ACT.Copy).then_inc(act_used, 1)

            @block.vector
            def _(dve):
                do = Chain(dve, steps)
                dve.wait_ge(logits_ready, 1)
                if b_router is not None:
                    do(dve.tensor_tensor(p[:], pl[0:PAIR, :, :],
                                         br[:].unsqueeze(1).broadcast_to(tuple(shape)), ALU.add))
                else:
                    do(dve.tensor_copy(p[:], pl[0:PAIR, :, :]))
                do(dve.tensor_reduce(m1[:], p[:], AX.X, ALU.max))
                dve.tensor_tensor(p[:], p[:], wide(m1), ALU.subtract).then_inc(arg_ready, 1)
                dve.wait_ge(exp_ready, 1)
                do(dve.tensor_reduce(s1[:], p[:], AX.X, ALU.add))
                do(dve.reciprocal(s1[:], s1[:]))
                do(dve.tensor_tensor(p[:], p[:], wide(s1), ALU.mult))

                def best(m, hot):
                    do(dve.tensor_reduce(m[:], p[:], AX.X, ALU.max))
                    do(dve.tensor_tensor(t1[:], p[:], wide(m), ALU.not_equal))
                    do(dve.scalar_tensor_tensor(t1[:], t1[:], 100.0,
                                                order[:].unsqueeze(1).broadcast_to(tuple(shape)),
                                                ALU.mult, ALU.add))
                    do(dve.tensor_reduce(s2[:], t1[:], AX.X, ALU.min))
                    do(dve.tensor_tensor(hot[:], wide(s2),
                                         order[:].unsqueeze(1).broadcast_to(tuple(shape)), ALU.is_equal))

                best(m1, hot1)
                if weigh == "top1":
                    dve.tensor_tensor(cw[:], hot1[:], wide(m1), ALU.mult).then_inc(cw_ready, 1)
                else:
                    do(dve.scalar_tensor_tensor(p[:], hot1[:], -2.0, p[:], ALU.mult, ALU.add))
                    best(m2, hot2)
                    eps = 1e-8 if weigh == "top2_L1" else 1e-10
                    do(dve.tensor_tensor(s1[:], m1[:], m2[:], ALU.add))
                    do(dve.tensor_scalar(s1[:], s1[:], eps, None, ALU.add))
                    do(dve.reciprocal(s1[:], s1[:]))
                    do(dve.tensor_tensor(m1[:], m1[:], s1[:], ALU.mult))
                    do(dve.tensor_tensor(m2[:], m2[:], s1[:], ALU.mult))
                    if weigh == "top2_L2":
                        do(dve.tensor_tensor(s2[:], m1[:], m2[:], ALU.add))
                        do(dve.tensor_scalar(s1[:], s2[:], eps, None, ALU.max))
                        do(dve.reciprocal(s1[:], s1[:]))
                        do(dve.tensor_scalar(s2[:], s2[:], eps, 1.0, ALU.mult, ALU.add))
                        do(dve.tensor_tensor(s1[:], s1[:], s2[:], ALU.mult))
                        do(dve.tensor_tensor(m1[:], m1[:], s1[:], ALU.mult))
                        do(dve.tensor_tensor(m2[:], m2[:], s1[:], ALU.mult))
                    do(dve.tensor_tensor(hot1[:], hot1[:], wide(m1), ALU.mult))
                    do(dve.tensor_tensor(hot2[:], hot2[:], wide(m2), ALU.mult))
                    dve.tensor_tensor(cw[:], hot1[:], hot2[:], ALU.add).then_inc(cw_ready, 1)
                for i in range(1, E * NQ, 2):
                    e, q = divmod(i, NQ)
                    dve.wait_ge(spread, i + 1)
                    dve.tensor_copy(cwb[:, e, q * QUAD:(q + 1) * QUAD], pb[i % 4][:, 0:QUAD]).then_inc(dve_used, 1)


def experts(nc, g, name, a, w_experts, cwb, b_experts=None, cw_t=None):
    r = scope(nc, name)
    with r.ctx:
        we = r.sb("we", [D, E, D])
        be = r.sb("be", [E, D])
        xs = r.sb("xs", [D, 2, T])
        py = [r.ps(f"py{q}", [128, 512]) for q in range(NQ)]
        loaded, xs_ready, xs_used, y_ready, y_copied = (
            r.sem(n) for n in ("loaded", "xs_ready", "xs_used", "y_ready", "y_copied"))
        with nc.Block() as block:
            @block.sync
            def _(sp):
                sp.dma_start(we[:], w_experts.rearrange("e h d -> h e d")).then_inc(loaded, 16)
                if b_experts is not None:
                    sp.dma_start(be[:], b_experts).then_inc(loaded, 16)

            @block.vector
            def _(dve):
                for e in range(E):
                    wait(dve, xs_used, e - 1)
                    dve.tensor_tensor(xs[:, e % 2, :], g.xn_t[:], cwb[:, e, :], ALU.mult).then_inc(xs_ready, 1)

            @block.tensor
            def _(pe):
                pe.wait_ge(loaded, 16 if b_experts is None else 32)
                if b_experts is not None:
                    for q in range(NQ):
                        pe.matmul(py[q][:, 0:QUAD], be[:], cw_t[:, q * QUAD:(q + 1) * QUAD], start=True, stop=False)
                for e in range(E):
                    pe.wait_ge(xs_ready, e + 1)
                    for q in range(NQ):
                        last = pe.matmul(py[q][:, 0:QUAD], we[:, e, :], xs[:, e % 2, q * QUAD:(q + 1) * QUAD],
                                         start=(e == 0 and b_experts is None), stop=(e == E - 1))
                    last.then_inc(xs_used, 1)

            @block.scalar
            def _(act):
                act.wait_ge(xs_used, E)
                for q in range(NQ):
                    act.activation(g.y_t[:, q * QUAD:(q + 1) * QUAD], py[q][:, 0:QUAD], ACT.Copy).then_inc(y_copied, 1)


def ffn2(nc, g, a):
    r = scope(nc, "ffn2")
    with r.ctx:
        cw, cwb = r.sb("cw", [PAIR, TILES, E]), r.sb("cwb", [128, E, T])
        route(nc, g, "route2", a, a["router2"], a["router2_b"], "top2_L2", cw, cwb)
        experts(nc, g, "experts2", a, a["experts2"], cwb)


def ffn3(nc, g, a):
    r = scope(nc, "ffn3")
    with r.ctx:
        cw, cwb, cw_t = r.sb("cw", [PAIR, TILES, E]), r.sb("cwb", [128, E, T]), r.sb("cw_t", [E, T])
        route(nc, g, "route3", a, a["router3"], a["router3_b"], "top1", cw, cwb, cw_t)
        experts(nc, g, "experts3", a, a["experts3"], cwb, a["experts3_b"], cw_t)


def ffn1(nc, g, a):
    r = scope(nc, "ffn1")
    with r.ctx:
        cw, cwb = r.sb("cw", [PAIR, TILES, E]), r.sb("cwb", [128, E + 1, T])
        route(nc, g, "route1", a, a["router1"], None, "top2_L1", cw, cwb[:, 1:, :])
        gu = r.sb("gu", [D, 2, 2 * F1])
        dn = r.sb("dn", [F1C, 2, F1K, D])
        silu, h = r.sb("silu", [F1C, 2, QUAD]), r.sb("h", [F1C, 2, QUAD])
        part = r.sb("part", [D, 2, QUAD])
        pg, pu, py = ([r.ps(f"{n}{i}", [128, 512]) for i in range(2)] for n in ("pg", "pu", "py"))
        w_in = [r.sem("w_even"), r.sem("w_odd")]
        up_ready, silu_ready, h_ready, down_ready, part_ready, sum_ready, zeroed = (
            r.sem(n) for n in ("up_ready", "silu_ready", "h_ready", "down_ready", "part_ready", "sum_ready", "zeroed"))
        items = [(q, k) for q in range(NQ) for k in range(F1K)]
        N = len(items)
        size = lambda k: min(F1C, F1 - k * F1C)
        FULL = F1C * (F1K - 1)

        def passes(eng, body):
            for n in (0, 1):
                body(n, n, 0)
            with eng.Fori(1, E // 2) as half:
                for j in (0, 1):
                    body(half * 2 + j, j, half)
            body(E, 0, E // 2)

        with nc.Block() as block:
            @block.sync
            def _(sp):
                def load(n, j, half):
                    wait(sp, down_ready, (n - 1) * N)
                    up, down = (a["shared_up_t"], a["shared_down_t"]) if is_at(n, 0) else \
                        (a["experts_up_t"][n - 1], a["experts_down_t"][n - 1])
                    sp.dma_start(gu[:, j, :], up).then_inc(w_in[j], 16)
                    sp.dma_start(dn[:, j, 0:F1K - 1, :],
                                 down[0:FULL, :].rearrange("(k p) d -> p k d", p=F1C)).then_inc(w_in[j], 16)
                    sp.dma_start(dn[0:F1 - FULL, j, F1K - 1, :], down[FULL:F1, :]).then_inc(w_in[j], 16)
                passes(sp, load)

            @block.tensor
            def _(pe):
                def down(n, j, i):
                    q, k = items[i]
                    pe.wait_ge(h_ready, n * N + i + 1)
                    if k == 0:
                        wait(pe, part_ready, n * NQ + q - 1)
                    pe.matmul(py[q % 2][:, 0:QUAD], dn[0:size(k), j, k, :], h[0:size(k), i % 2, :],
                              start=(k == 0), stop=(k == F1K - 1)).then_inc(down_ready, 1)

                def body(n, j, half):
                    pe.wait_ge(w_in[j], half * 48 + 48)
                    for i, (q, k) in enumerate(items):
                        wait(pe, h_ready, n * N + i - 1)
                        for bank, at in ((pg, 0), (pu, F1)):
                            last = pe.matmul(bank[i % 2][0:size(k), 0:QUAD],
                                             gu[:, j, at + k * F1C:at + k * F1C + size(k)],
                                             g.xn_t[:, q * QUAD:(q + 1) * QUAD], start=True, stop=True)
                        last.then_inc(up_ready, 1)
                        if i:
                            down(n, j, i - 1)
                        elif not is_at(n, 0):
                            down(n - 1, 1 - j, N - 1)
                passes(pe, body)
                down(E, 0, N - 1)

            @block.scalar
            def _(act):
                def body(n, j, half):
                    for i, (q, k) in enumerate(items):
                        act.wait_ge(up_ready, n * N + i + 1)
                        wait(act, h_ready, n * N + i - 1)
                        act.activation(silu[0:size(k), i % 2, :], pg[i % 2][0:size(k), 0:QUAD],
                                       ACT.Silu).then_inc(silu_ready, 1)
                passes(act, body)

            @block.gpsimd
            def _(pool):
                def body(n, j, half):
                    for q in range(NQ):
                        pool.wait_ge(part_ready, n * NQ + q + 1)
                        wait(pool, sum_ready, (n - 1) * NQ + q + 1)
                        cols = g.y_t[:, q * QUAD:(q + 1) * QUAD]
                        pool.tensor_tensor(cols, cols, part[:, q % 2, :], ALU.add).then_inc(sum_ready, 1)
                pool.wait_ge(zeroed, 2)
                passes(pool, body)

            @block.vector
            def _(dve):
                def take(n, q):
                    wait(dve, sum_ready, n * NQ + q - 1)
                    cols = cwb[:, n, q * QUAD:(q + 1) * QUAD] if isinstance(n, int) else \
                        cwb[:].rearrange("p e t -> p (e t)")[:, bass.ds(n * T + q * QUAD, QUAD)]
                    dve.tensor_tensor(part[:, q % 2, :], py[q % 2][:, 0:QUAD], cols, ALU.mult).then_inc(part_ready, 1)

                def body(n, j, half):
                    for i, (q, k) in enumerate(items):
                        dve.wait_ge(silu_ready, n * N + i + 1)
                        wait(dve, down_ready, n * N + i - 1)
                        dve.tensor_tensor(h[0:size(k), i % 2, :], silu[0:size(k), i % 2, :],
                                          pu[i % 2][0:size(k), 0:QUAD], ALU.mult).then_inc(h_ready, 1)
                        if k == 0 and not (is_at(n, 0) and q == 0):
                            dve.wait_ge(down_ready, n * N + i)
                            take(n if q else n - 1, (q - 1) % NQ)

                dve.memset(cwb[:, 0, :], 1.0).then_inc(zeroed, 1)
                dve.memset(g.y_t[:], 0.0).then_inc(zeroed, 1)
                dve.wait_ge(zeroed, 2)
                passes(dve, body)
                dve.wait_ge(down_ready, (E + 1) * N)
                take(E, NQ - 1)


def attention2(nc, g, a):
    whole = scope(nc, "attn2")
    INNER, HW = H2 * DH2, 512
    with whole.ctx:
        q_t = whole.sb("q_t", [128, HP, T])
        w_vo = whole.sb("w_vo", [D, H2, D])
        wk = whole.sb("wk", [D, INNER])
        bo = whole.sb("bo", [D, 1])

        r = scope(nc, "attn2q")
        with r.ctx:
            wq, wv_t, wo = r.sb("wq", [D, INNER]), r.sb("wv_t", [DH2, H2, D]), r.sb("wo", [DH2, H2, D])
            sq = r.sb("sq", [PAIR, 2, INNER])
            qn = r.sb("qn", [PAIR, 2, INNER])
            ss, rn = r.sb("ss", [PAIR, 2, H2]), r.sb("rn", [PAIR, 2, H2])
            pq = [r.ps(f"pq{i}", [128, 2, 512]) for i in range(2)]
            pt = [r.ps(f"pt{i}", [128, 2, 512]) for i in range(2)]
            loaded, vo_ready, vo_copied, q_ready, sq_ready, ss_ready, root_ready, steps, qn_ready, q_turned, act_copied, dve_copied = (
                r.sem(n) for n in ("loaded", "vo_ready", "vo_copied", "q_ready", "sq_ready", "ss_ready",
                                   "root_ready", "steps", "qn_ready", "q_turned", "act_copied", "dve_copied"))
            with nc.Block() as block:
                @block.sync
                def _(sp):
                    for dst, src in ((wq[:], a["wq2"]), (wk[:], a["wk2"]), (wv_t[:], a["wv2_t"].rearrange("(h r) c -> r h c", r=DH2)),
                                     (wo[:], a["wo2"].rearrange("(h r) c -> r h c", r=DH2)), (bo[:], a["bo2"])):
                        sp.dma_start(dst, src).then_inc(loaded, 16)
                    sp.wait_ge(loaded, 80)

                @block.tensor
                def _(pe):
                    pe.wait_ge(loaded, 80)
                    for half in range(2):
                        for h in range(8 * half, 8 * half + 8):
                            last = pe.matmul(pq[half][:, h % 8 // 4, (h % 4) * D:(h % 4 + 1) * D],
                                             wv_t[:, h, :], wo[:, h, :], start=True, stop=True)
                        last.then_inc(vo_ready, 1)

                    def turn(t):
                        pe.wait_ge(qn_ready, t + 1)
                        wait(pe, act_copied, t - 1)
                        wait(pe, dve_copied, t - 1)
                        for p in range(HP):
                            last = pe.transpose(pt[t % 2][:, p // 4, (p % 4) * PAIR:(p % 4 + 1) * PAIR],
                                                qn[:, t % 2, p * 128:(p + 1) * 128], g.ident[0:PAIR, 0:PAIR])
                        last.then_inc(q_turned, 1)

                    for t in range(TILES):
                        if t < 2:
                            pe.wait_ge(vo_copied, t + 1)
                        wait(pe, qn_ready, t - 1)
                        for c in range(2):
                            last = pe.matmul(pq[t % 2][0:PAIR, c, :], g.z_t[:, t * PAIR:(t + 1) * PAIR],
                                             wq[:, c * HW:(c + 1) * HW], start=True, stop=True)
                        last.then_inc(q_ready, 1)
                        if t:
                            turn(t - 1)
                    turn(TILES - 1)

                @block.scalar
                def _(act):
                    for half in range(2):
                        act.wait_ge(vo_ready, half + 1)
                        act.activation(w_vo[:, 8 * half:8 * half + 8, :].rearrange("p h d -> p (h d)"),
                                       pq[half][:].rearrange("p a b -> p (a b)"), ACT.Copy).then_inc(vo_copied, 1)

                    def copy(t):
                        act.wait_ge(q_turned, t + 1)
                        act.activation(q_t[:, 0:4, t * PAIR:(t + 1) * PAIR],
                                       pt[t % 2][:, 0, 0:QUAD].rearrange("p (a b) -> p a b", a=4),
                                       ACT.Copy).then_inc(act_copied, 1)
                    for t in range(TILES):
                        act.wait_ge(q_ready, t + 1)
                        wait(act, ss_ready, t - 1)
                        act.activation(sq[:, t % 2, :].rearrange("p (a b) -> p a b", a=2), pq[t % 2][0:PAIR, :, :],
                                       ACT.Square).then_inc(sq_ready, 1)
                        act.wait_ge(ss_ready, t + 1)
                        act.activation(ss[:, t % 2, :], ss[:, t % 2, :], ACT.Sqrt).then_inc(root_ready, 1)
                        if t:
                            copy(t - 1)
                    copy(TILES - 1)

                @block.vector
                def _(dve):
                    chain = Chain(dve, steps)

                    def copy(t):
                        dve.wait_ge(q_turned, t + 1)
                        dve.tensor_copy(q_t[:, 4:8, t * PAIR:(t + 1) * PAIR],
                                        pt[t % 2][:, 1, 0:QUAD].rearrange("p (a b) -> p a b", a=4)).then_inc(dve_copied, 1)
                    for t in range(TILES):
                        dve.wait_ge(sq_ready, t + 1)
                        dve.tensor_reduce(ss[:, t % 2, :], sq[:, t % 2, :].rearrange("p (h d) -> p h d", h=H2),
                                          AX.X, ALU.add).then_inc(ss_ready, 1)
                        if t:
                            copy(t - 1)
                        dve.wait_ge(root_ready, t + 1)
                        chain(dve.tensor_scalar(rn[:, t % 2, :], ss[:, t % 2, :], 1e-12, None, ALU.max))
                        chain(dve.reciprocal(rn[:, t % 2, :], rn[:, t % 2, :]))
                        wait(dve, q_turned, t - 1)
                        dve.tensor_tensor(qn[:, t % 2, :].rearrange("p (h d) -> p h d", h=H2),
                                          pq[t % 2][0:PAIR, :, :].rearrange("p a (h d) -> p (a h) d", h=8),
                                          rn[:, t % 2, :].unsqueeze(2).broadcast_to((PAIR, H2, DH2)),
                                          ALU.mult).then_inc(qn_ready, 1)
                    copy(TILES - 1)

        r = scope(nc, "attn2k")
        with r.ctx:
            ctx = r.sb("ctx", [KC, 2, CH, D])
            cn = r.sb("cn", [KC, 2, CH, D])
            gain, shift = r.sb("gain", [KC, D]), r.sb("shift", [KC, D])
            stats, mv = r.sb("stats", [KC, CH, 6]), r.sb("mv", [KC, CH, 2])
            var, rs = r.sb("var", [KC, CH]), r.sb("rs", [KC, CH])
            cn_t = r.sb("cn_t", [D, 2, KC])
            sq, kn = r.sb("sq", [KC, 2, INNER]), r.sb("kn", [KC, 2, INNER])
            ss, rn = r.sb("ss", [KC, 2, H2]), r.sb("rn", [KC, 2, H2])
            gram = r.sb("gram", [D, INNER])
            state = r.sb("state", [128, HP, D])
            q_now = r.sb("q_now", [128, HP, S])
            pk = [r.ps(f"pk{i}", [128, 2, 512]) for i in range(2)]
            pg = r.ps("pg", [128, 2, 512])
            pt, pz = r.ps("pt", [128, 512]), r.ps("pz", [128, 512])
            (held, const_in, ctx_even, ctx_odd, steps, var_ready, root_ctx, raw_ready, scaled, cn_ready, c_turned, c_copied, k_ready,
             sq_ready, ss_ready, root_ready, clipped, kn_ready, summed, gram_act, gram_dve, state_ready, state_copied,
             q_copied, y_ready, y_copied) = (r.sem(n) for n in (
                 "held", "const_in", "ctx_even", "ctx_odd", "steps", "var_ready", "root_ctx", "raw_ready", "scaled", "cn_ready", "c_turned",
                 "c_copied", "k_ready", "sq_ready", "ss_ready", "root_ready", "clipped", "kn_ready", "summed", "gram_act",
                 "gram_dve", "state_ready", "state_copied", "q_copied", "y_ready", "y_copied"))
            ctx_in = (ctx_even, ctx_odd)

            is_first, is_last = (lambda n: is_at(n, 0)), (lambda n: is_at(n, B - 1))

            with nc.Block() as block:
                @block.sync
                def _(sp):
                    sp.dma_start(gain[:], a["ln1_g_row"].partition_broadcast(KC)).then_inc(const_in, 16)
                    sp.dma_start(shift[:], a["ln1_b_row"].partition_broadcast(KC)).then_inc(const_in, 16)

                    def load(n, j, half):
                        wait(sp, raw_ready, (n - 1) * CH)
                        sp.dma_start(ctx[:, j, :, :], a["ctx"][n].rearrange("(c p) d -> p c d", p=KC)).then_inc(ctx_in[j], 16)
                    sequences(sp, load)

                @block.gpsimd
                def _(pool):
                    pool.wait_ge(const_in, 32)

                    def body(n, j, half):
                        pool.wait_ge(raw_ready, (n + 1) * CH)
                        pool.tensor_tensor(cn[:, j, :, :], cn[:, j, :, :],
                                           gain[:].unsqueeze(1).broadcast_to((KC, CH, D)), ALU.mult).then_inc(scaled, 1)
                        pool.wait_ge(scaled, n + 1)
                        pool.tensor_tensor(cn[:, j, :, :], cn[:, j, :, :],
                                           shift[:].unsqueeze(1).broadcast_to((KC, CH, D)), ALU.add).then_inc(cn_ready, 1)
                        wait(pool, y_ready, n)
                        src = q_t[:, :, n * S:(n + 1) * S] if isinstance(n, int) else q_t[:, :, bass.ds(n * S, S)]
                        pool.tensor_copy(q_now[:], src).then_inc(q_copied, 1)
                    sequences(pool, body)

                @block.tensor
                def _(pe):
                    def turn(n, j, c):
                        i = n * CH + c
                        if c == 0:
                            pe.wait_ge(cn_ready, n + 1)
                        wait(pe, c_copied, i)
                        pe.transpose(pt[:, 0:KC], cn[:, j, c, :], g.ident[0:KC, 0:KC]).then_inc(c_turned, 1)

                    def keys(n, c):
                        i = n * CH + c
                        pe.wait_ge(c_copied, i + 1)
                        wait(pe, kn_ready, i - 1)
                        for b in range(2):
                            last = pe.matmul(pk[c % 2][0:KC, b, :], cn_t[:, c % 2, :], wk[:, b * HW:(b + 1) * HW],
                                             start=True, stop=True)
                        last.then_inc(k_ready, 1)

                    def add(n, j, c):
                        pe.wait_ge(kn_ready, n * CH + c + 1)
                        if c == 0:
                            wait(pe, gram_act, n)
                            wait(pe, gram_dve, n)
                        for b in range(2):
                            last = pe.matmul(pg[:, b, :], cn[:, j, c, :], kn[:, c % 2, b * HW:(b + 1) * HW],
                                             start=(c == 0), stop=(c == CH - 1))
                        last.then_inc(summed, 1)

                    def states(n, half):
                        pe.wait_ge(gram_act if half == 0 else gram_dve, n + 1)
                        if half == 0:
                            wait(pe, y_copied, n)
                        else:
                            pe.wait_ge(state_copied, 2 * n + 1)
                        for h in range(8 * half, 8 * half + 8):
                            rows = slice(DH2 * (h % 2), DH2 * (h % 2) + DH2)
                            last = pe.matmul(pz[rows, (h % 8 // 2) * D:(h % 8 // 2 + 1) * D],
                                             gram[:, h * DH2:(h + 1) * DH2], w_vo[:, h, :], start=True, stop=True)
                        last.then_inc(state_ready, 1)

                    def out(n):
                        pe.wait_ge(state_copied, 2 * n + 2)
                        pe.wait_ge(q_copied, n + 1)
                        for p in range(HP):
                            last = pe.matmul(pz[:, 0:S], state[:, p, :], q_now[:, p, :], start=(p == 0), stop=(p == HP - 1))
                        last.then_inc(y_ready, 1)

                    pe.wait_ge(const_in, 32)
                    turn(0, 0, 0)

                    def body(n, j, half):
                        for c in range(CH):
                            keys(n, c)
                            if c < CH - 1:
                                turn(n, j, c + 1)
                            elif not is_last(n):
                                turn(n + 1, 1 - j, 0)
                            if c >= 2:
                                add(n, j, c - 2)
                            elif not is_first(n):
                                add(n - 1, 1 - j, CH - 2 + c)
                            if not is_first(n):
                                if c in (3, 5):
                                    states(n - 1, (c - 3) // 2)
                                if c == 7:
                                    out(n - 1)
                    sequences(pe, body)
                    add(B - 1, 1, CH - 2)
                    add(B - 1, 1, CH - 1)
                    states(B - 1, 0)
                    states(B - 1, 1)
                    out(B - 1)

                @block.scalar
                def _(act):
                    def root(n):
                        act.wait_ge(var_ready, n + 1)
                        act.activation(var[:], var[:], ACT.Sqrt).then_inc(root_ctx, 1)

                    def turned(n, c):
                        i = n * CH + c
                        act.wait_ge(c_turned, i + 1)
                        wait(act, k_ready, i - 1)
                        act.activation(cn_t[:, c % 2, :], pt[:, 0:KC], ACT.Copy).then_inc(c_copied, 1)

                    def tail(n, c):
                        if c == 1:
                            act.wait_ge(summed, (n + 1) * CH)
                            wait(act, state_ready, 2 * n)
                            act.activation(gram[:, 0:HW], pg[:, 0, :], ACT.Copy).then_inc(gram_act, 1)
                        if c in (3, 5):
                            hf = (c - 3) // 2
                            act.wait_ge(state_ready, 2 * n + hf + 1)
                            wait(act, y_ready, n)
                            act.activation(state[:, 4 * hf:4 * hf + 4, :].rearrange("p a d -> p (a d)"), pz[:],
                                           ACT.Copy).then_inc(state_copied, 1)
                        if c == 7:
                            act.wait_ge(y_ready, n + 1)
                            dst = g.y_t[:, n * S:(n + 1) * S] if isinstance(n, int) else g.y_t[:, bass.ds(n * S, S)]
                            act.activation(dst, pz[:, 0:S], ACT.Identity, bias=bo[:]).then_inc(y_copied, 1)

                    root(0)
                    turned(0, 0)

                    def body(n, j, half):
                        for c in range(CH):
                            i = n * CH + c
                            act.wait_ge(k_ready, i + 1)
                            wait(act, ss_ready, i - 1)
                            act.activation(sq[:, c % 2, :].rearrange("p (a b) -> p a b", a=2), pk[c % 2][0:KC, :, :],
                                           ACT.Square).then_inc(sq_ready, 1)
                            if c < CH - 1:
                                turned(n, c + 1)
                            act.wait_ge(ss_ready, i + 1)
                            act.activation(ss[:, c % 2, :], ss[:, c % 2, :], ACT.Sqrt).then_inc(root_ready, 1)
                            if c == 4 and not is_last(n):
                                root(n + 1)
                            if c == CH - 1 and not is_last(n):
                                turned(n + 1, 0)
                            if not is_first(n):
                                tail(n - 1, c)
                    sequences(act, body)
                    for c in (1, 3, 5, 7):
                        tail(B - 1, c)

                @block.vector
                def _(dve):
                    def stat(n, j, half):
                        dve.wait_ge(ctx_in[j], half * 16 + 16)
                        wait(dve, raw_ready, n * CH)
                        for c in range(CH):
                            last = dve.bn_stats(stats[:, c, :], ctx[:, j, c, :])
                        last.then_inc(steps, 1)
                        dve.wait_ge(steps, n * 3 + 1)
                        dve.sem_inc(held, 1)
                        for c in range(CH):
                            last = dve.bn_aggr(mv[:, c, :], stats[:, c, :])
                        last.then_inc(steps, 1)
                        dve.wait_ge(steps, n * 3 + 2)
                        dve.tensor_scalar(var[:], mv[:, :, 1], EPS, None, ALU.add).then_inc(var_ready, 1)

                    def normed(n, j, half):
                        dve.wait_ge(root_ctx, n + 1)
                        dve.reciprocal(rs[:], var[:]).then_inc(steps, 1)
                        dve.wait_ge(steps, n * 3 + 3)
                        wait(dve, summed, (n - 1) * CH)
                        for c in range(CH):
                            dve.tensor_scalar(cn[:, j, c, :], ctx[:, j, c, :], mv[:, c, 0:1], rs[:, c:c + 1],
                                              ALU.subtract, ALU.mult).then_inc(raw_ready, 1)

                    stat(0, 0, 0)
                    normed(0, 0, 0)

                    def body(n, j, half):
                        nj, nhalf = 1 - j, (half if j == 0 else half + 1)
                        for c in range(CH):
                            i = n * CH + c
                            dve.wait_ge(sq_ready, i + 1)
                            wait(dve, kn_ready, i - 1)
                            dve.tensor_reduce(ss[:, c % 2, :], sq[:, c % 2, :].rearrange("p (h d) -> p h d", h=H2),
                                              AX.X, ALU.add).then_inc(ss_ready, 1)
                            if c == 3 and not is_last(n):
                                stat(n + 1, nj, nhalf)
                            if c == 5 and not is_last(n):
                                normed(n + 1, nj, nhalf)
                            dve.wait_ge(root_ready, i + 1)
                            dve.tensor_scalar(rn[:, c % 2, :], ss[:, c % 2, :], 1e-12, None, ALU.max).then_inc(clipped, 1)
                            dve.wait_ge(clipped, 2 * i + 1)
                            dve.reciprocal(rn[:, c % 2, :], rn[:, c % 2, :]).then_inc(clipped, 1)
                            dve.wait_ge(clipped, 2 * i + 2)
                            wait(dve, summed, i - 1)
                            dve.tensor_tensor(kn[:, c % 2, :].rearrange("p (h d) -> p h d", h=H2),
                                              pk[c % 2][0:KC, :, :].rearrange("p a (h d) -> p (a h) d", h=8),
                                              rn[:, c % 2, :].unsqueeze(2).broadcast_to((KC, H2, DH2)),
                                              ALU.mult).then_inc(kn_ready, 1)
                            if c == 1 and not is_first(n):
                                last_half(n - 1)

                    def last_half(n):
                        dve.wait_ge(summed, (n + 1) * CH)
                        wait(dve, state_ready, 2 * n)
                        dve.tensor_copy(gram[:, HW:INNER], pg[:, 1, :]).then_inc(gram_dve, 1)

                    sequences(dve, body)
                    last_half(B - 1)

    r = scope(nc, "attn2m")
    with r.ctx:
        g2, s2 = r.sb("g2", [D, 1]), r.sb("s2", [D, 1])
        w1, w2 = r.sb("w1", [D, 4, 128]), r.sb("w2", [128, 4, D])
        b1, b2 = r.sb("b1", [128, 4]), r.sb("b2", [D, 1])
        loaded, added = r.sem("loaded"), r.sem("added")
        with nc.Block() as block:
            @block.sync
            def _(sp):
                for dst, src in ((g2[:], a["ln2_g"]), (s2[:], a["ln2_b"]), (w1[:], a["w1_2"].rearrange("i (k f) -> i k f", k=4)),
                                 (w2[:], a["w2_2"].rearrange("(k f) o -> f k o", f=128)), (b1[:], a["b1_2"]), (b2[:], a["b2_2"])):
                    sp.dma_start(dst, src).then_inc(loaded, 16)
                sp.wait_ge(loaded, 96)

            @block.vector
            def _(dve):
                dve.tensor_tensor(g.y_t[:], g.y_t[:], g.xn_t[:], ALU.add).then_inc(added, 1)
                dve.wait_ge(added, 1)
        norm(nc, g, "norm4m", only_y=(g2[:], s2[:]))

        def gelu(act, out, in_, k, i, raw_free, h_ready):
            return act.activation(out, in_, ACT.Gelu, bias=b1[:, k:k + 1])

        def put(dve, q, y):
            cols = g.y_t[:, q * QUAD:(q + 1) * QUAD]
            return dve.scalar_tensor_tensor(cols, y, b2[:], cols, ALU.add, ALU.add)

        with nc.Block() as block:
            hidden_layer(nc, r, block, g.z_t, lambda k: w1[:, k, :], lambda k: w2[:, k, :], 4, 128, gelu, put, r.ps)


CONSTS = ("c_ident", "c_head_of", "c_in_group", "c_head_rows", "c_eye2")


def constants():
    rows, f = np.arange(PAIR), np.arange(D)
    head_rows = np.zeros((PAIR, HP, D), np.float32)
    for p in range(HP):
        head_rows[:, p, :] = (2 * p + rows // S)[:, None] == (f // DH)[None, :]
    return {
        "c_order": np.arange(E, dtype=np.float32),
        "c_ident": np.eye(128, dtype=np.float32),
        "c_head_of": ((f // DH)[:, None] == np.arange(H)[None, :]).astype(np.float32),
        "c_in_group": ((f // DH % 4)[:, None] == np.arange(4)[None, :]).astype(np.float32),
        "c_head_rows": head_rows,
        "c_eye2": ((rows % S)[:, None] == np.arange(S)[None, :]).astype(np.float32),
    }


def layout(i):
    c = np.ascontiguousarray
    col = lambda name: c(i[name].reshape(-1, 1))
    out = {
        "x": c(i["x"].reshape(T, D)),
        "ctx": c(i["ctx_1024"]),
        "ctx_t": c(i["ctx_1024"].transpose(0, 2, 1)),
        "bias": c(i["fside_1x16xSxS2_0"].reshape(HP, PAIR, KEYS).transpose(1, 0, 2)),
        "mask0": c(i["mask_Bx1xSxS2_ik1"].reshape(B, S, KEYS)),
        "mask0_t": c(i["mask_Bx1xSxS2_ik1"].reshape(B, S, CH, KC).transpose(0, 3, 2, 1)),
        "mask3": c(i["mask_Bx1xSxS2_fk0"].reshape(B, S, KEYS)),
        "g_xattn": c(i["g_xattn"]), "g_ffn": c(i["g_ffn"]),
    }
    for n, names in ((0, ("W_q", "W_k", "W_v", "W_o")), (1, ("w_q", "w_k", "w_v", "w_o")),
                     (3, ("Wq", "Wk", "Wv", "Wo"))):
        for short, name in zip("qkvo", names):
            out[f"w{short}{n}"] = c(i[f"L{n}_xattn_{name}"].T)
    for n, pre in ((0, "b_"), (3, "b")):
        for short in "qko":
            out[f"b{short}{n}"] = col(f"L{n}_xattn_{pre}{short}")
        out[f"bv{n}"] = c(i[f"L{n}_xattn_{pre}v"])
    f = lambda name: c(i[name])
    out.update(w_fc=f("L0_ffn_w_fc"), w_proj=f("L0_ffn_w_proj"), v_t=c(i["L0_ffn_v"].T),
               fast_b_t=c(i["L0_ffn_fast_b"].T), u_t=c(i["L0_ffn_u"].T), gate0=c(i["L0_ffn_gate"].reshape(1)),
               router1=c(i["L1_ffn_gate_weight"].T), shared_up_t=c(i["L1_ffn_shared_gate_up"].T),
               shared_down_t=c(i["L1_ffn_shared_down"].T),
               experts_up_t=c(i["L1_ffn_experts_gate_up"].transpose(0, 2, 1)),
               experts_down_t=c(i["L1_ffn_experts_down"].transpose(0, 2, 1)),
               router2=c(i["L2_ffn_router_w"].T), router2_b=f("L2_ffn_router_b"),
               experts2=f("L2_ffn_expert_weights"),
               router3=f("L3_ffn_router_w"), router3_b=f("L3_ffn_router_b"),
               experts3=f("L3_ffn_expert_w"), experts3_b=f("L3_ffn_expert_b"),
               wq2=f("L2_xattn_wq"), wk2=f("L2_xattn_wk"), wv2_t=c(i["L2_xattn_wv"].T), wo2=f("L2_xattn_wo"),
               bo2=col("L2_xattn_bo"), w1_2=f("L2_xattn_w1"), w2_2=f("L2_xattn_w2"),
               b1_2=c(i["L2_xattn_b1"].reshape(4, 128).T), b2_2=col("L2_xattn_b2"),
               ln1_g=col("L2_xattn_ln1_g"), ln1_b=col("L2_xattn_ln1_b"), ln1_g_row=f("L2_xattn_ln1_g"),
               ln1_b_row=f("L2_xattn_ln1_b"), ln2_g=col("L2_xattn_ln2_g"), ln2_b=col("L2_xattn_ln2_b"))
    out.update(constants())
    return out


def loads(nc, name, pairs):
    r = scope(nc, name)
    with r.ctx:
        loaded = r.sem("loaded")
        with nc.Block() as block:
            @block.sync
            def _(sp):
                for dst, src in pairs:
                    sp.dma_start(dst[:], src).then_inc(loaded, 16)
                sp.wait_ge(loaded, 16 * len(pairs))


def program(nc, a, only=None):
    with ExitStack() as ctx:
        g = Names()
        sb = lambda n, shape: ctx.enter_context(nc.sbuf_tensor(n, shape, F32))
        g.x, g.ident, g.gates = sb("x_sb", [PAIR, TILES, D]), sb("ident", [128, 128]), sb("gates", [PAIR, 8])
        g.xn_t, g.y_t = sb("xn_t", [D, T]), sb("y_t", [D, T])
        parts = [
            lambda: attention(nc, g, "attn0", a, dict(
                wq=a["wq0"], wk=a["wk0"], wv=a["wv0"], wo=a["wo0"], bq=a["bq0"], bk=a["bk0"], bv=a["bv0"], bo=a["bo0"],
                mask=a["mask0"], mask_t=a["mask0_t"]), "select"),
            lambda: ffn0(nc, g, a),
            lambda: attention(nc, g, "attn1", a, dict(
                wq=a["wq1"], wk=a["wk1"], wv=a["wv1"], wo=a["wo1"], bq=None), "plain"),
            lambda: ffn1(nc, g, a),
            lambda: attention2(nc, g, a),
            lambda: ffn2(nc, g, a),
            lambda: attention(nc, g, "attn3", a, dict(
                wq=a["wq3"], wk=a["wk3"], wv=a["wv3"], wo=a["wo3"], bq=a["bq3"], bk=a["bk3"], bv=a["bv3"], bo=a["bo3"],
                mask=a["mask3"]), "add"),
            lambda: ffn3(nc, g, a),
        ]
        setup(nc, g, a)
        gate = None
        for n, part in enumerate(parts):
            if only is not None and n != only:
                continue
            if n == 4:
                with ExitStack() as own:
                    g.z_t = own.enter_context(nc.sbuf_tensor("z_t", [D, T], F32))
                    twice = [own.enter_context(nc.sbuf_tensor(m, [D, 1], F32)) for m in ("ln1_gain", "ln1_shift")]
                    loads(nc, "ln1", ((twice[0], a["ln1_g"]), (twice[1], a["ln1_b"])))
                    norm(nc, g, f"norm{n}", gate=gate, twice=(twice[0][:], twice[1][:]))
                    part()
            else:
                norm(nc, g, f"norm{n}", gate=gate)
                part()
            gate = n // 2 + 4 * (n % 2)
        norm(nc, g, "last", gate=gate, out=a["out"])


def kernel(**inputs):
    import concourse.bacc as bacc
    from concourse.bass_utils import run_bass_kernel_spmd

    nc = bacc.Bacc("TRN2", target_bir_lowering=False, num_devices=1)
    arrays, aps = {}, {}
    for name, value in layout({k: np.asarray(v) for k, v in inputs.items()}).items():
        arrays[f"in_{name}"] = value
        aps[name] = nc.dram_tensor(f"in_{name}", value.shape, mybir.dt.from_np(value.dtype), kind="ExternalInput").ap()
    aps["out"] = nc.dram_tensor("out", (T, D), F32, kind="ExternalOutput").ap()
    program(nc, aps)
    got = run_bass_kernel_spmd(nc, [arrays], core_ids=[0])
    return got.results[0]["out"].reshape(B, S, D)
```

```python
import math
from contextlib import ExitStack

import numpy as np
import concourse.bass as bass
from concourse import mybir

F32 = mybir.dt.float32
I32 = mybir.dt.int32
BF16 = mybir.dt.bfloat16
ALU = mybir.AluOpType
ACT = mybir.ActivationFunctionType
AX = mybir.AxisListType

B, S, KEYS, D = 32, 56, 1500, 128
T = B * S
PAIR = 2 * S
TILES = T // PAIR
QUAD = 4 * PAIR
NQ = T // QUAD
H, DH = 16, 8
HP = H // 2
CH, KC = 12, 125
THIRD = KEYS // 3
BIG = 2.0 ** 100
LOW = -3.0e38
FLT_MAX = float(np.finfo(np.float32).max)
MASKED = -10000.0
EPS = 1e-5
E = 8
F1, F1C, F1K = 938, 118, 8
H2, DH2 = 16, 64


STEPS = (0, 1, "k", "pv", 2, 3, 4, 5, "v", 6, 7)
TURNED = {2: (-2, -1, None, None, 0, 1, 2, 3, 4, 5, None),
          4: (-2, -1, None, None, None, 0, 1, 2, 3, 4, 5)}


def bank(step, parity):
    return (STEPS.index(step) + parity) % 2


K_PART = (0, 0, 0, 1, 1, 2)
Q_PART = (0, 1, 2, 0, 1, 0)
PACKED = 16 * len(K_PART)


class Names:
    pass


def wait(eng, sem, count):
    if isinstance(count, int) and count <= 0:
        return
    eng.wait_ge(sem, count)


def sequences(eng, body):
    for n in (0, 1):
        body(n, n, 0)
    with eng.Fori(1, B // 2 - 1) as half:
        for j in (0, 1):
            body(half * 2 + j, j, half)
    for n in (B - 2, B - 1):
        body(n, n % 2, n // 2)


def is_at(n, where):
    return isinstance(n, int) and n == where


class Chain:

    def __init__(self, eng, sem):
        self.eng, self.sem, self.n = eng, sem, 0

    def __call__(self, ins):
        self.n += 1
        ins.then_inc(self.sem, 1)
        self.eng.wait_ge(self.sem, self.n)


def scope(nc, name):
    ctx = ExitStack()
    r = Names()
    r.ctx = ctx
    r.sb = lambda n, shape, dt=F32: ctx.enter_context(nc.sbuf_tensor(f"{name}_{n}", shape, dt))
    r.ps = lambda n, shape: ctx.enter_context(nc.psum_tensor(f"{name}_{n}", shape, F32))
    sems = []

    def sem(n):
        sems.append(nc.alloc_semaphore(f"{name}_{n}"))
        return sems[-1]

    def clear():
        nc.clear_and_free_semaphores(sems)
        nc.all_engine_barrier()

    r.sem = sem
    ctx.callback(clear)
    return r


def setup(nc, g, a):
    r = scope(nc, "setup")
    with r.ctx:
        loaded, tanhs = r.sem("loaded"), r.sem("tanhs")
        with nc.Block() as block:
            @block.sync
            def _(sp):
                sp.dma_start(g.x[:], a["x"].rearrange("(t p) d -> p t d", p=PAIR)).then_inc(loaded, 16)
                sp.dma_start(g.ident[:], a["c_ident"]).then_inc(loaded, 16)
                sp.dma_start(g.gates[:, 0:4], a["g_xattn"].partition_broadcast(PAIR)).then_inc(loaded, 16)
                sp.dma_start(g.gates[:, 4:8], a["g_ffn"].partition_broadcast(PAIR)).then_inc(loaded, 16)
                sp.wait_ge(loaded, 64)

            @block.scalar
            def _(act):
                act.wait_ge(loaded, 64)
                act.activation(g.gates[:], g.gates[:], ACT.Tanh).then_inc(tanhs, 1)
                act.wait_ge(tanhs, 1)


def norm(nc, g, name, gate=None, out=None, twice=None, only_y=None):
    r = scope(nc, name)
    with r.ctx:
        x = r.sb("y_rows", [PAIR, TILES, D]) if only_y else g.x
        stats = r.sb("stats", [PAIR, TILES, 6])
        mv = r.sb("mv", [PAIR, TILES, 2])
        sd = r.sb("sd", [PAIR, TILES])
        rs = r.sb("rs", [PAIR, TILES])
        xn = r.sb("xn", [PAIR, TILES, D])
        py = r.ps("py", [128, NQ, 512])
        px = r.ps("px", [128, NQ, 512])
        y_turned, x_ready, steps, var_ready, sd_ready, xn_ready, xn_turned, copied, stored = (
            r.sem(n) for n in ("y_turned", "x_ready", "steps", "var_ready", "sd_ready", "xn_ready",
                               "xn_turned", "copied", "stored"))
        rounds = 2 if twice else 1
        with nc.Block() as block:
            @block.tensor
            def _(pe):
                if gate is not None or only_y:
                    for t in range(TILES):
                        last = pe.transpose(py[0:PAIR, t // 4, (t % 4) * D:(t % 4 + 1) * D],
                                            g.y_t[:, t * PAIR:(t + 1) * PAIR], g.ident[:])
                        if t % 4 == 3:
                            last.then_inc(y_turned, 1)
                if out is not None:
                    return
                for rd in range(rounds):
                    for t in range(TILES):
                        pe.wait_ge(xn_ready, rd * TILES + t + 1)
                        if rd and t % 4 == 0:
                            pe.wait_ge(copied, t // 4 + 1)
                        last = pe.transpose(px[:, t // 4, (t % 4) * PAIR:(t % 4 + 1) * PAIR],
                                            xn[:, t, :], g.ident[0:PAIR, 0:PAIR])
                        if t % 4 == 3:
                            last.then_inc(xn_turned, 1)

            @block.vector
            def _(dve):
                if gate is not None or only_y:
                    for q in range(NQ):
                        dve.wait_ge(y_turned, q + 1)
                        xq = x[:, 4 * q:4 * q + 4, :].rearrange("p t d -> p (t d)")
                        if only_y:
                            dve.tensor_copy(xq, py[0:PAIR, q, :]).then_inc(x_ready, 1)
                            continue
                        dve.scalar_tensor_tensor(xq, py[0:PAIR, q, :], g.gates[:, gate:gate + 1], xq,
                                                 ALU.mult, ALU.add).then_inc(x_ready, 1)
                if out is not None:
                    return
                chain = Chain(dve, steps)
                for rd in range(rounds):
                    src = x if rd == 0 else xn
                    if rd:
                        dve.wait_ge(xn_turned, NQ)
                        dve.wait_ge(xn_ready, TILES)
                    for t in range(TILES):
                        if (gate is not None or only_y) and t % 4 == 0 and rd == 0:
                            dve.wait_ge(x_ready, t // 4 + 1)
                        last = dve.bn_stats(stats[:, t, :], src[:, t, :])
                    chain(last)
                    for t in range(TILES):
                        last = dve.bn_aggr(mv[:, t, :], stats[:, t, :])
                    chain(last)
                    dve.tensor_scalar(sd[:], mv[:, :, 1], EPS, None, ALU.add).then_inc(var_ready, 1)
                    dve.wait_ge(sd_ready, rd + 1)
                    chain(dve.reciprocal(rs[:], sd[:]))
                    for t in range(TILES):
                        dve.tensor_scalar(xn[:, t, :], src[:, t, :], mv[:, t, 0:1], rs[:, t:t + 1],
                                          ALU.subtract, ALU.mult).then_inc(xn_ready, 1)

            @block.scalar
            def _(act):
                if out is not None:
                    return
                for rd in range(rounds):
                    act.wait_ge(var_ready, rd + 1)
                    act.activation(sd[:], sd[:], ACT.Sqrt).then_inc(sd_ready, 1)
                    for q in range(NQ):
                        act.wait_ge(xn_turned, rd * NQ + q + 1)
                        cols = slice(q * QUAD, (q + 1) * QUAD)
                        affine = only_y or (rd and twice)
                        if not affine:
                            act.activation(g.xn_t[:, cols], px[:, q, 0:QUAD], ACT.Copy).then_inc(copied, 1)
                        else:
                            act.activation(g.z_t[:, cols], px[:, q, 0:QUAD], ACT.Identity,
                                           bias=affine[1], scale=affine[0]).then_inc(copied, 1)

            @block.sync
            def _(sp):
                if out is not None:
                    sp.wait_ge(x_ready, NQ)
                    sp.dma_start(out.rearrange("(t p) d -> p t d", p=PAIR), g.x[:]).then_inc(stored, 16)
                    sp.wait_ge(stored, 16)


def attention(nc, g, name, a, w, mode):
    r = scope(nc, name)
    select, plain, add = mode == "select", mode == "plain", mode == "add"
    with r.ctx:
        wq, wk, wv, wo = (r.sb(n, [D, D]) for n in ("wq", "wk", "wv", "wo"))
        bq, bk, bo = (r.sb(n, [D, 1]) for n in ("bq", "bk", "bo"))
        bv = r.sb("bv", [128, D])
        q_t = g.y_t
        packed = not select
        if packed:
            q_blocks = r.sb("q_blocks", [PACKED, 2, H, S], BF16)
            q_packed = r.sb("q_packed", [PACKED, HP, T], BF16)
            parts = r.sb("parts", [D, 3, T], BF16)
            k_parts = parts[:, :, 0:KEYS]
            k_whole = g.xn_t[:, 0:KEYS]
            k_packed = r.sb("k_packed", [PACKED, 2, HP, KEYS], BF16)
            row_head = r.sb("row_head", [PACKED, 2])
            (x_away, q_split, q_stored, q_in, whole_ready, k_split, k_stored, k_in_even, k_in_odd) = (r.sem(n) for n in (
                "x_away", "q_split", "q_stored", "q_in", "whole_ready", "k_split", "k_stored", "k_in_even", "k_in_odd"))
            k_in = (k_in_even, k_in_odd)
        else:
            q_blocks = r.sb("q_blocks", [D, 2, H, S])
            head_of = r.sb("head_of", [D, H])
            k_t = r.sb("k_t", [D, 2, KEYS])
        in_group = r.sb("in_group", [D, 4])
        head_rows = r.sb("head_rows", [PAIR, 2 * D - 16])
        eye2 = r.sb("eye2", [PAIR, S])
        ctx_t = r.sb("ctx_t", [D, KEYS])
        v = r.sb("v", [KC, 2, CH, D])
        probs = [r.sb(f"probs{i}", [PAIR, KEYS])[:] for i in range(2 if select else 3)]
        if not select:
            probs.append(g.x[:].rearrange("p t d -> p (t d)")[:, 0:KEYS])
        NB = len(probs)
        turned_in = TURNED[NB]
        left = [HP + p for p in turned_in if p is not None and p < 0]
        probs_t = r.sb("probs_t", [KC, CH, H * S])
        top = r.sb("top", [PAIR, HP])
        neg_top = r.sb("neg_top", [PAIR, 2, HP])
        sums = r.sb("sums", [PAIR, 2, HP])
        inv = r.sb("inv", [PAIR, HP])
        NR = 2 if select else 1
        spread = r.sb("spread", [PAIR, HP, NR, S])
        diag = r.sb("diag", [D, 4, S])
        mixed = r.sb("mixed", [D, S])
        scores = [r.ps(f"scores{i}", [128, 3, 512]) for i in range(2)]
        pt = [r.ps(f"pt{i}", [128, 512]) for i in range(2)]
        shift = r.sb("shift", [PAIR, 2, KEYS])
        if select:
            mask = r.sb("mask", [PAIR, 1, KEYS], I32)
            out_t = r.sb("out_t", [KC, 2, CH, S])
            push = r.sb("push", [PAIR, KEYS])
            bias = r.sb("bias", [PAIR, HP, KEYS])
            counted = r.sb("counted", [PAIR, 2])
            floor = r.sb("floor", [PAIR, 1])
            tenk = r.sb("tenk", [PAIR, 1])
            odd = r.sb("odd", [128, CH * D], I32)
            stand_ins = r.sb("stand_ins", [128, 2, 3])
            share = r.sb("share", [PAIR, HP])
            share_den = r.sb("share_den", [PAIR, HP])
            out_sum = r.sb("out_sum", [D, S])
            out_part = r.sb("out_part", [D, S])

        (const_in, steps, psteps, q_turned, q_ready, blocks_ready, ctx_in, scores_ready, k_turned, k_ready,
         v_turned, v_ready, top_ready, probs_ready, logits_ready, pt_ready, act_copied, dve_copied,
         spread_ready, pv_ready, attn_ready, y_turned, mask_in, mask_t_in, shift_ready, push_ready,
         out_t_ready, counted_ready, guarded, raw_top, inv_steps, share_ready, clean_steps, mask_t_in1, mask_in1, bias_in, held) = (
            r.sem(n) for n in (
                "const_in", "steps", "psteps", "q_turned", "q_ready", "blocks_ready", "ctx_in", "scores_ready",
                "k_turned", "k_ready", "v_turned", "v_ready", "top_ready", "probs_ready", "logits_ready",
                "pt_ready", "act_copied", "dve_copied", "spread_ready", "pv_ready", "attn_ready",
                "y_turned", "mask_in", "mask_t_in", "shift_ready", "push_ready", "out_t_ready",
                "counted_ready", "guarded", "raw_top", "inv_steps", "share_ready", "clean_steps", "mask_t_in1", "mask_in1", "bias_in", "held"))
        mask_t_in = (mask_t_in, mask_t_in1)
        mask_in = (mask_in, mask_in1)
        by_act = (0, 1, 2) if select else (0, 2)
        scale = 1.0 / math.sqrt(DH)

        def hold(eng):
            eng.sem_inc(held, 1)

        GUARD = 6
        GUARD_Q = 2 * GUARD
        GUARD_END = GUARD_Q + B * 2 * GUARD

        consts = [(wq, w["wq"]), (wk, w["wk"]), (wv, w["wv"]), (wo, w["wo"]),
                  (in_group, a["c_in_group"]), (head_rows, a["c_head_rows"]), (eye2, a["c_eye2"])]
        if w["bq"] is not None:
            consts += [(bq, w["bq"]), (bk, w["bk"]), (bo, w["bo"]), (bv, w["bv"].partition_broadcast(128))]
        consts += [(row_head, a["c_row_head"])] if packed else [(head_of, a["c_head_of"])]
        nconst = 16 * len(consts)

        with nc.Block() as block:
            @block.sync
            def _(sp):
                for dst, src in consts:
                    sp.dma_start(dst[:], src).then_inc(const_in, 16)

                def pack(parts, scratch, rows_of, part_of, stored, done, came):
                    sp.dma_start(scratch.rearrange("a f k -> f a k"), parts).then_inc(stored, 16)
                    sp.wait_ge(stored, done)
                    for i, part in enumerate(part_of):
                        sp.dma_start(rows_of(i), scratch[part].rearrange("(p r) k -> r p k", r=16)).then_inc(came, 16)

                def pack_queries():
                    sp.wait_ge(q_split, 4)
                    pack(parts[:], a["q_scratch"], lambda i: q_packed[16 * i:16 * i + 16, :, :], Q_PART,
                         q_stored, 16, q_in)

                def pack_keys(n, j, half):
                    sp.wait_ge(k_split, n * 3 + 3)
                    hold(sp)
                    wait(sp, scores_ready, (n - 1) * HP)
                    if not is_at(n, 0) and not is_at(n, 1):
                        sp.wait_ge(k_in[j], half * len(K_PART) * 16)
                    hold(sp)
                    pack(k_parts, a["k_scratch"][j], lambda i: k_packed[16 * i:16 * i + 16, j, :, :], K_PART,
                         k_stored, n * 16 + 16, k_in[j])

                if packed:
                    sp.dma_start(a["x_scratch"], g.x[:]).then_inc(x_away, 16)

                def loads(n, j, half):
                    wait(sp, v_turned, n)
                    sp.dma_start(ctx_t[:], a["ctx_t"][n]).then_inc(ctx_in, 16)
                    if add:
                        wait(sp, logits_ready, (n - 1) * HP)
                        for i in range(2):
                            sp.dma_start(shift[i * S:(i + 1) * S, j, :], w["mask"][n]).then_inc(mask_in[j], 16)
                    if select:
                        wait(sp, push_ready, n)
                        wait(sp, counted_ready, n)
                        for i in range(2):
                            sp.dma_start(mask[i * S:(i + 1) * S, 0, :], w["mask"][n]).then_inc(mask_in[0], 16)
                    if select:
                        wait(sp, pv_ready, n - 1)
                        sp.dma_start(out_t[:, j, :, :].bitcast(I32), w["mask_t"][n]).then_inc(mask_t_in[j], 16)
                        if is_at(n, 0):
                            sp.dma_start(bias[:], a["bias"]).then_inc(bias_in, 16)
                    if packed:
                        if is_at(n, 0):
                            pack_queries()
                        pack_keys(n, j, half)

                sequences(sp, loads)
                if packed:
                    sp.wait_ge(pt_ready, B * HP * 3)
                    sp.dma_start(g.x[:], a["x_scratch"]).then_inc(x_away, 16)
                    sp.wait_ge(x_away, 32)

            @block.gpsimd
            def _(pool):
                chain = Chain(pool, psteps)
                if w["bq"] is None:
                    for t in (bq, bk, bo, bv):
                        pool.memset(t[:], 0.0)
                    chain(pool.memset(shift[:, 0, :], 0.0))
                if select:
                    for i, value in enumerate((0.0, -MASKED, MASKED)):
                        pool.memset(stand_ins[:, 0, i:i + 1], value)
                        pool.memset(stand_ins[:, 1, i:i + 1], value * scale)
                    chain(pool.memset(tenk[:], MASKED))
                pool.wait_ge(const_in, nconst)

                def prepare(n, j, half):
                    if add:
                        pool.wait_ge(mask_in[j], half * 32 + 32)
                        hold(pool)
                        pool.tensor_scalar(shift[:, j, :], shift[:, j, :], -1000000.0, None,
                                           ALU.mult).then_inc(push_ready, 1)
                    if select:
                        pool.wait_ge(guarded, GUARD_Q)
                    else:
                        pool.wait_ge(q_in, len(Q_PART) * 16)
                    wait(pool, scores_ready, (n - 1) * HP)
                    cols = slice(n * S, (n + 1) * S) if isinstance(n, int) else bass.ds(n * S, S)
                    if packed:
                        pool.tensor_tensor(q_blocks[:, j, :, :].rearrange("p (a b) s -> p a b s", b=2),
                                           q_packed[:, :, cols].unsqueeze(2).broadcast_to((PACKED, HP, 2, S)),
                                           row_head[:].unsqueeze(1).unsqueeze(3).broadcast_to((PACKED, HP, 2, S)),
                                           ALU.mult).then_inc(blocks_ready, 1)
                    else:
                        pool.tensor_tensor(q_blocks[:, j, :, :],
                                           q_t[:, cols].unsqueeze(1).broadcast_to((D, H, S)),
                                           head_of[:].unsqueeze(2).broadcast_to((D, H, S)),
                                           ALU.mult).then_inc(blocks_ready, 1)
                    if select:
                        pool.wait_ge(mask_t_in[j], half * 16 + 16)
                        hold(pool)
                        pool.tensor_scalar(out_t[:, j, :, :], out_t[:, j, :, :].bitcast(I32), 0.0, None,
                                           ALU.is_equal).then_inc(out_t_ready, 1)
                        for p in range(HP):
                            if p == 0:
                                pool.wait_ge(push_ready, n + 1)
                                wait(pool, clean_steps, 1 + 3 * HP)
                            wait(pool, logits_ready, n * HP + p - 1)
                            pool.tensor_tensor(shift[:, p % 2, :], bias[:, p, :], push[:],
                                               ALU.add).then_inc(shift_ready, 1)

                sequences(pool, prepare)

            @block.tensor
            def _(pe):
                pe.wait_ge(const_in, nconst)
                for q in range(NQ):
                    pe.matmul(scores[q // 3][:, q % 3, 0:QUAD], wq[:], g.xn_t[:, q * QUAD:(q + 1) * QUAD],
                              start=True, stop=True).then_inc(q_turned, 1)
                pe.wait_ge(q_ready, NQ)

                def k_proj(slot, c):
                    last = pe.matmul(scores[slot][:, c, 0:THIRD], wk[:],
                                     ctx_t[:, c * THIRD:(c + 1) * THIRD], start=True, stop=True)
                    if c == 2:
                        last.then_inc(k_turned, 1)

                def v_proj(slot, b):
                    for c in range(4 * b, 4 * b + 4):
                        last = pe.matmul(scores[slot][0:KC, b, (c % 4) * D:(c % 4 + 1) * D],
                                         ctx_t[:, c * KC:(c + 1) * KC], wv[:], start=True, stop=True)
                    if b == 2:
                        last.then_inc(v_turned, 1)

                def turn(n, p, t):
                    if t == 0:
                        pe.wait_ge(probs_ready, n * HP + p + 1)
                    pairs = n * HP + p
                    if select:
                        wait(pe, act_copied, pairs * 3 + t - 1)
                    elif t == 0:
                        wait(pe, dve_copied, pairs)
                    else:
                        wait(pe, act_copied, pairs * 2 + t - 1)
                    for c in range(4 * t, 4 * t + 4):
                        last = pe.transpose(pt[(p + t) % 2][0:KC, (c % 4) * PAIR:(c % 4 + 1) * PAIR],
                                            probs[p % NB][:, c * KC:(c + 1) * KC], g.ident[0:PAIR, 0:PAIR])
                    last.then_inc(pt_ready, 1)

                def values(m, j):
                    pe.wait_ge(act_copied, (m + 1) * HP * len(by_act))
                    if not select:
                        pe.wait_ge(dve_copied, (m + 1) * HP)
                    wait(pe, attn_ready, m)
                    if select:
                        pe.wait_ge(guarded, GUARD_END if is_at(m, B - 1) else GUARD_Q + (m * 2 + 3) * GUARD)
                    po = scores[bank("pv", 1 - j)][:, 0, :]
                    for c in range(CH):
                        for grp in range(4):
                            pe.matmul(po[32 * grp:32 * grp + 32, 0:4 * S], v[:, j, c, 32 * grp:32 * grp + 32],
                                      probs_t[:, c, grp * 4 * S:(grp + 1) * 4 * S],
                                      start=(c == 0), stop=(c == CH - 1))
                    pe.wait_ge(spread_ready, m + 1)
                    for p in range(HP):
                        last = pe.matmul(po[:, 4 * S:(4 + NR) * S], head_rows[:, D - 16 * (p + 1):2 * D - 16 * (p + 1)],
                                         spread[:, p, :, :].rearrange("p a s -> p (a s)"),
                                         start=(p == 0), stop=(p == HP - 1))
                    if select:
                        pe.wait_ge(out_t_ready, m + 1)
                        for c in range(CH):
                            last = pe.matmul(po[:, 6 * S:7 * S], v[:, j, c, :], out_t[:, j, c, :],
                                             start=(c == 0), stop=(c == CH - 1))
                    last.then_inc(pv_ready, 1)

                pe.wait_ge(ctx_in, 16)
                for c in range(3):
                    k_proj(bank("k", 1), c)
                pe.wait_ge(k_ready, 1)
                for c in range(3):
                    v_proj(bank("v", 1), c)

                def sequence(n, j, half):
                    first, final = is_at(n, 0), is_at(n, B - 1)

                    def used(step):
                        return not (first and step == "pv" or final and step in ("k", "v"))

                    def wait_for_bank(at):
                        at, m = at - 2, n
                        while at >= 0 and not used(STEPS[at]):
                            at -= 2
                        if at < 0:
                            at, m = at + len(STEPS), n - 1
                        last = STEPS[at]
                        if last == "pv":
                            wait(pe, attn_ready, m)
                        elif last in ("k", "v"):
                            wait(pe, k_ready if last == "k" else v_ready, m + 2)
                        else:
                            wait(pe, logits_ready, m * HP + last + 1)

                    for at, (step, turned) in enumerate(zip(STEPS, turned_in)):
                        if used(step):
                            wait_for_bank(at)
                        if step == "k" and not final:
                            pe.wait_ge(ctx_in, n * 16 + 32)
                        if step == "pv":
                            if not first:
                                values(n - 1, 1 - j)
                            continue
                        if step == 0:
                            pe.wait_ge(blocks_ready, n + 1)
                            if select:
                                pe.wait_ge(guarded, GUARD_Q + (GUARD if first else n * 2 * GUARD))
                            pe.wait_ge(k_ready, n + 1)
                            if packed:
                                pe.wait_ge(k_in[j], (half + 1) * len(K_PART) * 16)
                        if step == 1:
                            pe.wait_ge(v_ready, n + 1)
                        for c in range(3):
                            if step == "k":
                                if not final:
                                    k_proj(bank(step, j), c)
                            elif step == "v":
                                if not final:
                                    v_proj(bank(step, j), c)
                            else:
                                mm = pe.matmul(scores[bank(step, j)][0:PAIR, c, 0:THIRD],
                                               q_blocks[:, j, 2 * step:2 * step + 2, :].rearrange("p a s -> p (a s)"),
                                               (k_packed[:, j, step, c * THIRD:(c + 1) * THIRD] if packed else
                                                k_t[:, j, c * THIRD:(c + 1) * THIRD]), start=True, stop=True)
                                if c == 2:
                                    mm.then_inc(scores_ready, 1)
                            if turned is not None and turned >= 0:
                                turn(n, turned, c)
                            elif turned is not None and not first:
                                turn(n - 1, HP + turned, c)

                sequences(pe, sequence)
                for p in left:
                    for c in range(3):
                        turn(B - 1, p, c)
                pe.wait_ge(logits_ready, B * HP)
                values(B - 1, 1)
                pe.wait_ge(attn_ready, B)
                if select:
                    pe.wait_ge(guarded, GUARD_END + 4)
                for q in range(NQ):
                    pe.matmul(scores[q // 3][:, q % 3, 0:QUAD], wo[:], q_t[:, q * QUAD:(q + 1) * QUAD],
                              start=True, stop=True).then_inc(y_turned, 1)

            @block.scalar
            def _(act):
                act.wait_ge(const_in, nconst)
                if w["bq"] is None:
                    act.wait_ge(psteps, 1)
                for q in range(NQ):
                    act.wait_ge(q_turned, q + 1)
                    qs = q_t[:, q * QUAD:(q + 1) * QUAD]
                    act.activation(qs, scores[q // 3][:, q % 3, 0:QUAD], ACT.Identity,
                                   bias=bq[:]).then_inc(steps, 1)
                    act.wait_ge(steps, q + 1)
                    act.activation(qs, qs, ACT.Copy, scale=scale).then_inc(q_ready, 1)

                def k_copy(n, j):
                    act.wait_ge(k_turned, n + 1)
                    wait(act, scores_ready, (n - 1) * HP)
                    banks = scores[bank("k", 1 - j)][:, :, 0:THIRD]
                    if packed:
                        wait(act, k_split, n * 3)
                        wait(act, k_stored, n * 16)
                        if is_at(n, 0):
                            act.wait_ge(q_stored, 16)
                        act.activation(k_whole.rearrange("p (c k) -> p c k", c=3), banks,
                                       ACT.Identity, bias=bk[:]).then_inc(whole_ready, 1)
                        dst = k_parts[:, 0, :]
                    else:
                        dst = k_t[:, j, :]
                    act.activation(dst.rearrange("p (c k) -> p c k", c=3), banks,
                                   ACT.Identity, bias=bk[:]).then_inc(k_ready, 1)

                def copy(n, p, t):
                    act.wait_ge(pt_ready, (n * HP + p) * 3 + t + 1)
                    if p == 0:
                        wait(act, pv_ready, n)
                    act.activation(probs_t[:, 4 * t:4 * t + 4, p * PAIR:(p + 1) * PAIR],
                                   pt[(p + t) % 2][0:KC, 0:QUAD].rearrange("p (c q) -> p c q", c=4),
                                   ACT.Copy).then_inc(act_copied, 1)

                k_copy(0, 0)

                def exp(n, j, p):
                    act.wait_ge(top_ready, n * HP + p + 1)
                    act.activation(probs[p % NB], probs[p % NB], ACT.Exp, bias=neg_top[:, j, p:p + 1],
                                   accum_out=sums[:, j, p:p + 1]).then_inc(probs_ready, 1)

                def close(n, j):
                    exp(n, j, HP - 1)
                    if select:
                        wait(act, spread_ready, n)
                        act.activation(share[:], neg_top[:, j, :], ACT.Exp, bias=tenk[:]).then_inc(share_ready, 1)

                made = (-1, 0, 1, None, None, 2, 3, 4, 5, None, 6)

                def sequence(n, j, half):
                    first, final = is_at(n, 0), is_at(n, B - 1)
                    for step, turned, p in zip(STEPS, turned_in, made):
                        for t in by_act:
                            if turned is not None and turned >= 0:
                                copy(n, turned, t)
                            elif turned is not None and not first:
                                copy(n - 1, HP + turned, t)
                            if t > 0:
                                continue
                            if p == -1 and not first:
                                close(n - 1, 1 - j)
                            if step == "k" and not final:
                                k_copy(n + 1, 1 - j)
                            if p not in (-1, None):
                                exp(n, j, p)
                        if select and step == 7 and not final:
                            count(n + 1, 1 - j)

                def count(n, j):
                    act.wait_ge(push_ready, n + 1)
                    wait(act, spread_ready, n - 1)
                    act.activation(mask[:, 0, :].bitcast(F32), push[:], ACT.Copy, scale=-1.0 / BIG,
                                   accum_out=counted[:, j:j + 1]).then_inc(counted_ready, 1)

                if select:
                    act.wait_ge(psteps, 1)
                    count(0, 0)
                sequences(act, sequence)
                for p in left:
                    for t in by_act:
                        copy(B - 1, p, t)
                        if p == left[0] and t == 0:
                            close(B - 1, 1)
                for q in range(NQ):
                    act.wait_ge(y_turned, q + 1)
                    act.activation(g.y_t[:, q * QUAD:(q + 1) * QUAD], scores[q // 3][:, q % 3, 0:QUAD],
                                   ACT.Identity, bias=bo[:]).then_inc(steps, 1)

            @block.vector
            def _(dve):
                dve.wait_ge(const_in, nconst)
                if w["bq"] is None:
                    dve.wait_ge(psteps, 1)
                def guard(i, x, done, scaled=0):
                    rows, cols = x.shape
                    where = odd[0:rows, 0:cols]
                    wait(dve, guarded, done)
                    if i % 2:
                        hold(dve)
                        dve.copy_predicated(x, where, stand_ins[0:rows, scaled, i // 2:i // 2 + 1].broadcast_to(
                            (rows, cols))).then_inc(guarded, 1)
                    elif i == 0:
                        dve.tensor_tensor(where, x, x, ALU.not_equal).then_inc(guarded, 1)
                    else:
                        dve.tensor_scalar(where, x, FLT_MAX if i == 2 else -FLT_MAX, None,
                                          ALU.is_gt if i == 2 else ALU.is_lt).then_inc(guarded, 1)

                def guard_keys(n, j, steps):
                    done = GUARD_Q + (0 if is_at(n, 0) else (n * 2 - 1) * GUARD)
                    for i in steps:
                        dve.wait_ge(k_ready, n + 1)
                        guard(i, k_t[:, j, :], done + i)

                def guard_values(n, j, steps):
                    done = GUARD_END - GUARD if is_at(n, B - 1) else GUARD_Q + (n * 2 + 2) * GUARD
                    for i in steps:
                        dve.wait_ge(v_ready, n + 1)
                        guard(i, v[:, j, :, :].rearrange("p c d -> p (c d)"), done + i)

                if select:
                    dve.wait_ge(psteps, 1)
                    dve.wait_ge(q_ready, NQ)
                    for h in range(2):
                        for i in range(GUARD):
                            guard(i, q_t[:, h * T // 2:(h + 1) * T // 2], h * GUARD + i, 1)
                    guard_keys(0, 0, range(GUARD))

                def split_queries():
                    dve.tensor_copy(parts[:, 0, :], q_t[:]).then_inc(q_split, 1)
                    dve.wait_ge(q_split, 1)
                    dve.tensor_tensor(q_t[:], q_t[:], parts[:, 0, :], ALU.subtract).then_inc(q_split, 1)
                    dve.wait_ge(q_split, 2)
                    dve.tensor_copy(parts[:, 1, :], q_t[:]).then_inc(q_split, 1)
                    dve.wait_ge(q_split, 3)
                    dve.tensor_tensor(parts[:, 2, :], q_t[:], parts[:, 1, :], ALU.subtract).then_inc(q_split, 1)

                def split_keys(n):
                    dve.wait_ge(whole_ready, n + 1)
                    dve.wait_ge(k_ready, n + 1)
                    wait(dve, k_stored, n * 16)
                    dve.tensor_tensor(k_whole, k_whole, k_parts[:, 0, :], ALU.subtract).then_inc(k_split, 1)
                    dve.wait_ge(k_split, n * 3 + 1)
                    dve.tensor_copy(k_parts[:, 1, :], k_whole).then_inc(k_split, 1)
                    dve.wait_ge(k_split, n * 3 + 2)
                    dve.tensor_tensor(k_parts[:, 2, :], k_whole, k_parts[:, 1, :], ALU.subtract).then_inc(k_split, 1)

                if packed:
                    dve.wait_ge(x_away, 16)
                    dve.wait_ge(q_ready, NQ)
                    split_queries()
                    split_keys(0)

                def push_masked(n):
                    dve.wait_ge(mask_in[0], n * 32 + 32)
                    wait(dve, counted_ready, n)
                    wait(dve, shift_ready, n * HP)
                    dve.tensor_scalar(push[:], mask[:, 0, :], 0.0, -BIG, ALU.is_equal,
                                      ALU.mult).then_inc(push_ready, 1)

                def v_copy(n, j):
                    dve.wait_ge(v_turned, n + 1)
                    wait(dve, pv_ready, n - 1)
                    dve.tensor_tensor(v[:, j, :, :].rearrange("p (b c) d -> p b c d", b=3),
                                      scores[bank("v", 1 - j)][0:KC, :, :].rearrange("p b (c d) -> p b c d", c=4),
                                      bv[0:KC, :].unsqueeze(1).unsqueeze(1).broadcast_to((KC, 3, 4, D)),
                                      ALU.add).then_inc(v_ready, 1)

                def copy(n, p):
                    dve.wait_ge(pt_ready, (n * HP + p) * 3 + 2)
                    if p == 0:
                        wait(dve, pv_ready, n)
                    dve.tensor_copy(probs_t[:, 4:8, p * PAIR:(p + 1) * PAIR],
                                    pt[(p + 1) % 2][0:KC, 0:QUAD].rearrange("p (c q) -> p c q", c=4)).then_inc(dve_copied, 1)

                K_INV = 5 if select else 1
                K_FIN = 5 if select else 2

                def divide(m, j):
                    dve.wait_ge(probs_ready, (m + 1) * HP)
                    at = m * (K_INV + K_FIN)
                    if select:
                        dve.wait_ge(share_ready, m + 1)
                        dve.wait_ge(counted_ready, m + 1)
                        dve.tensor_scalar(share_den[:], share[:], counted[:, j:j + 1], None,
                                          ALU.mult).then_inc(inv_steps, 1)
                        dve.wait_ge(inv_steps, at + 1)
                        dve.tensor_tensor(share_den[:], share_den[:], sums[:, j, :],
                                          ALU.add).then_inc(inv_steps, 1)
                        dve.wait_ge(inv_steps, at + 2)
                        dve.reciprocal(inv[:], share_den[:]).then_inc(inv_steps, 1)
                        dve.wait_ge(inv_steps, at + 3)
                        dve.tensor_tensor(share_den[:], share[:], inv[:], ALU.mult).then_inc(inv_steps, 1)
                        dve.wait_ge(inv_steps, at + 4)
                        wait(dve, pv_ready, m)
                        dve.tensor_tensor(spread[:, :, 1, :], eye2[:].unsqueeze(1).broadcast_to((PAIR, HP, S)),
                                          share_den[:].unsqueeze(2).broadcast_to((PAIR, HP, S)),
                                          ALU.mult).then_inc(inv_steps, 1)
                    else:
                        dve.reciprocal(inv[:], sums[:, j, :]).then_inc(inv_steps, 1)
                        dve.wait_ge(inv_steps, at + 1)
                        wait(dve, pv_ready, m)
                    dve.tensor_tensor(spread[:, :, 0, :], eye2[:].unsqueeze(1).broadcast_to((PAIR, HP, S)),
                                      inv[:].unsqueeze(2).broadcast_to((PAIR, HP, S)),
                                      ALU.mult).then_inc(spread_ready, 1)

                def finish(m, j):
                    dve.wait_ge(pv_ready, m + 1)
                    po = scores[bank("pv", 1 - j)][:, 0, :]
                    at = m * (K_INV + K_FIN) + K_INV
                    wait(dve, attn_ready, m)
                    dve.tensor_tensor(diag[:], po[:, 0:4 * S].rearrange("p (h q) -> p h q", h=4),
                                      in_group[:].unsqueeze(2).broadcast_to((D, 4, S)),
                                      ALU.mult).then_inc(inv_steps, 1)
                    dve.wait_ge(inv_steps, at + 1)
                    dve.tensor_reduce(mixed[:], diag[:].rearrange("p h q -> p q h"), AX.X,
                                      ALU.add).then_inc(inv_steps, 1)
                    dve.wait_ge(inv_steps, at + 2)
                    dst = q_t[:, m * S:(m + 1) * S] if isinstance(m, int) else q_t[:, bass.ds(m * S, S)]
                    if select:
                        dve.tensor_copy(out_sum[:], po[:, 6 * S:7 * S]).then_inc(inv_steps, 1)
                        dve.wait_ge(inv_steps, at + 3)
                        dve.tensor_tensor(out_part[:], out_sum[:], po[:, 5 * S:6 * S],
                                          ALU.mult).then_inc(inv_steps, 1)
                        dve.tensor_tensor(mixed[:], mixed[:], po[:, 4 * S:5 * S], ALU.mult).then_inc(inv_steps, 1)
                        dve.wait_ge(inv_steps, at + 5)
                        dve.tensor_tensor(dst, mixed[:], out_part[:], ALU.add).then_inc(attn_ready, 1)
                    else:
                        dve.tensor_tensor(dst, mixed[:], po[:, 4 * S:5 * S], ALU.mult).then_inc(attn_ready, 1)

                v_copy(0, 0)
                if select:
                    push_masked(0)
                    dve.wait_ge(bias_in, 16)
                    clean = Chain(dve, clean_steps)
                    clean(dve.memset(shift[:, 0, :], 0.0))
                    for p in range(HP):
                        is_nan = probs[0].bitcast(I32)
                        clean(dve.tensor_tensor(is_nan, bias[:, p, :], bias[:, p, :], ALU.not_equal))
                        clean(dve.copy_predicated(bias[:, p, :], is_nan, shift[:, 0, :]))
                        clean(dve.tensor_scalar(bias[:, p, :], bias[:, p, :], -MASKED, MASKED, ALU.min, ALU.max))
                VALUE_GUARDS = {3: (0,), 4: (1,), 5: (2,), "v": (3, 4), 7: (5,)}
                KEY_GUARDS = {"k": (0, 1, 2, 3), 2: (4, 5)}

                def sequence(n, j, half):
                    first, final = is_at(n, 0), is_at(n, B - 1)
                    for p, turned in zip(STEPS, turned_in):
                        if p == 1 and not first:
                            divide(n - 1, 1 - j)
                        if p == "pv":
                            if not first:
                                finish(n - 1, 1 - j)
                            continue
                        if p == 6 and not final:
                            v_copy(n + 1, 1 - j)
                        if turned is not None and turned >= 0 and not select:
                            copy(n, turned)
                        elif turned is not None and not first and not select:
                            copy(n - 1, HP + turned)
                        if packed and p == "k" and not final:
                            split_keys(n + 1)
                        if select and p in VALUE_GUARDS:
                            guard_values(n, j, VALUE_GUARDS[p])
                        if select and p in KEY_GUARDS and not final:
                            guard_keys(n + 1, 1 - j, KEY_GUARDS[p])
                        if select and p == 6 and not final:
                            push_masked(n + 1)
                        if p in ("k", "v"):
                            continue
                        if select and p == 0:
                            dve.wait_ge(counted_ready, n + 1)
                            wait(dve, top_ready, n * HP)
                            dve.tensor_scalar(floor[:], counted[:, j:j + 1], 0.5, LOW, ALU.is_lt,
                                              ALU.mult).then_inc(raw_top, 1)
                            dve.wait_ge(raw_top, n * 2 + 1)
                            dve.tensor_scalar(floor[:], floor[:], MASKED, None, ALU.add).then_inc(raw_top, 1)
                        dve.wait_ge(scores_ready, n * HP + p + 1)
                        sc = scores[bank(p, j)][0:PAIR, :, 0:THIRD]
                        wait(dve, top_ready, n * HP + p)
                        wait(dve, pt_ready, (n * HP + p - NB + 1) * 3)
                        if select:
                            dve.wait_ge(counted_ready, n + 1)
                            dve.wait_ge(shift_ready, n * HP + p + 1)
                            sh = shift[:, p % 2, :]
                        elif add:
                            dve.wait_ge(push_ready, n + 1)
                            sh = shift[:, j, :]
                        else:
                            sh = shift[:, 0, :]
                        hold(dve)
                        dve.tensor_tensor_reduce(
                            out=probs[p % NB].rearrange("p (c k) -> p c k", c=3), in0=sc,
                            in1=sh.rearrange("p (c k) -> p c k", c=3), scale=1.0, scalar=LOW,
                            op0=ALU.add, op1=ALU.max, accum_out=top[:, p:p + 1]).then_inc(logits_ready, 1)
                        dve.wait_ge(logits_ready, n * HP + p + 1)
                        wait(dve, probs_ready, (n - 1) * HP)
                        if select:
                            dve.wait_ge(raw_top, n * 2 + 2)
                            wait(dve, share_ready, n - 1)
                            dve.tensor_scalar(neg_top[:, j, p:p + 1], top[:, p:p + 1], floor[:], -1.0,
                                              ALU.max, ALU.mult).then_inc(top_ready, 1)
                        else:
                            dve.tensor_scalar(neg_top[:, j, p:p + 1], top[:, p:p + 1], -1.0, None,
                                              ALU.mult).then_inc(top_ready, 1)

                sequences(dve, sequence)
                divide(B - 1, 1)
                if not select:
                    for p in left:
                        copy(B - 1, p)
                finish(B - 1, 1)
                if select:
                    dve.wait_ge(attn_ready, B)
                    for h in range(2):
                        for i in (0, 1):
                            guard(i, q_t[:, h * T // 2:(h + 1) * T // 2], GUARD_END + 2 * h + i)




def hidden_layer(nc, r, block, src, up, down, chunks, rows, act_fn, put, psum, extra=None):
    up_ready, raw_free, h_ready, down_ready, y_used = (
        r.sem(n) for n in ("up_ready", "raw_free", "h_ready", "down_ready", "y_used"))
    h = r.sb("h", [rows, 2, QUAD])
    pu = [psum("pu0", [128, 512]), psum("pu1", [128, 512])]
    py = [psum("py0", [128, 512]), psum("py1", [128, 512])]
    items = [(q, k) for q in range(NQ) for k in range(chunks)]

    @block.tensor
    def _(pe):
        def add_down(i):
            q, k = items[i]
            pe.wait_ge(h_ready, i + 1)
            if k == 0:
                wait(pe, y_used, q - 1)
            pe.matmul(py[q % 2][:, 0:QUAD], down(k), h[:, i % 2, :], start=(k == 0),
                      stop=(k == chunks - 1)).then_inc(down_ready, 1)

        if extra is not None:
            extra["tensor"](pe)
        for i, (q, k) in enumerate(items):
            wait(pe, h_ready, i - 1)
            last = pe.matmul(pu[i % 2][0:rows, 0:QUAD], up(k), src[:, q * QUAD:(q + 1) * QUAD],
                             start=True, stop=extra is None)
            if extra is not None:
                last = extra["add"](pe, pu[i % 2][0:rows, 0:QUAD], q, k)
            last.then_inc(up_ready, 1)
            if i:
                add_down(i - 1)
        add_down(len(items) - 1)

    @block.scalar
    def _(act):
        if extra is not None:
            extra["scalar"](act)
        for i, (q, k) in enumerate(items):
            act.wait_ge(up_ready, i + 1)
            wait(act, down_ready, i - 1)
            act_fn(act, h[:, i % 2, :], pu[i % 2][0:rows, 0:QUAD], k, i, raw_free, h_ready).then_inc(h_ready, 1)

    @block.vector
    def _(dve):
        if extra is not None:
            extra["vector"](dve)
        for q in range(NQ):
            dve.wait_ge(down_ready, (q + 1) * chunks)
            put(dve, q, py[q % 2][:, 0:QUAD]).then_inc(y_used, 1)


def ternary(dve, chain, w, r, name, rows, cols):
    scale, half, neg = (r.sb(f"{name}_{n}", [128, rows]) for n in ("scale", "half", "neg"))
    below, tern = r.sb(f"{name}_below", [128, cols]), r.sb(f"{name}_tern", [128, cols])
    chain(dve.tensor_reduce(scale[:], w[:], AX.X, ALU.add, apply_absolute_value=True))
    chain(dve.tensor_scalar(scale[:], scale[:], 1.0 / cols, 1e-5, ALU.mult, ALU.max))
    chain(dve.tensor_scalar(half[:], scale[:], 0.5, None, ALU.mult))
    chain(dve.tensor_scalar(neg[:], scale[:], -0.5, None, ALU.mult))
    for i in range(rows):
        wi = w[:, i, :]
        chain(dve.tensor_scalar(below[:], wi, neg[:, i:i + 1], None, ALU.is_lt))
        chain(dve.scalar_tensor_tensor(tern[:], wi, half[:, i:i + 1], below[:], ALU.is_gt, ALU.subtract))
        chain(dve.tensor_tensor(tern[:], tern[:], wi, ALU.subtract))
        chain(dve.tensor_tensor(wi, wi, tern[:], ALU.add))
        chain(dve.tensor_scalar(wi, wi, scale[:, i:i + 1], None, ALU.mult))


def ffn0(nc, g, a):
    r = scope(nc, "ffn0")
    FC, RANK = 4, 16
    with r.ctx:
        w_fc, w_proj = r.sb("w_fc", [128, FC, D]), r.sb("w_proj", [128, 1, FC * D])
        fc_t, proj_t = r.sb("fc_t", [D, FC, 128]), r.sb("proj_t", [128, FC, D])
        v_t, b_t, u_t = r.sb("v_t", [D, RANK]), r.sb("b_t", [RANK, RANK]), r.sb("u_t", [RANK, FC * 128])
        gate = r.sb("gate", [RANK, 1])
        low, mid = r.sb("low", [RANK, T]), r.sb("mid", [RANK, T])
        relu = r.sb("relu", [128, QUAD])
        loaded, steps, w_ready, w_turned, w_copied, low_ready, low_copied, mid_ready, mid_copied = (
            r.sem(n) for n in ("loaded", "steps", "w_ready", "w_turned", "w_copied", "low_ready",
                               "low_copied", "mid_ready", "mid_copied"))
        pw = [r.ps("pw0", [128, 512]), r.ps("pw1", [128, 512])]
        pl = [r.ps("pl0", [128, 512]), r.ps("pl1", [128, 512])]
        loads = [(w_fc[:], a["w_fc"].rearrange("(k p) i -> p k i", p=128)), (w_proj[:, 0, :], a["w_proj"]),
                 (v_t[:], a["v_t"]), (b_t[:], a["fast_b_t"]), (u_t[:], a["u_t"]),
                 (gate[:], a["gate0"].partition_broadcast(RANK))]

        def tensor(pe):
            pe.wait_ge(w_ready, 1)
            for k in range(FC):
                last = pe.transpose(pw[0][:, k * 128:(k + 1) * 128], w_fc[:, k, :], g.ident[:])
            last.then_inc(w_turned, 1)
            for k in range(FC):
                last = pe.transpose(pw[1][:, k * D:(k + 1) * D], w_proj[:, 0, k * 128:(k + 1) * 128], g.ident[:])
            last.then_inc(w_turned, 1)
            for q in range(NQ):
                cols = slice(q * QUAD, (q + 1) * QUAD)
                wait(pe, low_copied, q - 1)
                pe.matmul(pl[q % 2][0:RANK, 0:QUAD], v_t[:], g.xn_t[:, cols], start=True,
                          stop=True).then_inc(low_ready, 1)
            for q in range(NQ):
                cols = slice(q * QUAD, (q + 1) * QUAD)
                pe.wait_ge(low_copied, NQ)
                wait(pe, mid_copied, q - 1)
                pe.matmul(pl[q % 2][0:RANK, 0:QUAD], b_t[:], low[:, cols], start=True,
                          stop=True).then_inc(mid_ready, 1)
            pe.wait_ge(mid_copied, NQ)
            pe.wait_ge(w_copied, 2)

        def scalar(act):
            act.wait_ge(loaded, 16 * len(loads))
            for i, dst in ((0, fc_t), (1, proj_t)):
                act.wait_ge(w_turned, i + 1)
                act.activation(dst[:].rearrange("p k f -> p (k f)"), pw[i][:], ACT.Copy).then_inc(w_copied, 1)
            for q in range(NQ):
                act.wait_ge(low_ready, q + 1)
                act.activation(low[:, q * QUAD:(q + 1) * QUAD], pl[q % 2][0:RANK, 0:QUAD],
                               ACT.Copy).then_inc(low_copied, 1)
            for q in range(NQ):
                act.wait_ge(mid_ready, q + 1)
                act.activation(mid[:, q * QUAD:(q + 1) * QUAD], pl[q % 2][0:RANK, 0:QUAD], ACT.Copy,
                               scale=gate[:]).then_inc(mid_copied, 1)

        def vector(dve):
            chain = Chain(dve, steps)
            dve.wait_ge(loaded, 16 * len(loads))
            ternary(dve, chain, w_fc, r, "fc", FC, D)
            ternary(dve, chain, w_proj, r, "proj", 1, FC * D)
            dve.drain().then_inc(w_ready, 1)

        def add(pe, out, q, k):
            return pe.matmul(out, u_t[:, k * 128:(k + 1) * 128], mid[:, q * QUAD:(q + 1) * QUAD],
                             start=False, stop=True)

        def square_of_relu(act, out, in_, k, i, raw_free, h_ready):
            wait(act, h_ready, i)
            act.activation(relu[:], in_, ACT.Relu).then_inc(raw_free, 1)
            act.wait_ge(raw_free, i + 1)
            return act.activation(out, relu[:], ACT.Square)

        def put(dve, q, y):
            return dve.tensor_copy(g.y_t[:, q * QUAD:(q + 1) * QUAD], y)

        with nc.Block() as block:
            @block.sync
            def _(sp):
                for dst, src in loads:
                    sp.dma_start(dst, src).then_inc(loaded, 16)

            hidden_layer(nc, r, block, g.xn_t, lambda k: fc_t[:, k, :], lambda k: proj_t[:, k, :], FC, 128,
                         square_of_relu, put, r.ps,
                         extra=dict(tensor=tensor, scalar=scalar, vector=vector, add=add))


def route(nc, g, name, a, w_router, b_router, weigh, cw, cwb, cw_t=None):
    r = scope(nc, name)
    with r.ctx:
        wr, br, order = r.sb("wr", [D, E]), r.sb("br", [PAIR, E]), r.sb("order", [PAIR, E])
        shape = [PAIR, TILES, E]
        p, t1, hot1, hot2 = (r.sb(n, shape) for n in ("p", "t1", "hot1", "hot2"))
        m1, m2, s1, s2 = (r.sb(n, [PAIR, TILES]) for n in ("m1", "m2", "s1", "s2"))
        pl = r.ps("pl", [128, TILES, E])
        pb = [r.ps(f"pb{i}", [128, 512]) for i in range(4)]
        loaded, logits_ready, steps, arg_ready, exp_ready, cw_ready, spread, act_used, dve_used, turned = (
            r.sem(n) for n in ("loaded", "logits_ready", "steps", "arg_ready", "exp_ready", "cw_ready",
                               "spread", "act_used", "dve_used", "turned"))
        wide = lambda t: t[:].unsqueeze(2).broadcast_to(tuple(shape))
        with nc.Block() as block:
            @block.sync
            def _(sp):
                sp.dma_start(wr[:], w_router).then_inc(loaded, 16)
                sp.dma_start(order[:], a["c_order"].partition_broadcast(PAIR)).then_inc(loaded, 16)
                if b_router is not None:
                    sp.dma_start(br[:], b_router.partition_broadcast(PAIR)).then_inc(loaded, 16)

            @block.tensor
            def _(pe):
                pe.wait_ge(loaded, 48 if b_router is not None else 32)
                for t in range(TILES):
                    last = pe.matmul(pl[0:PAIR, t, :], g.xn_t[:, t * PAIR:(t + 1) * PAIR], wr[:],
                                     start=True, stop=True)
                last.then_inc(logits_ready, 1)
                pe.wait_ge(cw_ready, 1)
                for i in range(E * NQ):
                    e, q = divmod(i, NQ)
                    if i >= 4:
                        pe.wait_ge(act_used if i % 2 == 0 else dve_used, i // 2 - 1)
                    for t in range(4 * q, 4 * q + 4):
                        last = pe.matmul(pb[i % 4][:, (t % 4) * PAIR:(t % 4 + 1) * PAIR],
                                         cw[:, t, e:e + 1].broadcast_to((PAIR, 128)),
                                         g.ident[0:PAIR, 0:PAIR], start=True, stop=True)
                    last.then_inc(spread, 1)
                if cw_t is not None:
                    for q in range(NQ):
                        pe.wait_ge(act_used if q % 2 == 0 else dve_used, E * NQ // 2)
                        for t in range(4 * q, 4 * q + 4):
                            last = pe.transpose(pb[q][0:E, (t % 4) * PAIR:(t % 4 + 1) * PAIR],
                                                cw[:, t, :], g.ident[0:PAIR, 0:PAIR])
                        last.then_inc(turned, 1)

            @block.scalar
            def _(act):
                act.wait_ge(arg_ready, 1)
                act.activation(p[:], p[:], ACT.Exp).then_inc(exp_ready, 1)
                for i in range(0, E * NQ, 2):
                    e, q = divmod(i, NQ)
                    act.wait_ge(spread, i + 1)
                    act.activation(cwb[:, e, q * QUAD:(q + 1) * QUAD], pb[i % 4][:, 0:QUAD],
                                   ACT.Copy).then_inc(act_used, 1)
                if cw_t is not None:
                    for q in range(NQ):
                        act.wait_ge(turned, q + 1)
                        act.activation(cw_t[:, q * QUAD:(q + 1) * QUAD], pb[q][0:E, 0:QUAD],
                                       ACT.Copy).then_inc(act_used, 1)

            @block.vector
            def _(dve):
                do = Chain(dve, steps)
                dve.wait_ge(logits_ready, 1)
                if b_router is not None:
                    do(dve.tensor_tensor(p[:], pl[0:PAIR, :, :],
                                         br[:].unsqueeze(1).broadcast_to(tuple(shape)), ALU.add))
                else:
                    do(dve.tensor_copy(p[:], pl[0:PAIR, :, :]))
                do(dve.tensor_reduce(m1[:], p[:], AX.X, ALU.max))
                dve.tensor_tensor(p[:], p[:], wide(m1), ALU.subtract).then_inc(arg_ready, 1)
                dve.wait_ge(exp_ready, 1)
                do(dve.tensor_reduce(s1[:], p[:], AX.X, ALU.add))
                do(dve.reciprocal(s1[:], s1[:]))
                do(dve.tensor_tensor(p[:], p[:], wide(s1), ALU.mult))

                def best(m, hot):
                    do(dve.tensor_reduce(m[:], p[:], AX.X, ALU.max))
                    do(dve.tensor_tensor(t1[:], p[:], wide(m), ALU.not_equal))
                    do(dve.scalar_tensor_tensor(t1[:], t1[:], 100.0,
                                                order[:].unsqueeze(1).broadcast_to(tuple(shape)),
                                                ALU.mult, ALU.add))
                    do(dve.tensor_reduce(s2[:], t1[:], AX.X, ALU.min))
                    do(dve.tensor_tensor(hot[:], wide(s2),
                                         order[:].unsqueeze(1).broadcast_to(tuple(shape)), ALU.is_equal))

                best(m1, hot1)
                if weigh == "top1":
                    dve.tensor_tensor(cw[:], hot1[:], wide(m1), ALU.mult).then_inc(cw_ready, 1)
                else:
                    do(dve.scalar_tensor_tensor(p[:], hot1[:], -2.0, p[:], ALU.mult, ALU.add))
                    best(m2, hot2)
                    eps = 1e-8 if weigh == "top2_L1" else 1e-10
                    do(dve.tensor_tensor(s1[:], m1[:], m2[:], ALU.add))
                    do(dve.tensor_scalar(s1[:], s1[:], eps, None, ALU.add))
                    do(dve.reciprocal(s1[:], s1[:]))
                    do(dve.tensor_tensor(m1[:], m1[:], s1[:], ALU.mult))
                    do(dve.tensor_tensor(m2[:], m2[:], s1[:], ALU.mult))
                    if weigh == "top2_L2":
                        do(dve.tensor_tensor(s2[:], m1[:], m2[:], ALU.add))
                        do(dve.tensor_scalar(s1[:], s2[:], eps, None, ALU.max))
                        do(dve.reciprocal(s1[:], s1[:]))
                        do(dve.tensor_scalar(s2[:], s2[:], eps, 1.0, ALU.mult, ALU.add))
                        do(dve.tensor_tensor(s1[:], s1[:], s2[:], ALU.mult))
                        do(dve.tensor_tensor(m1[:], m1[:], s1[:], ALU.mult))
                        do(dve.tensor_tensor(m2[:], m2[:], s1[:], ALU.mult))
                    do(dve.tensor_tensor(hot1[:], hot1[:], wide(m1), ALU.mult))
                    do(dve.tensor_tensor(hot2[:], hot2[:], wide(m2), ALU.mult))
                    dve.tensor_tensor(cw[:], hot1[:], hot2[:], ALU.add).then_inc(cw_ready, 1)
                for i in range(1, E * NQ, 2):
                    e, q = divmod(i, NQ)
                    dve.wait_ge(spread, i + 1)
                    dve.tensor_copy(cwb[:, e, q * QUAD:(q + 1) * QUAD], pb[i % 4][:, 0:QUAD]).then_inc(dve_used, 1)


def experts(nc, g, name, a, w_experts, cwb, b_experts=None, cw_t=None):
    r = scope(nc, name)
    with r.ctx:
        we = r.sb("we", [D, E, D])
        be = r.sb("be", [E, D])
        xs = r.sb("xs", [D, 2, T])
        py = [r.ps(f"py{q}", [128, 512]) for q in range(NQ)]
        loaded, xs_ready, xs_used, y_ready, y_copied = (
            r.sem(n) for n in ("loaded", "xs_ready", "xs_used", "y_ready", "y_copied"))
        with nc.Block() as block:
            @block.sync
            def _(sp):
                sp.dma_start(we[:], w_experts.rearrange("e h d -> h e d")).then_inc(loaded, 16)
                if b_experts is not None:
                    sp.dma_start(be[:], b_experts).then_inc(loaded, 16)

            @block.vector
            def _(dve):
                for e in range(E):
                    wait(dve, xs_used, e - 1)
                    dve.tensor_tensor(xs[:, e % 2, :], g.xn_t[:], cwb[:, e, :], ALU.mult).then_inc(xs_ready, 1)

            @block.tensor
            def _(pe):
                pe.wait_ge(loaded, 16 if b_experts is None else 32)
                if b_experts is not None:
                    for q in range(NQ):
                        pe.matmul(py[q][:, 0:QUAD], be[:], cw_t[:, q * QUAD:(q + 1) * QUAD], start=True, stop=False)
                for e in range(E):
                    pe.wait_ge(xs_ready, e + 1)
                    for q in range(NQ):
                        last = pe.matmul(py[q][:, 0:QUAD], we[:, e, :], xs[:, e % 2, q * QUAD:(q + 1) * QUAD],
                                         start=(e == 0 and b_experts is None), stop=(e == E - 1))
                    last.then_inc(xs_used, 1)

            @block.scalar
            def _(act):
                act.wait_ge(xs_used, E)
                for q in range(NQ):
                    act.activation(g.y_t[:, q * QUAD:(q + 1) * QUAD], py[q][:, 0:QUAD], ACT.Copy).then_inc(y_copied, 1)


def ffn2(nc, g, a):
    r = scope(nc, "ffn2")
    with r.ctx:
        cw, cwb = r.sb("cw", [PAIR, TILES, E]), r.sb("cwb", [128, E, T])
        route(nc, g, "route2", a, a["router2"], a["router2_b"], "top2_L2", cw, cwb)
        experts(nc, g, "experts2", a, a["experts2"], cwb)


def ffn3(nc, g, a):
    r = scope(nc, "ffn3")
    with r.ctx:
        cw, cwb, cw_t = r.sb("cw", [PAIR, TILES, E]), r.sb("cwb", [128, E, T]), r.sb("cw_t", [E, T])
        route(nc, g, "route3", a, a["router3"], a["router3_b"], "top1", cw, cwb, cw_t)
        experts(nc, g, "experts3", a, a["experts3"], cwb, a["experts3_b"], cw_t)


def ffn1(nc, g, a):
    r = scope(nc, "ffn1")
    with r.ctx:
        cw, cwb = r.sb("cw", [PAIR, TILES, E]), r.sb("cwb", [128, E + 1, T])
        route(nc, g, "route1", a, a["router1"], None, "top2_L1", cw, cwb[:, 1:, :])
        gu = r.sb("gu", [D, 2, 2 * F1])
        dn = r.sb("dn", [F1C, 2, F1K, D])
        silu, h = r.sb("silu", [F1C, 2, QUAD]), r.sb("h", [F1C, 2, QUAD])
        part = r.sb("part", [D, 2, QUAD])
        pg, pu, py = ([r.ps(f"{n}{i}", [128, 512]) for i in range(2)] for n in ("pg", "pu", "py"))
        w_in = [r.sem("w_even"), r.sem("w_odd")]
        up_ready, silu_ready, h_ready, down_ready, part_ready, sum_ready, zeroed = (
            r.sem(n) for n in ("up_ready", "silu_ready", "h_ready", "down_ready", "part_ready", "sum_ready", "zeroed"))
        items = [(q, k) for q in range(NQ) for k in range(F1K)]
        N = len(items)
        size = lambda k: min(F1C, F1 - k * F1C)
        FULL = F1C * (F1K - 1)

        def passes(eng, body):
            for n in (0, 1):
                body(n, n, 0)
            with eng.Fori(1, E // 2) as half:
                for j in (0, 1):
                    body(half * 2 + j, j, half)
            body(E, 0, E // 2)

        with nc.Block() as block:
            @block.sync
            def _(sp):
                def load(n, j, half):
                    wait(sp, down_ready, (n - 1) * N)
                    up, down = (a["shared_up_t"], a["shared_down_t"]) if is_at(n, 0) else \
                        (a["experts_up_t"][n - 1], a["experts_down_t"][n - 1])
                    sp.dma_start(gu[:, j, :], up).then_inc(w_in[j], 16)
                    sp.dma_start(dn[:, j, 0:F1K - 1, :],
                                 down[0:FULL, :].rearrange("(k p) d -> p k d", p=F1C)).then_inc(w_in[j], 16)
                    sp.dma_start(dn[0:F1 - FULL, j, F1K - 1, :], down[FULL:F1, :]).then_inc(w_in[j], 16)
                passes(sp, load)

            @block.tensor
            def _(pe):
                def down(n, j, i):
                    q, k = items[i]
                    pe.wait_ge(h_ready, n * N + i + 1)
                    if k == 0:
                        wait(pe, part_ready, n * NQ + q - 1)
                    pe.matmul(py[q % 2][:, 0:QUAD], dn[0:size(k), j, k, :], h[0:size(k), i % 2, :],
                              start=(k == 0), stop=(k == F1K - 1)).then_inc(down_ready, 1)

                def body(n, j, half):
                    pe.wait_ge(w_in[j], half * 48 + 48)
                    for i, (q, k) in enumerate(items):
                        wait(pe, h_ready, n * N + i - 1)
                        for bank, at in ((pg, 0), (pu, F1)):
                            last = pe.matmul(bank[i % 2][0:size(k), 0:QUAD],
                                             gu[:, j, at + k * F1C:at + k * F1C + size(k)],
                                             g.xn_t[:, q * QUAD:(q + 1) * QUAD], start=True, stop=True)
                        last.then_inc(up_ready, 1)
                        if i:
                            down(n, j, i - 1)
                        elif not is_at(n, 0):
                            down(n - 1, 1 - j, N - 1)
                passes(pe, body)
                down(E, 0, N - 1)

            @block.scalar
            def _(act):
                def body(n, j, half):
                    for i, (q, k) in enumerate(items):
                        act.wait_ge(up_ready, n * N + i + 1)
                        wait(act, h_ready, n * N + i - 1)
                        act.activation(silu[0:size(k), i % 2, :], pg[i % 2][0:size(k), 0:QUAD],
                                       ACT.Silu).then_inc(silu_ready, 1)
                passes(act, body)

            @block.gpsimd
            def _(pool):
                def body(n, j, half):
                    for q in range(NQ):
                        pool.wait_ge(part_ready, n * NQ + q + 1)
                        wait(pool, sum_ready, (n - 1) * NQ + q + 1)
                        cols = g.y_t[:, q * QUAD:(q + 1) * QUAD]
                        pool.tensor_tensor(cols, cols, part[:, q % 2, :], ALU.add).then_inc(sum_ready, 1)
                pool.wait_ge(zeroed, 2)
                passes(pool, body)

            @block.vector
            def _(dve):
                def take(n, q):
                    wait(dve, sum_ready, n * NQ + q - 1)
                    cols = cwb[:, n, q * QUAD:(q + 1) * QUAD] if isinstance(n, int) else \
                        cwb[:].rearrange("p e t -> p (e t)")[:, bass.ds(n * T + q * QUAD, QUAD)]
                    dve.tensor_tensor(part[:, q % 2, :], py[q % 2][:, 0:QUAD], cols, ALU.mult).then_inc(part_ready, 1)

                def body(n, j, half):
                    for i, (q, k) in enumerate(items):
                        dve.wait_ge(silu_ready, n * N + i + 1)
                        wait(dve, down_ready, n * N + i - 1)
                        dve.tensor_tensor(h[0:size(k), i % 2, :], silu[0:size(k), i % 2, :],
                                          pu[i % 2][0:size(k), 0:QUAD], ALU.mult).then_inc(h_ready, 1)
                        if k == 0 and not (is_at(n, 0) and q == 0):
                            dve.wait_ge(down_ready, n * N + i)
                            take(n if q else n - 1, (q - 1) % NQ)

                dve.memset(cwb[:, 0, :], 1.0).then_inc(zeroed, 1)
                dve.memset(g.y_t[:], 0.0).then_inc(zeroed, 1)
                dve.wait_ge(zeroed, 2)
                passes(dve, body)
                dve.wait_ge(down_ready, (E + 1) * N)
                take(E, NQ - 1)


def attention2(nc, g, a):
    whole = scope(nc, "attn2")
    INNER, HW = H2 * DH2, 512
    with whole.ctx:
        q_t = whole.sb("q_t", [128, HP, T])
        w_vo = whole.sb("w_vo", [D, H2, D])
        wk = whole.sb("wk", [D, INNER])
        bo = whole.sb("bo", [D, 1])

        r = scope(nc, "attn2q")
        with r.ctx:
            wq, wv_t, wo = r.sb("wq", [D, INNER]), r.sb("wv_t", [DH2, H2, D]), r.sb("wo", [DH2, H2, D])
            sq = r.sb("sq", [PAIR, 2, INNER])
            qn = r.sb("qn", [PAIR, 2, INNER])
            ss, rn = r.sb("ss", [PAIR, 2, H2]), r.sb("rn", [PAIR, 2, H2])
            pq = [r.ps(f"pq{i}", [128, 2, 512]) for i in range(2)]
            pt = [r.ps(f"pt{i}", [128, 2, 512]) for i in range(2)]
            loaded, vo_ready, vo_copied, q_ready, sq_ready, ss_ready, root_ready, steps, qn_ready, q_turned, act_copied, dve_copied = (
                r.sem(n) for n in ("loaded", "vo_ready", "vo_copied", "q_ready", "sq_ready", "ss_ready",
                                   "root_ready", "steps", "qn_ready", "q_turned", "act_copied", "dve_copied"))
            with nc.Block() as block:
                @block.sync
                def _(sp):
                    for dst, src in ((wq[:], a["wq2"]), (wk[:], a["wk2"]), (wv_t[:], a["wv2_t"].rearrange("(h r) c -> r h c", r=DH2)),
                                     (wo[:], a["wo2"].rearrange("(h r) c -> r h c", r=DH2)), (bo[:], a["bo2"])):
                        sp.dma_start(dst, src).then_inc(loaded, 16)
                    sp.wait_ge(loaded, 80)

                @block.tensor
                def _(pe):
                    pe.wait_ge(loaded, 80)
                    for half in range(2):
                        for h in range(8 * half, 8 * half + 8):
                            last = pe.matmul(pq[half][:, h % 8 // 4, (h % 4) * D:(h % 4 + 1) * D],
                                             wv_t[:, h, :], wo[:, h, :], start=True, stop=True)
                        last.then_inc(vo_ready, 1)

                    def turn(t):
                        pe.wait_ge(qn_ready, t + 1)
                        wait(pe, act_copied, t - 1)
                        wait(pe, dve_copied, t - 1)
                        for p in range(HP):
                            last = pe.transpose(pt[t % 2][:, p // 4, (p % 4) * PAIR:(p % 4 + 1) * PAIR],
                                                qn[:, t % 2, p * 128:(p + 1) * 128], g.ident[0:PAIR, 0:PAIR])
                        last.then_inc(q_turned, 1)

                    for t in range(TILES):
                        if t < 2:
                            pe.wait_ge(vo_copied, t + 1)
                        wait(pe, qn_ready, t - 1)
                        for c in range(2):
                            last = pe.matmul(pq[t % 2][0:PAIR, c, :], g.z_t[:, t * PAIR:(t + 1) * PAIR],
                                             wq[:, c * HW:(c + 1) * HW], start=True, stop=True)
                        last.then_inc(q_ready, 1)
                        if t:
                            turn(t - 1)
                    turn(TILES - 1)

                @block.scalar
                def _(act):
                    for half in range(2):
                        act.wait_ge(vo_ready, half + 1)
                        act.activation(w_vo[:, 8 * half:8 * half + 8, :].rearrange("p h d -> p (h d)"),
                                       pq[half][:].rearrange("p a b -> p (a b)"), ACT.Copy).then_inc(vo_copied, 1)

                    def copy(t):
                        act.wait_ge(q_turned, t + 1)
                        act.activation(q_t[:, 0:4, t * PAIR:(t + 1) * PAIR],
                                       pt[t % 2][:, 0, 0:QUAD].rearrange("p (a b) -> p a b", a=4),
                                       ACT.Copy).then_inc(act_copied, 1)
                    for t in range(TILES):
                        act.wait_ge(q_ready, t + 1)
                        wait(act, ss_ready, t - 1)
                        act.activation(sq[:, t % 2, :].rearrange("p (a b) -> p a b", a=2), pq[t % 2][0:PAIR, :, :],
                                       ACT.Square).then_inc(sq_ready, 1)
                        act.wait_ge(ss_ready, t + 1)
                        act.activation(ss[:, t % 2, :], ss[:, t % 2, :], ACT.Sqrt).then_inc(root_ready, 1)
                        if t:
                            copy(t - 1)
                    copy(TILES - 1)

                @block.vector
                def _(dve):
                    chain = Chain(dve, steps)

                    def copy(t):
                        dve.wait_ge(q_turned, t + 1)
                        dve.tensor_copy(q_t[:, 4:8, t * PAIR:(t + 1) * PAIR],
                                        pt[t % 2][:, 1, 0:QUAD].rearrange("p (a b) -> p a b", a=4)).then_inc(dve_copied, 1)
                    for t in range(TILES):
                        dve.wait_ge(sq_ready, t + 1)
                        dve.tensor_reduce(ss[:, t % 2, :], sq[:, t % 2, :].rearrange("p (h d) -> p h d", h=H2),
                                          AX.X, ALU.add).then_inc(ss_ready, 1)
                        if t:
                            copy(t - 1)
                        dve.wait_ge(root_ready, t + 1)
                        chain(dve.tensor_scalar(rn[:, t % 2, :], ss[:, t % 2, :], 1e-12, None, ALU.max))
                        chain(dve.reciprocal(rn[:, t % 2, :], rn[:, t % 2, :]))
                        wait(dve, q_turned, t - 1)
                        dve.tensor_tensor(qn[:, t % 2, :].rearrange("p (h d) -> p h d", h=H2),
                                          pq[t % 2][0:PAIR, :, :].rearrange("p a (h d) -> p (a h) d", h=8),
                                          rn[:, t % 2, :].unsqueeze(2).broadcast_to((PAIR, H2, DH2)),
                                          ALU.mult).then_inc(qn_ready, 1)
                    copy(TILES - 1)

        r = scope(nc, "attn2k")
        with r.ctx:
            ctx = r.sb("ctx", [KC, 2, CH, D])
            cn = r.sb("cn", [KC, 2, CH, D])
            gain, shift = r.sb("gain", [KC, D]), r.sb("shift", [KC, D])
            stats, mv = r.sb("stats", [KC, CH, 6]), r.sb("mv", [KC, CH, 2])
            var, rs, off = r.sb("var", [KC, CH]), r.sb("rs", [KC, CH]), r.sb("off", [KC, CH])
            cn_t = r.sb("cn_t", [D, 2, KC])
            sq, kn = r.sb("sq", [KC, 2, INNER]), r.sb("kn", [KC, 2, INNER])
            ss, rn = r.sb("ss", [KC, 2, H2]), r.sb("rn", [KC, 2, H2])
            gram = r.sb("gram", [D, INNER])
            state = r.sb("state", [128, HP, D])
            q_now = r.sb("q_now", [128, HP, S])
            pk = [r.ps(f"pk{i}", [128, 2, 512]) for i in range(2)]
            pg = r.ps("pg", [128, 2, 512])
            pt, pz = r.ps("pt", [128, 512]), r.ps("pz", [128, 512])
            (held, const_in, ctx_even, ctx_odd, steps, var_ready, root_ctx, scale_ready, raw_ready, scaled, cn_ready, c_turned, c_copied, k_ready,
             sq_ready, ss_ready, root_ready, clipped, kn_ready, summed, gram_low, gram_high, state_ready, state_copied,
             q_copied, y_ready, y_copied) = (r.sem(n) for n in (
                 "held", "const_in", "ctx_even", "ctx_odd", "steps", "var_ready", "root_ctx", "scale_ready", "raw_ready", "scaled", "cn_ready", "c_turned",
                 "c_copied", "k_ready", "sq_ready", "ss_ready", "root_ready", "clipped", "kn_ready", "summed", "gram_low",
                 "gram_high", "state_ready", "state_copied", "q_copied", "y_ready", "y_copied"))
            ctx_in = (ctx_even, ctx_odd)

            is_first, is_last = (lambda n: is_at(n, 0)), (lambda n: is_at(n, B - 1))

            with nc.Block() as block:
                @block.sync
                def _(sp):
                    sp.dma_start(gain[:], a["ln1_g_row"].partition_broadcast(KC)).then_inc(const_in, 16)
                    sp.dma_start(shift[:], a["ln1_b_row"].partition_broadcast(KC)).then_inc(const_in, 16)

                    def load(n, j, half):
                        wait(sp, raw_ready, (n - 1) * CH)
                        sp.dma_start(ctx[:, j, :, :], a["ctx"][n].rearrange("(c p) d -> p c d", p=KC)).then_inc(ctx_in[j], 16)
                    sequences(sp, load)

                @block.gpsimd
                def _(pool):
                    pool.wait_ge(const_in, 32)

                    def body(n, j, half):
                        pool.wait_ge(raw_ready, (n + 1) * CH)
                        pool.tensor_tensor(cn[:, j, :, :], cn[:, j, :, :],
                                           gain[:].unsqueeze(1).broadcast_to((KC, CH, D)), ALU.mult).then_inc(scaled, 1)
                        pool.wait_ge(scaled, n + 1)
                        pool.tensor_tensor(cn[:, j, :, :], cn[:, j, :, :],
                                           shift[:].unsqueeze(1).broadcast_to((KC, CH, D)), ALU.add).then_inc(cn_ready, 1)
                        wait(pool, y_ready, n)
                        src = q_t[:, :, n * S:(n + 1) * S] if isinstance(n, int) else q_t[:, :, bass.ds(n * S, S)]
                        pool.tensor_copy(q_now[:], src).then_inc(q_copied, 1)
                    sequences(pool, body)

                @block.tensor
                def _(pe):
                    def turn(n, j, c):
                        i = n * CH + c
                        if c == 0:
                            pe.wait_ge(cn_ready, n + 1)
                        wait(pe, c_copied, i)
                        pe.transpose(pt[:, 0:KC], cn[:, j, c, :], g.ident[0:KC, 0:KC]).then_inc(c_turned, 1)

                    def keys(n, c):
                        i = n * CH + c
                        pe.wait_ge(c_copied, i + 1)
                        wait(pe, kn_ready, i - 1)
                        for b in range(2):
                            last = pe.matmul(pk[c % 2][0:KC, b, :], cn_t[:, c % 2, :], wk[:, b * HW:(b + 1) * HW],
                                             start=True, stop=True)
                        last.then_inc(k_ready, 1)

                    def add(n, j, c):
                        pe.wait_ge(kn_ready, n * CH + c + 1)
                        if c == 0:
                            wait(pe, gram_low, n)
                            wait(pe, gram_high, n)
                        for b in range(2):
                            last = pe.matmul(pg[:, b, :], cn[:, j, c, :], kn[:, c % 2, b * HW:(b + 1) * HW],
                                             start=(c == 0), stop=(c == CH - 1))
                        last.then_inc(summed, 1)

                    def states(n, half):
                        pe.wait_ge(gram_low if half == 0 else gram_high, n + 1)
                        if half == 0:
                            wait(pe, y_copied, n)
                        else:
                            pe.wait_ge(state_copied, 2 * n + 1)
                        for h in range(8 * half, 8 * half + 8):
                            rows = slice(DH2 * (h % 2), DH2 * (h % 2) + DH2)
                            last = pe.matmul(pz[rows, (h % 8 // 2) * D:(h % 8 // 2 + 1) * D],
                                             gram[:, h * DH2:(h + 1) * DH2], w_vo[:, h, :], start=True, stop=True)
                        last.then_inc(state_ready, 1)

                    def out(n):
                        pe.wait_ge(state_copied, 2 * n + 2)
                        pe.wait_ge(q_copied, n + 1)
                        for p in range(HP):
                            last = pe.matmul(pz[:, 0:S], state[:, p, :], q_now[:, p, :], start=(p == 0), stop=(p == HP - 1))
                        last.then_inc(y_ready, 1)

                    pe.wait_ge(const_in, 32)
                    turn(0, 0, 0)

                    def body(n, j, half):
                        for c in range(CH):
                            keys(n, c)
                            if c < CH - 1:
                                turn(n, j, c + 1)
                            elif not is_last(n):
                                turn(n + 1, 1 - j, 0)
                            if c >= 2:
                                add(n, j, c - 2)
                            elif not is_first(n):
                                add(n - 1, 1 - j, CH - 2 + c)
                            if not is_first(n):
                                if c in (3, 5):
                                    states(n - 1, (c - 3) // 2)
                                if c == 7:
                                    out(n - 1)
                    sequences(pe, body)
                    add(B - 1, 1, CH - 2)
                    add(B - 1, 1, CH - 1)
                    states(B - 1, 0)
                    states(B - 1, 1)
                    out(B - 1)

                @block.scalar
                def _(act):
                    def root(n):
                        act.wait_ge(var_ready, n + 1)
                        act.activation(var[:], var[:], ACT.Sqrt).then_inc(root_ctx, 1)

                    def turned(n, c):
                        i = n * CH + c
                        act.wait_ge(c_turned, i + 1)
                        wait(act, k_ready, i - 1)
                        act.activation(cn_t[:, c % 2, :], pt[:, 0:KC], ACT.Copy).then_inc(c_copied, 1)

                    def tail(n, c):
                        if c == 1:
                            act.wait_ge(summed, (n + 1) * CH)
                            wait(act, state_ready, 2 * n)
                            act.activation(gram[:, 0:HW], pg[:, 0, :], ACT.Copy).then_inc(gram_low, 1)
                            act.activation(gram[:, HW:INNER], pg[:, 1, :], ACT.Copy).then_inc(gram_high, 1)
                        if c in (3, 5):
                            hf = (c - 3) // 2
                            act.wait_ge(state_ready, 2 * n + hf + 1)
                            wait(act, y_ready, n)
                            act.activation(state[:, 4 * hf:4 * hf + 4, :].rearrange("p a d -> p (a d)"), pz[:],
                                           ACT.Copy).then_inc(state_copied, 1)
                        if c == 7:
                            act.wait_ge(y_ready, n + 1)
                            dst = g.y_t[:, n * S:(n + 1) * S] if isinstance(n, int) else g.y_t[:, bass.ds(n * S, S)]
                            act.activation(dst, pz[:, 0:S], ACT.Identity, bias=bo[:]).then_inc(y_copied, 1)

                    def normed(n, j, chunks):
                        act.wait_ge(scale_ready, n + 1)
                        wait(act, summed, (n - 1) * CH)
                        for c in chunks:
                            act.activation(cn[:, j, c, :], ctx[:, j, c, :], ACT.Identity, bias=off[:, c:c + 1],
                                           scale=rs[:, c:c + 1]).then_inc(raw_ready, 1)

                    root(0)
                    normed(0, 0, range(CH))
                    turned(0, 0)

                    def body(n, j, half):
                        for c in range(CH):
                            i = n * CH + c
                            act.wait_ge(k_ready, i + 1)
                            wait(act, ss_ready, i - 1)
                            act.activation(sq[:, c % 2, :].rearrange("p (a b) -> p a b", a=2), pk[c % 2][0:KC, :, :],
                                           ACT.Square).then_inc(sq_ready, 1)
                            if c < CH - 1:
                                turned(n, c + 1)
                            act.wait_ge(ss_ready, i + 1)
                            act.activation(ss[:, c % 2, :], ss[:, c % 2, :], ACT.Sqrt).then_inc(root_ready, 1)
                            if c == 4 and not is_last(n):
                                root(n + 1)
                            if 5 <= c < 9 and not is_last(n):
                                normed(n + 1, 1 - j, range(3 * (c - 5), 3 * (c - 4)))
                            if c == CH - 1 and not is_last(n):
                                turned(n + 1, 0)
                            if not is_first(n):
                                tail(n - 1, c)
                    sequences(act, body)
                    for c in (1, 3, 5, 7):
                        tail(B - 1, c)

                @block.vector
                def _(dve):
                    def stat(n, j, half, step):
                        if step < 3:
                            if step == 0:
                                dve.wait_ge(ctx_in[j], half * 16 + 16)
                                wait(dve, steps, n * 3)
                            for c in range(4 * step, 4 * step + 4):
                                last = dve.bn_stats(stats[:, c, :], ctx[:, j, c, :])
                            if step == 2:
                                last.then_inc(steps, 1)
                            return
                        dve.wait_ge(steps, n * 3 + 1)
                        wait(dve, scale_ready, n)
                        dve.sem_inc(held, 1)
                        for c in range(CH):
                            last = dve.bn_aggr(mv[:, c, :], stats[:, c, :])
                        last.then_inc(steps, 1)
                        dve.wait_ge(steps, n * 3 + 2)
                        dve.tensor_scalar(var[:], mv[:, :, 1], EPS, None, ALU.add).then_inc(var_ready, 1)

                    def scales(n):
                        dve.wait_ge(root_ctx, n + 1)
                        wait(dve, raw_ready, n * CH)
                        dve.reciprocal(rs[:], var[:]).then_inc(steps, 1)
                        dve.wait_ge(steps, n * 3 + 3)
                        dve.scalar_tensor_tensor(off[:], mv[:, :, 0], -1.0, rs[:], ALU.mult, ALU.mult).then_inc(scale_ready, 1)

                    for step in range(4):
                        stat(0, 0, 0, step)
                    scales(0)

                    def body(n, j, half):
                        nj, nhalf = 1 - j, (half if j == 0 else half + 1)
                        for c in range(CH):
                            i = n * CH + c
                            dve.wait_ge(sq_ready, i + 1)
                            wait(dve, kn_ready, i - 1)
                            dve.tensor_reduce(ss[:, c % 2, :], sq[:, c % 2, :].rearrange("p (h d) -> p h d", h=H2),
                                              AX.X, ALU.add).then_inc(ss_ready, 1)
                            if c < 4 and not is_last(n):
                                stat(n + 1, nj, nhalf, c)
                            if c == 5 and not is_last(n):
                                scales(n + 1)
                            dve.wait_ge(root_ready, i + 1)
                            dve.tensor_scalar(rn[:, c % 2, :], ss[:, c % 2, :], 1e-12, None, ALU.max).then_inc(clipped, 1)
                            dve.wait_ge(clipped, 2 * i + 1)
                            dve.reciprocal(rn[:, c % 2, :], rn[:, c % 2, :]).then_inc(clipped, 1)
                            dve.wait_ge(clipped, 2 * i + 2)
                            wait(dve, summed, i - 1)
                            dve.tensor_tensor(kn[:, c % 2, :].rearrange("p (h d) -> p h d", h=H2),
                                              pk[c % 2][0:KC, :, :].rearrange("p a (h d) -> p (a h) d", h=8),
                                              rn[:, c % 2, :].unsqueeze(2).broadcast_to((KC, H2, DH2)),
                                              ALU.mult).then_inc(kn_ready, 1)

                    sequences(dve, body)

    r = scope(nc, "attn2m")
    with r.ctx:
        g2, s2 = r.sb("g2", [D, 1]), r.sb("s2", [D, 1])
        w1, w2 = r.sb("w1", [D, 4, 128]), r.sb("w2", [128, 4, D])
        b1, b2 = r.sb("b1", [128, 4]), r.sb("b2", [D, 1])
        loaded, added = r.sem("loaded"), r.sem("added")
        with nc.Block() as block:
            @block.sync
            def _(sp):
                for dst, src in ((g2[:], a["ln2_g"]), (s2[:], a["ln2_b"]), (w1[:], a["w1_2"].rearrange("i (k f) -> i k f", k=4)),
                                 (w2[:], a["w2_2"].rearrange("(k f) o -> f k o", f=128)), (b1[:], a["b1_2"]), (b2[:], a["b2_2"])):
                    sp.dma_start(dst, src).then_inc(loaded, 16)
                sp.wait_ge(loaded, 96)

            @block.vector
            def _(dve):
                dve.tensor_tensor(g.y_t[:], g.y_t[:], g.xn_t[:], ALU.add).then_inc(added, 1)
                dve.wait_ge(added, 1)
        norm(nc, g, "norm4m", only_y=(g2[:], s2[:]))

        def gelu(act, out, in_, k, i, raw_free, h_ready):
            return act.activation(out, in_, ACT.Gelu, bias=b1[:, k:k + 1])

        def put(dve, q, y):
            cols = g.y_t[:, q * QUAD:(q + 1) * QUAD]
            return dve.scalar_tensor_tensor(cols, y, b2[:], cols, ALU.add, ALU.add)

        with nc.Block() as block:
            hidden_layer(nc, r, block, g.z_t, lambda k: w1[:, k, :], lambda k: w2[:, k, :], 4, 128, gelu, put, r.ps)


def constants():
    rows, f = np.arange(PAIR), np.arange(D)
    head_rows = (rows // S)[:, None] == (np.arange(2 * D - 16)[None, :] - (D - 16)) // DH
    return {
        "c_order": np.arange(E, dtype=np.float32),
        "c_ident": np.eye(128, dtype=np.float32),
        "c_head_of": ((f // DH)[:, None] == np.arange(H)[None, :]).astype(np.float32),
        "c_in_group": ((f // DH % 4)[:, None] == np.arange(4)[None, :]).astype(np.float32),
        "c_head_rows": head_rows.astype(np.float32),
        "c_row_head": ((np.arange(PACKED) // DH % 2)[:, None] == np.arange(2)[None, :]).astype(np.float32),
        "c_eye2": ((rows % S)[:, None] == np.arange(S)[None, :]).astype(np.float32),
    }


def layout(i):
    c = np.ascontiguousarray
    col = lambda name: c(i[name].reshape(-1, 1))
    out = {
        "x": c(i["x"].reshape(T, D)),
        "ctx": c(i["ctx_1024"]),
        "ctx_t": c(i["ctx_1024"].transpose(0, 2, 1)),
        "bias": c(i["fside_1x16xSxS2_0"].reshape(HP, PAIR, KEYS).transpose(1, 0, 2)),
        "mask0": c(i["mask_Bx1xSxS2_ik1"].reshape(B, S, KEYS)),
        "mask0_t": c(i["mask_Bx1xSxS2_ik1"].reshape(B, S, CH, KC).transpose(0, 3, 2, 1)),
        "mask3": c(i["mask_Bx1xSxS2_fk0"].reshape(B, S, KEYS)),
        "g_xattn": c(i["g_xattn"]), "g_ffn": c(i["g_ffn"]),
    }
    for n, names in ((0, ("W_q", "W_k", "W_v", "W_o")), (1, ("w_q", "w_k", "w_v", "w_o")),
                     (3, ("Wq", "Wk", "Wv", "Wo"))):
        for short, name in zip("qkvo", names):
            out[f"w{short}{n}"] = c(i[f"L{n}_xattn_{name}"].T)
    for n, pre in ((0, "b_"), (3, "b")):
        for short in "qko":
            out[f"b{short}{n}"] = col(f"L{n}_xattn_{pre}{short}")
        out[f"bv{n}"] = c(i[f"L{n}_xattn_{pre}v"])
    f = lambda name: c(i[name])
    out.update(w_fc=f("L0_ffn_w_fc"), w_proj=f("L0_ffn_w_proj"), v_t=c(i["L0_ffn_v"].T),
               fast_b_t=c(i["L0_ffn_fast_b"].T), u_t=c(i["L0_ffn_u"].T), gate0=c(i["L0_ffn_gate"].reshape(1)),
               router1=c(i["L1_ffn_gate_weight"].T), shared_up_t=c(i["L1_ffn_shared_gate_up"].T),
               shared_down_t=c(i["L1_ffn_shared_down"].T),
               experts_up_t=c(i["L1_ffn_experts_gate_up"].transpose(0, 2, 1)),
               experts_down_t=c(i["L1_ffn_experts_down"].transpose(0, 2, 1)),
               router2=c(i["L2_ffn_router_w"].T), router2_b=f("L2_ffn_router_b"),
               experts2=f("L2_ffn_expert_weights"),
               router3=f("L3_ffn_router_w"), router3_b=f("L3_ffn_router_b"),
               experts3=f("L3_ffn_expert_w"), experts3_b=f("L3_ffn_expert_b"),
               wq2=f("L2_xattn_wq"), wk2=f("L2_xattn_wk"), wv2_t=c(i["L2_xattn_wv"].T), wo2=f("L2_xattn_wo"),
               bo2=col("L2_xattn_bo"), w1_2=f("L2_xattn_w1"), w2_2=f("L2_xattn_w2"),
               b1_2=c(i["L2_xattn_b1"].reshape(4, 128).T), b2_2=col("L2_xattn_b2"),
               ln1_g=col("L2_xattn_ln1_g"), ln1_b=col("L2_xattn_ln1_b"), ln1_g_row=f("L2_xattn_ln1_g"),
               ln1_b_row=f("L2_xattn_ln1_b"), ln2_g=col("L2_xattn_ln2_g"), ln2_b=col("L2_xattn_ln2_b"))
    out.update(constants())
    return out


def loads(nc, name, pairs):
    r = scope(nc, name)
    with r.ctx:
        loaded = r.sem("loaded")
        with nc.Block() as block:
            @block.sync
            def _(sp):
                for dst, src in pairs:
                    sp.dma_start(dst[:], src).then_inc(loaded, 16)
                sp.wait_ge(loaded, 16 * len(pairs))


def program(nc, a, only=None):
    with ExitStack() as ctx:
        g = Names()
        sb = lambda n, shape: ctx.enter_context(nc.sbuf_tensor(n, shape, F32))
        g.x, g.ident, g.gates = sb("x_sb", [PAIR, TILES, D]), sb("ident", [128, 128]), sb("gates", [PAIR, 8])
        g.xn_t, g.y_t = sb("xn_t", [D, T]), sb("y_t", [D, T])
        a = dict(a)
        a["q_scratch"] = nc.dram_tensor("q_scratch", (3, D, T), BF16, kind="Internal").ap()
        a["x_scratch"] = nc.dram_tensor("x_scratch", (PAIR, TILES, D), F32, kind="Internal").ap()
        a["k_scratch"] = nc.dram_tensor("k_scratch", (2, 3, D, KEYS), BF16, kind="Internal").ap()
        parts = [
            lambda: attention(nc, g, "attn0", a, dict(
                wq=a["wq0"], wk=a["wk0"], wv=a["wv0"], wo=a["wo0"], bq=a["bq0"], bk=a["bk0"], bv=a["bv0"], bo=a["bo0"],
                mask=a["mask0"], mask_t=a["mask0_t"]), "select"),
            lambda: ffn0(nc, g, a),
            lambda: attention(nc, g, "attn1", a, dict(
                wq=a["wq1"], wk=a["wk1"], wv=a["wv1"], wo=a["wo1"], bq=None), "plain"),
            lambda: ffn1(nc, g, a),
            lambda: attention2(nc, g, a),
            lambda: ffn2(nc, g, a),
            lambda: attention(nc, g, "attn3", a, dict(
                wq=a["wq3"], wk=a["wk3"], wv=a["wv3"], wo=a["wo3"], bq=a["bq3"], bk=a["bk3"], bv=a["bv3"], bo=a["bo3"],
                mask=a["mask3"]), "add"),
            lambda: ffn3(nc, g, a),
        ]
        setup(nc, g, a)
        gate = None
        for n, part in enumerate(parts):
            if only is not None and n != only:
                continue
            if n == 4:
                with ExitStack() as own:
                    g.z_t = own.enter_context(nc.sbuf_tensor("z_t", [D, T], F32))
                    twice = [own.enter_context(nc.sbuf_tensor(m, [D, 1], F32)) for m in ("ln1_gain", "ln1_shift")]
                    loads(nc, "ln1", ((twice[0], a["ln1_g"]), (twice[1], a["ln1_b"])))
                    norm(nc, g, f"norm{n}", gate=gate, twice=(twice[0][:], twice[1][:]))
                    part()
            else:
                norm(nc, g, f"norm{n}", gate=gate)
                part()
            gate = n // 2 + 4 * (n % 2)
        norm(nc, g, "last", gate=gate, out=a["out"])


def kernel(**inputs):
    import concourse.bacc as bacc
    from concourse.bass_utils import run_bass_kernel_spmd

    nc = bacc.Bacc("TRN2", target_bir_lowering=False, num_devices=1)
    arrays, aps = {}, {}
    for name, value in layout({k: np.asarray(v) for k, v in inputs.items()}).items():
        arrays[f"in_{name}"] = value
        aps[name] = nc.dram_tensor(f"in_{name}", value.shape, mybir.dt.from_np(value.dtype), kind="ExternalInput").ap()
    aps["out"] = nc.dram_tensor("out", (T, D), F32, kind="ExternalOutput").ap()
    program(nc, aps)
    got = run_bass_kernel_spmd(nc, [arrays], core_ids=[0])
    return got.results[0]["out"].reshape(B, S, D)
```
